# Optimizing a Trainium2 kernel written in Bass

```python
import numpy as np
import jax
import jax.numpy as jnp

def _softmax(x, axis=-1):
    return jax.nn.softmax(x, axis=axis)

def _gelu(x):
    return jax.nn.gelu(x, approximate=True)

def _silu(x):
    return jax.nn.silu(x)

def _sigmoid(x):
    return jax.nn.sigmoid(x)

def _layernorm(x, axis=-1, eps=1e-05):
    m = jnp.mean(x, axis=axis, keepdims=True)
    v = jnp.var(x, axis=axis, keepdims=True)
    return (x - m) / jnp.sqrt(v + eps)

def _scatter_add(tgt, idx, src, axis=0):
    return tgt.at[idx].add(src)

def _segment_sum(src, seg, n):
    return jax.ops.segment_sum(src, seg, n)
kernel_name = 'mk_early_fusion_d2_tok_img256_r4_34a9f4'

def setup_inputs(seed: int=0):
    np.random.seed(seed)
    _w = jnp.asarray

    def _rec_inputs():
        import jax
        import jax.numpy as jnp
        _rk = jax.random.key(seed)
        x = -0.000209053 + 0.999977 * jax.random.normal(jax.random.fold_in(_rk, 1), (4, 64, 56, 56), jnp.float32)
        txt = -0.00183845 + 0.129704 * jax.random.normal(jax.random.fold_in(_rk, 2), (4, 32, 64), jnp.float32)
        return (x, txt)
    x, txt = _rec_inputs()

    def _L0_tok_setup():
        import jax, jax.numpy as jnp
        import numpy as np
        B, EMB, HT, WD = (32, 64, 56, 56)
        NH, WS, SHIFTED = (8, 4, True)

        def _rel_indices(ws):
            coords = np.array([[i, j] for i in range(ws) for j in range(ws)])
            rel = coords[None, :, :] - coords[:, None, :] + ws - 1
            return jnp.asarray(rel)

        def _shift_masks(ws):
            m = np.zeros((ws * ws, ws * ws), np.float32)
            s = ws * (ws // 2)
            m[-s:, :-s] = -np.inf
            m[:-s, -s:] = -np.inf
            col = m.reshape(ws, ws, ws, ws).transpose(1, 0, 3, 2).reshape(ws * ws, ws * ws)
            return (jnp.asarray(m), jnp.asarray(col))
        key = jax.random.key(seed)
        ks = jax.random.split(key, 6)
        x = jax.random.normal(ks[0], (B, EMB, HT, WD), jnp.float32)
        s = 1.0 / np.sqrt(EMB)
        w1 = jax.random.uniform(ks[1], (3 * EMB, EMB), jnp.float32, -s, s)
        b1 = jax.random.uniform(ks[2], (3 * EMB,), jnp.float32, -s, s)
        w2 = jax.random.uniform(ks[3], (EMB, EMB), jnp.float32, -s, s)
        b2 = jax.random.uniform(ks[4], (EMB,), jnp.float32, -s, s)
        pos_emb = jax.random.normal(ks[5], (2 * WS - 1, 2 * WS - 1), jnp.float32)
        return {'x': x, 'w1': w1, 'b1': b1, 'w2': w2, 'b2': b2, 'pos_emb': pos_emb}
    _L0_tok_all = _L0_tok_setup()
    _L0_tok_in = {k: v for k, v in _L0_tok_all.items() if k in ('w1', 'b1', 'w2', 'b2', 'pos_emb')}
    del _L0_tok_all

    def _L0_attn_setup():
        import jax, jax.numpy as jnp
        import numpy as np
        DIM = 64
        HEADS = 4
        HEAD_DIM = DIM // HEADS
        SCALE = HEAD_DIM ** (-0.5)
        key = jax.random.key(seed)
        k_x, k_wqkv, k_bqkv, k_wp, k_bp = jax.random.split(key, 5)
        B, N = (8, 512)
        x = jax.random.normal(k_x, (B, N, DIM), dtype=jnp.float32)
        W_qkv = jax.random.normal(k_wqkv, (3 * DIM, DIM), dtype=jnp.float32) * DIM ** (-0.5)
        b_qkv = jax.random.normal(k_bqkv, (3 * DIM,), dtype=jnp.float32) * 0.02
        W_proj = jax.random.normal(k_wp, (DIM, DIM), dtype=jnp.float32) * DIM ** (-0.5)
        b_proj = jax.random.normal(k_bp, (DIM,), dtype=jnp.float32) * 0.02
        return {'x': x, 'W_qkv': W_qkv, 'b_qkv': b_qkv, 'W_proj': W_proj, 'b_proj': b_proj}
    _L0_attn_all = _L0_attn_setup()
    _L0_attn_in = {k: v for k, v in _L0_attn_all.items() if k in ('W_qkv', 'b_qkv', 'W_proj', 'b_proj')}
    del _L0_attn_all

    def _L0_ffn_setup():
        import jax, jax.numpy as jnp
        import numpy as np
        E, D, H, TOP_K = (6, 64, 64, 2)
        ROUTER_H = D // 2
        key = jax.random.key(seed)
        ks = jax.random.split(key, 12)
        s = 1.0 / np.sqrt(D)
        sh = 1.0 / np.sqrt(H)
        sr = 1.0 / np.sqrt(ROUTER_H)
        return {'features': jax.random.normal(ks[0], (8, 1024, D), dtype=jnp.float32), 'router_w1': jax.random.uniform(ks[1], (D, ROUTER_H), jnp.float32, -s, s), 'router_b1': jnp.zeros((ROUTER_H,), jnp.float32), 'router_w2': jax.random.uniform(ks[2], (ROUTER_H, E), jnp.float32, -sr, sr), 'router_b2': jnp.zeros((E,), jnp.float32), 'expert_w1': jax.random.uniform(ks[3], (E, D, H), jnp.float32, -s, s), 'expert_b1': jnp.zeros((E, H), jnp.float32), 'expert_w2': jax.random.uniform(ks[4], (E, H, H), jnp.float32, -sh, sh), 'expert_b2': jnp.zeros((E, H), jnp.float32), 'expert_w3': jax.random.uniform(ks[5], (E, H, D), jnp.float32, -sh, sh), 'expert_b3': jnp.zeros((E, D), jnp.float32)}
    _L0_ffn_all = _L0_ffn_setup()
    _L0_ffn_in = {k: v for k, v in _L0_ffn_all.items() if k in ('router_w1', 'router_b1', 'router_w2', 'router_b2', 'expert_w1', 'expert_b1', 'expert_w2', 'expert_b2', 'expert_w3', 'expert_b3')}
    del _L0_ffn_all

    def _L1_attn_setup():
        import jax, jax.numpy as jnp
        import numpy as np
        B, N, D, H = (4, 256, 64, 8)
        key = jax.random.key(seed)
        k1, k2, k3 = jax.random.split(key, 3)
        x = jax.random.normal(k1, (B, N, D), dtype=jnp.float32)
        Wqkv = jax.random.normal(k2, (D, 3 * D * H), dtype=jnp.float32) * 0.02
        bqkv = jnp.zeros((3 * D * H,), dtype=jnp.float32)
        W0 = jax.random.normal(k3, (D * H, D), dtype=jnp.float32) * 0.02
        b0 = jnp.zeros((D,), dtype=jnp.float32)
        return {'x': x, 'Wqkv': Wqkv, 'bqkv': bqkv, 'W0': W0, 'b0': b0}
    _L1_attn_all = _L1_attn_setup()
    _L1_attn_in = {k: v for k, v in _L1_attn_all.items() if k in ('Wqkv', 'bqkv', 'W0', 'b0')}
    del _L1_attn_all

    def _L1_ffn_setup():
        import jax, jax.numpy as jnp
        import numpy as np
        C = 64
        HID = 256
        E = 8
        TEMP = 1.0
        key = jax.random.key(seed)
        ks = jax.random.split(key, 7)
        x = jax.random.normal(ks[0], (8, 4096, C), dtype=jnp.float32)
        W1 = jax.random.normal(ks[1], (C, HID), dtype=jnp.float32) * 0.02
        b1 = jnp.zeros((HID,), dtype=jnp.float32)
        Wg = jax.random.normal(ks[2], (HID, E), dtype=jnp.float32) * 0.02
        bg = jnp.zeros((E,), dtype=jnp.float32)
        Wd = jax.random.normal(ks[3], (E, HID, C), dtype=jnp.float32) * 0.02
        bd = jnp.zeros((E, C), dtype=jnp.float32)
        return {'x': x, 'W1': W1, 'b1': b1, 'Wg': Wg, 'bg': bg, 'Wd': Wd, 'bd': bd}
    _L1_ffn_all = _L1_ffn_setup()
    _L1_ffn_in = {k: v for k, v in _L1_ffn_all.items() if k in ('W1', 'b1', 'Wg', 'bg', 'Wd', 'bd')}
    del _L1_ffn_all
    return {'x': x, 'txt': txt, 'L0_tok_w1': _L0_tok_in['w1'], 'L0_tok_b1': _L0_tok_in['b1'], 'L0_tok_w2': _L0_tok_in['w2'], 'L0_tok_b2': _L0_tok_in['b2'], 'L0_tok_pos_emb': _L0_tok_in['pos_emb'], 'L0_attn_W_qkv': _L0_attn_in['W_qkv'], 'L0_attn_b_qkv': _L0_attn_in['b_qkv'], 'L0_attn_W_proj': _L0_attn_in['W_proj'], 'L0_attn_b_proj': _L0_attn_in['b_proj'], 'L0_ffn_router_w1': _L0_ffn_in['router_w1'], 'L0_ffn_router_b1': _L0_ffn_in['router_b1'], 'L0_ffn_router_w2': _L0_ffn_in['router_w2'], 'L0_ffn_router_b2': _L0_ffn_in['router_b2'], 'L0_ffn_expert_w1': _L0_ffn_in['expert_w1'], 'L0_ffn_expert_b1': _L0_ffn_in['expert_b1'], 'L0_ffn_expert_w2': _L0_ffn_in['expert_w2'], 'L0_ffn_expert_b2': _L0_ffn_in['expert_b2'], 'L0_ffn_expert_w3': _L0_ffn_in['expert_w3'], 'L0_ffn_expert_b3': _L0_ffn_in['expert_b3'], 'L1_attn_Wqkv': _L1_attn_in['Wqkv'], 'L1_attn_bqkv': _L1_attn_in['bqkv'], 'L1_attn_W0': _L1_attn_in['W0'], 'L1_attn_b0': _L1_attn_in['b0'], 'L1_ffn_W1': _L1_ffn_in['W1'], 'L1_ffn_b1': _L1_ffn_in['b1'], 'L1_ffn_Wg': _L1_ffn_in['Wg'], 'L1_ffn_bg': _L1_ffn_in['bg'], 'L1_ffn_Wd': _L1_ffn_in['Wd'], 'L1_ffn_bd': _L1_ffn_in['bd']}

def reference(x, txt, L0_tok_w1, L0_tok_b1, L0_tok_w2, L0_tok_b2, L0_tok_pos_emb, L0_attn_W_qkv, L0_attn_b_qkv, L0_attn_W_proj, L0_attn_b_proj, L0_ffn_router_w1, L0_ffn_router_b1, L0_ffn_router_w2, L0_ffn_router_b2, L0_ffn_expert_w1, L0_ffn_expert_b1, L0_ffn_expert_w2, L0_ffn_expert_b2, L0_ffn_expert_w3, L0_ffn_expert_b3, L1_attn_Wqkv, L1_attn_bqkv, L1_attn_W0, L1_attn_b0, L1_ffn_W1, L1_ffn_b1, L1_ffn_Wg, L1_ffn_bg, L1_ffn_Wd, L1_ffn_bd):
    import jax
    import jax.numpy as jnp

    def _L0_tok_ref(x, w1, b1, w2, b2, pos_emb):
        import jax, jax.numpy as jnp
        import numpy as np
        B, EMB, HT, WD = (32, 64, 56, 56)
        NH, WS, SHIFTED = (8, 4, True)

        def _rel_indices(ws):
            coords = np.array([[i, j] for i in range(ws) for j in range(ws)])
            rel = coords[None, :, :] - coords[:, None, :] + ws - 1
            return jnp.asarray(rel)

        def _shift_masks(ws):
            m = np.zeros((ws * ws, ws * ws), np.float32)
            s = ws * (ws // 2)
            m[-s:, :-s] = -np.inf
            m[:-s, -s:] = -np.inf
            col = m.reshape(ws, ws, ws, ws).transpose(1, 0, 3, 2).reshape(ws * ws, ws * ws)
            return (jnp.asarray(m), jnp.asarray(col))
        b, c, ht, wd = x.shape
        ws, nh = (WS, NH)
        e = c // nh
        xt = x.reshape(b, c, ht * wd).transpose(0, 2, 1)
        qkv = xt @ w1.T + b1
        qkv = qkv.reshape(b, ht, wd, c, 3)
        if SHIFTED:
            qkv = jnp.roll(qkv, (-ws // 2, -ws // 2), axis=(1, 2))
        Wh, Ww = (ht // ws, wd // ws)
        qkv = qkv.reshape(b, Wh, ws, Ww, ws, e, nh, 3)
        qkv = qkv.transpose(0, 6, 1, 3, 2, 4, 5, 7).reshape(b, nh, Wh, Ww, ws * ws, e, 3)
        Q, K, V = (qkv[..., 0], qkv[..., 1], qkv[..., 2])
        scale = jnp.sqrt(jnp.float32(c / nh))
        wei = jnp.einsum('bhijpe,bhijqe->bhijpq', Q, K) / scale
        rel = _rel_indices(ws)
        wei = wei + pos_emb[rel[..., 0], rel[..., 1]]
        if SHIFTED:
            row_mask, col_mask = _shift_masks(ws)
            wei = wei.at[:, :, -1, :].add(row_mask)
            wei = wei.at[:, :, :, -1].add(col_mask)
        attn = jax.nn.softmax(wei, axis=-1)
        out = jnp.einsum('bhijpq,bhijqe->bhijpe', attn, V)
        out = out.reshape(b, nh, Wh, Ww, ws, ws, e)
        out = out.transpose(0, 2, 4, 3, 5, 1, 6).reshape(b, ht, wd, nh * e)
        out = out.reshape(b, ht * wd, c)
        return out @ w2.T + b2

    def _L0_attn_ref(x, W_qkv, b_qkv, W_proj, b_proj):
        import jax, jax.numpy as jnp
        import numpy as np
        DIM = 64
        HEADS = 4
        HEAD_DIM = DIM // HEADS
        SCALE = HEAD_DIM ** (-0.5)
        B, N, C = x.shape
        h, d = (HEADS, HEAD_DIM)
        qkv = jnp.einsum('bnc,oc->bno', x, W_qkv) + b_qkv
        qkv = qkv.reshape(B, N, 3, h, d).transpose(2, 0, 3, 1, 4)
        q, k, v = (qkv[0], qkv[1], qkv[2])
        attn = jnp.einsum('bhnd,bhmd->bhnm', q, k) * SCALE
        attn = jax.nn.softmax(attn, axis=-1)
        out = jnp.einsum('bhnm,bhmd->bhnd', attn, v)
        out = out.transpose(0, 2, 1, 3).reshape(B, N, C)
        return jnp.einsum('bnc,oc->bno', out, W_proj) + b_proj

    def _L0_ffn_ref(features, router_w1, router_b1, router_w2, router_b2, expert_w1, expert_b1, expert_w2, expert_b2, expert_w3, expert_b3):
        import jax, jax.numpy as jnp
        import numpy as np
        E, D, H, TOP_K = (6, 64, 64, 2)
        ROUTER_H = D // 2
        rh = jax.nn.relu(features @ router_w1 + router_b1)
        expert_logits = jax.nn.softmax(rh @ router_w2 + router_b2, axis=-1)
        top_w, top_i = jax.lax.top_k(expert_logits, TOP_K)
        routing_weights = jax.nn.softmax(top_w, axis=-1)
        h1 = jax.nn.relu(jnp.einsum('bsd,edh->bseh', features, expert_w1) + expert_b1)
        h2 = jax.nn.relu(jnp.einsum('bseh,ehf->bsef', h1, expert_w2) + expert_b2)
        expert_out = jnp.einsum('bsef,efo->bseo', h2, expert_w3) + expert_b3
        sel = jnp.take_along_axis(expert_out, top_i[:, :, :, None], axis=2)
        combined = jnp.sum(sel * routing_weights[..., None], axis=2)
        return combined

    def _L1_attn_ref(x, Wqkv, bqkv, W0, b0):
        import jax, jax.numpy as jnp
        import numpy as np
        B, N, D, H = (4, 256, 64, 8)
        b, n, d = x.shape
        h = Wqkv.shape[1] // (3 * d)
        qkv = x @ Wqkv + bqkv
        q, k, v = jnp.reshape(qkv, (3, b, n, d, h))
        score = jnp.einsum('bnqh,btqh->bnth', q, k) * d ** (-0.5)
        attn = jax.nn.softmax(score, axis=1)
        av = jnp.einsum('bnnh,bnqh->bnqh', attn, v)
        out = av.reshape(b, n, d * h) @ W0 + b0
        return out

    def _L1_ffn_ref(x, W1, b1, Wg, bg, Wd, bd):
        import jax, jax.numpy as jnp
        import numpy as np
        C = 64
        HID = 256
        E = 8
        TEMP = 1.0
        orig_shape = x.shape
        xf = x.reshape(-1, orig_shape[-1])
        H = jax.nn.gelu(xf @ W1 + b1, approximate=False)
        probs = jax.nn.softmax((H @ Wg + bg) / TEMP, axis=-1)
        assign = jnp.argmax(probs, axis=-1)
        out = jnp.zeros_like(xf)
        for e in range(Wd.shape[0]):
            y = H @ Wd[e] + bd[e]
            sel = (assign == e)[:, None]
            out = out + jnp.where(sel, probs[:, e:e + 1] * y, 0.0)
        return out.reshape(orig_shape)
    h = _L0_tok_ref(x, L0_tok_w1, L0_tok_b1, L0_tok_w2, L0_tok_b2, L0_tok_pos_emb)
    h = jnp.concatenate([h, txt], axis=1)
    h = h + _L0_attn_ref(_layernorm(h, axis=-1), L0_attn_W_qkv, L0_attn_b_qkv, L0_attn_W_proj, L0_attn_b_proj)
    h = h + _L0_ffn_ref(_layernorm(h, axis=-1), L0_ffn_router_w1, L0_ffn_router_b1, L0_ffn_router_w2, L0_ffn_router_b2, L0_ffn_expert_w1, L0_ffn_expert_b1, L0_ffn_expert_w2, L0_ffn_expert_b2, L0_ffn_expert_w3, L0_ffn_expert_b3)
    h = h + _L1_attn_ref(_layernorm(h, axis=-1), L1_attn_Wqkv, L1_attn_bqkv, L1_attn_W0, L1_attn_b0)
    h = h + _L1_ffn_ref(_layernorm(h, axis=-1), L1_ffn_W1, L1_ffn_b1, L1_ffn_Wg, L1_ffn_bg, L1_ffn_Wd, L1_ffn_bd)
    return h

_drawn_inputs = setup_inputs


def setup_inputs(seed=0):
    import zlib

    import numpy as np

    out = dict(_drawn_inputs(seed))
    spreads = {'L0_ffn_router_b1': (0.0, 0.344),
     'L0_ffn_router_b2': (0.0, 0.8),
     'L0_ffn_expert_b1': (0.0, 0.45),
     'L0_ffn_expert_b2': (0.0, 0.1),
     'L0_ffn_expert_b3': (0.0, 0.1),
     'L1_attn_bqkv': (0.0, 0.8),
     'L1_attn_b0': (0.0, 0.1),
     'L1_ffn_b1': (0.0, 0.8),
     'L1_ffn_bg': (0.0, 0.8),
     'L1_ffn_bd': (0.0, 0.349)}
    factors = {'L1_attn_Wqkv': 8.0,
     'L1_attn_W0': 8.0,
     'L1_ffn_W1': 5.099,
     'L1_ffn_Wg': 8.0,
     'L1_ffn_Wd': 8.0}
    for name, (base, spread) in spreads.items():
        noise = np.random.default_rng([zlib.crc32(name.encode()), seed]).standard_normal(out[name].shape)
        drawn = base * np.exp(spread * noise) if base else spread * noise
        out[name] = jnp.asarray(drawn.astype(out[name].dtype))
    for name, factor in factors.items():
        out[name] = (out[name] * factor).astype(out[name].dtype)
    return out
```

```python
from contextlib import ExitStack

import concourse.bass as bass
from concourse import mybir

F32 = mybir.dt.float32
BF16 = mybir.dt.bfloat16
ALU = mybir.AluOpType
ACT = mybir.ActivationFunctionType
AX = mybir.AxisListType

NB = 4
C = 64
SIDE = 56
IMG = SIDE * SIDE
TXT = 32
N = IMG + TXT
P = 128
NT = 25
LAST = N - (NT - 1) * P
WS = 4
WT = WS * WS
NH = 8
WR = SIDE // WS
HW = WR // 2
HT = HW * WT
MASKED = -1e30
EPS = 1e-5


class Chain:

    def __init__(self, eng, sem, i=0, per=0):
        self.eng, self.sem, self.base, self.n, self.per = eng, sem, i * per, 0, per

    def link(self, ins):
        self.n += 1
        ins.then_inc(self.sem, 1)
        self.eng.wait_ge(self.sem, self.base + self.n)

    def end(self):
        assert self.n == self.per, self.n


def phase_a(nc, io, h_cm):
    with ExitStack() as ctx:
        sb = lambda n, s, d=F32: ctx.enter_context(nc.sbuf_tensor("a_" + n, s, d))
        ps = lambda n, s, d=F32: ctx.enter_context(nc.psum_tensor("a_p_" + n, s, d))
        sem = lambda n: ctx.enter_context(nc.semaphore("a_s_" + n))
        X = sb("x", [C, NB * IMG])
        w1 = sb("w1", [C, 3, P])
        b1 = sb("b1", [P, 3])
        w2 = sb("w2", [P, C])
        b2 = sb("b2", [C, 1])
        mask = sb("mask", [P, NH])
        ident = sb("ident", [P, P])
        bias = sb("bias", [HT, WR, 2, WT])
        unmet = sb("unmet", [HT, WR, 2, WT])
        qkv = sb("qkv", [P, 3, HT])
        kexp = sb("kexp", [P, HW, NH, WT])
        vexp = sb("vexp", [P, HW, NH, WT])
        ssb = sb("ssb", [P, 2, HT])
        prob = sb("prob", [HT, 2, NH, WT])
        stat = sb("stat", [HT, 3, 2 * NH])
        vw = sb("vw", [P, WR, C])
        pt = sb("pt", [P, 2, HT])
        yrow = sb("yrow", [C, WS * SIDE])
        p_proj = ps("proj", [P, 2, 512])
        p_s = ps("s", [P, 2, 512])
        p_t = ps("t", [P, 512])
        p_pty = ps("pty", [P, 512])
        p_pt = p_pty[:, 0:2 * HT]
        p_y = p_pty[:, 2 * HT:4 * HT]
        p_vw = ps("vw", [P, 2, 512])

        loaded = sem("loaded")
        bias_in = sem("bias_in")
        bias_ok = sem("bias_ok")
        txt_in = sem("txt_in")
        proj_done = sem("proj_done")
        qkv_ready = sem("qkv_ready")
        kexp_ready = sem("kexp_ready")
        vexp_ready = sem("vexp_ready")
        s_done = sem("s_done")
        ssb_ready = sem("ssb_ready")
        t_done = sem("t_done")
        t_read = sem("t_read")
        shifted = sem("shifted")
        exp_done = sem("exp_done")
        p_ready = sem("p_ready")
        vw_done = sem("vw_done")
        vw_ready = sem("vw_ready")
        pt_done = sem("pt_done")
        pt_ready = sem("pt_ready")
        y_done = sem("y_done")
        y_read = sem("y_read")
        y_out = sem("y_out")
        dve_own = sem("dve_own")
        dve_set = sem("dve_set")

        Xv = X[:].rearrange("c (b h w) -> c b h w", b=NB, h=SIDE)
        x = io["x"]
        R = SIDE - 2
        with nc.Block() as block:
            @block.sync
            def _(sp):
                n = 0
                for t, k in ((w1, "tok_w1"), (b1, "tok_b1"), (w2, "tok_w2"), (b2, "tok_b2"),
                             (mask, "head_mask"), (ident, "ident")):
                    sp.dma_start(t[:], io[k]).then_inc(loaded, 16)
                for b in range(NB):
                    for i0, i1, s0 in ((0, R, 2), (R, SIDE, 0)):
                        for j0, j1, t0 in ((0, R, 2), (R, SIDE, 0)):
                            sp.dma_start(Xv[:, b, i0:i1, j0:j1],
                                         x[b, :, s0:s0 + i1 - i0, t0:t0 + j1 - j0]).then_inc(loaded, 16)
                for p in range(WT):
                    pi, pj = divmod(p, WS)
                    sp.dma_start(bias[p:HT:WT, 0, 0, :].rearrange("p (a c) -> p a c", a=WS),
                                 io["pos"][:, 3 - pi:7 - pi, 3 - pj:7 - pj].to_broadcast([HW, WS, WS])).then_inc(bias_in, 16)
                sp.dma_start(h_cm.rearrange("c (b n) -> c b n", b=NB)[:, :, IMG:N], io["txt"]).then_inc(txt_in, 16)
                with sp.Fori(0, NB) as b:
                    with sp.Fori(0, WR) as r:
                        sp.wait_ge(y_read, b * WR + r + 1)
                        sp.dma_start(h_cm[:, bass.ds(b * N + r * WS * SIDE, WS * SIDE)], yrow[:]).then_inc(y_out, 16)
                sp.wait_ge(y_out, NB * WR * 16)
                sp.wait_ge(txt_in, 16)

            @block.tensor
            def _(pe):
                pe.wait_ge(loaded, 16 * (6 + 4 * NB))

                def front(b, r):
                    g = b * WR + r
                    pe.wait_ge(qkv_ready, g)
                    for s in range(3):
                        rows = X[:, bass.ds(g * WS * SIDE, WS * SIDE)].rearrange("c (r w s) -> c w r s", r=WS, s=WS)
                        last = pe.matmul(p_proj[:, s // 2, (s % 2) * 2 * HT:(s % 2 + 1) * 2 * HT], w1[:, s, :], rows,
                                         start=True, stop=True)
                    last.then_inc(proj_done, 1)
                    pe.wait_ge(kexp_ready, g + 1)
                    pe.wait_ge(ssb_ready, g)
                    for half in range(2):
                        for w in range(HW):
                            h0 = half * C
                            last = pe.matmul(p_s[:, half, w * WT:(w + 1) * WT],
                                             kexp[h0:h0 + C, w, :, :].rearrange("p h k -> p (h k)"),
                                             qkv[h0:h0 + C, 0, w * WT:(w + 1) * WT], start=True, stop=True)
                    last.then_inc(s_done, 1)
                    pe.wait_ge(vexp_ready, g + 1)
                    pe.wait_ge(vw_ready, g)
                    for half in range(2):
                        for w in range(HW):
                            h0 = half * C
                            last = pe.matmul(p_vw[:, half, w * C:(w + 1) * C],
                                             vexp[h0:h0 + C, w, :, :].rearrange("p h k -> p (h k)"),
                                             w2[h0:h0 + C, :], start=True, stop=True)
                    last.then_inc(vw_done, 1)
                    pe.wait_ge(ssb_ready, g + 1)
                    pe.wait_ge(t_read, g)
                    for half in range(2):
                        last = pe.transpose(p_t[0:HT, half * P:(half + 1) * P], ssb[:, half, :], ident[:])
                    last.then_inc(t_done, 1)

                def back(g):
                    pe.wait_ge(p_ready, g + 1)
                    pe.wait_ge(pt_ready, g)
                    for half in range(2):
                        last = pe.transpose(p_pt[:, half * HT:(half + 1) * HT],
                                            prob[:, half, :, :].rearrange("q h k -> q (h k)"), ident[0:HT, 0:HT])
                    last.then_inc(pt_done, 1)
                    pe.wait_ge(pt_ready, g + 1)
                    pe.wait_ge(vw_ready, g + 1)
                    pe.wait_ge(y_read, g)
                    for w in range(WR):
                        last = pe.matmul(p_y[0:C, w * WT:(w + 1) * WT], vw[:, w, :],
                                         pt[:, w // HW, (w % HW) * WT:(w % HW + 1) * WT], start=True, stop=True)
                    last.then_inc(y_done, 1)

                with pe.Fori(0, NB) as b:
                    front(b, 0)
                    with pe.Fori(1, WR) as r:
                        front(b, r)
                        back(b * WR + r - 1)
                    back(b * WR + WR - 1)

            @block.vector
            def _(dve):
                dve.wait_ge(bias_in, 16 * WT)
                own = Chain(dve, dve_set)
                own.link(dve.tensor_copy(bias[:, 0, 1, :], bias[:, 0, 0, :]))
                for r in range(1, WR):
                    last = dve.tensor_copy(bias[:, r, :, :], bias[:, 0, :, :])
                own.link(last)
                dve.wait_ge(bias_ok, 16)
                own.link(dve.tensor_tensor(bias[:], bias[:], unmet[:], ALU.add))
                dve.wait_ge(loaded, 16 * (6 + 4 * NB))
                with dve.Fori(0, NB) as b:
                    with dve.Fori(0, WR) as r:
                        g = b * WR + r
                        own = Chain(dve, dve_own, g, 4)
                        dve.wait_ge(proj_done, g + 1)
                        dve.wait_ge(vexp_ready, g)
                        dve.wait_ge(s_done, g)
                        for half in range(2):
                            lanes = slice(half * C, half * C + C)
                            dve.tensor_tensor(qkv[lanes, 0:2, :], p_proj[lanes, 0, 0:4 * HT].rearrange(
                                "p (s t) -> p s t", s=2)[:, :, half * HT:(half + 1) * HT],
                                b1[lanes, 0:2].unsqueeze(2).to_broadcast([C, 2, HT]), ALU.add)
                            last = dve.tensor_tensor(qkv[lanes, 2, :], p_proj[lanes, 1, half * HT:(half + 1) * HT],
                                                     b1[lanes, 2:3].to_broadcast([C, HT]), ALU.add)
                        last.then_inc(qkv_ready, 1)
                        dve.wait_ge(qkv_ready, g + 1)
                        dve.tensor_tensor(kexp[:],
                                          qkv[:, 1, :].rearrange("p (w k) -> p w k", k=WT).unsqueeze(2).to_broadcast([P, HW, NH, WT]),
                                          mask[:].unsqueeze(1).unsqueeze(3).to_broadcast([P, HW, NH, WT]), ALU.mult).then_inc(kexp_ready, 1)
                        dve.wait_ge(t_done, g + 1)
                        dve.wait_ge(pt_done, g)
                        dve.tensor_tensor(prob[:],
                                          p_t[0:HT, 0:2 * P].rearrange("q (t h k) -> q t h k", t=2, h=NH),
                                          bias[:, bass.ds(r, 1), :, :].rearrange("q r t k -> q (r t) k").unsqueeze(2).to_broadcast([HT, 2, NH, WT]),
                                          ALU.add).then_inc(t_read, 1)
                        dve.wait_ge(t_read, g + 1)
                        flat = prob[:].rearrange("q t h k -> q (t h) k")
                        wide = lambda i: stat[:, i, :].unsqueeze(2).to_broadcast([HT, 2 * NH, WT])
                        own.link(dve.tensor_reduce(stat[:, 0, :], flat, AX.X, ALU.max))
                        dve.tensor_tensor(flat, flat, wide(0), ALU.subtract).then_inc(shifted, 1)
                        dve.wait_ge(exp_done, g + 1)
                        own.link(dve.tensor_reduce(stat[:, 1, :], flat, AX.X, ALU.add))
                        own.link(dve.reciprocal(stat[:, 2, :], stat[:, 1, :]))
                        dve.tensor_tensor(flat, flat, wide(2), ALU.mult).then_inc(p_ready, 1)
                        own.link(dve.tensor_copy(stat[:, 1, :], stat[:, 2, :]))
                        own.end()

            @block.gpsimd
            def _(pool):
                pool.dma_start(unmet[:], io["masks"]).then_inc(bias_ok, 16)
                pool.wait_ge(loaded, 16 * (6 + 4 * NB))
                with pool.Fori(0, NB) as b:
                    with pool.Fori(0, WR) as r:
                        g = b * WR + r
                        pool.wait_ge(qkv_ready, g + 1)
                        pool.wait_ge(vw_done, g)
                        pool.tensor_tensor(vexp[:],
                                           qkv[:, 2, :].rearrange("p (w k) -> p w k", k=WT).unsqueeze(2).to_broadcast([P, HW, NH, WT]),
                                           mask[:].unsqueeze(1).unsqueeze(3).to_broadcast([P, HW, NH, WT]), ALU.mult).then_inc(vexp_ready, 1)

            @block.scalar
            def _(act):
                act.wait_ge(loaded, 16 * (6 + 4 * NB))

                def scores(g):
                    act.wait_ge(s_done, g + 1)
                    act.wait_ge(t_done, g)
                    act.activation(ssb[:], p_s[:, :, 0:HT], ACT.Copy, scale=float((C / NH) ** -0.5)).then_inc(ssb_ready, 1)

                def values(g):
                    act.wait_ge(vw_done, g + 1)
                    act.wait_ge(y_done, g)
                    act.activation(vw[:].rearrange("p (t w) o -> p t (w o)", t=2), p_vw[:, :, 0:HW * C], ACT.Copy).then_inc(vw_ready, 1)

                def exps(g):
                    act.wait_ge(shifted, g + 1)
                    act.activation(prob[:], prob[:], ACT.Exp).then_inc(exp_done, 1)

                def probs(g):
                    act.wait_ge(pt_done, g + 1)
                    act.activation(pt[:].rearrange("p t q -> p (t q)"), p_pt[:, 0:2 * HT], ACT.Copy).then_inc(pt_ready, 1)

                def out(b, r):
                    act.wait_ge(y_done, b * WR + r + 1)
                    act.wait_ge(y_out, (b * WR + r) * 16)
                    act.activation(yrow[:].rearrange("c (r w s) -> c w r s", r=WS, s=WS),
                                   p_y[0:C, 0:WS * SIDE].rearrange("c (w r s) -> c w r s", r=WS, s=WS),
                                   ACT.Identity, bias=b2[:, 0:1]).then_inc(y_read, 1)

                with act.Fori(0, NB) as b:
                    scores(b * WR)
                    values(b * WR)
                    exps(b * WR)
                    with act.Fori(1, WR) as r:
                        g = b * WR + r
                        scores(g)
                        probs(g - 1)
                        values(g)
                        out(b, r - 1)
                        exps(g)
                    probs(b * WR + WR - 1)
                    out(b, WR - 1)


NP = NT * P
G0 = 4
D0 = C // G0
QC = 3 * P
NQ = N // QC
KC = 396
NK = N // KC
RING = 3
STEPS = NT
ROWS = 6 * D0
M0 = ROWS
E0 = 6
PARTS = ((0, 0), (0, 1), (1, 0), (1, 1), (0, 2), (2, 0))


def ln_vector(dve, own, H, xh, sq, stat, s, k):
    wide = lambda i: stat[:, i, :].unsqueeze(2).to_broadcast([P, NT, C])
    own.link(dve.tensor_reduce(stat[:, 0, :], H[:], AX.X, ALU.add))
    own.link(dve.tensor_scalar(stat[:, 0, :], stat[:, 0, :], 1.0 / C, None, ALU.mult))
    own.link(dve.tensor_tensor(xh[:], H[:], wide(0), ALU.subtract))
    own.link(dve.tensor_tensor(sq[:], xh[:], xh[:], ALU.mult))
    own.link(dve.tensor_reduce(stat[:, 1, :], sq[:], AX.X, ALU.add))
    dve.tensor_scalar(stat[:, 1, :], stat[:, 1, :], 1.0 / C, EPS, ALU.mult, ALU.add).then_inc(s["var"], 1)
    dve.wait_ge(s["std"], k + 1)
    own.link(dve.reciprocal(stat[:, 3, :], stat[:, 2, :]))
    dve.tensor_tensor(xh[:], xh[:], wide(3), ALU.mult).then_inc(s["xh"], 1)


def ln_scalar(act, stat, s, k):
    act.wait_ge(s["var"], k + 1)
    act.activation(stat[:, 2, :], stat[:, 1, :], ACT.Sqrt).then_inc(s["std"], 1)


GROUPS = [(4 * g, min(4 * g + 4, NT)) for g in range((NT + 3) // 4)]


def turn_tensor(pe, xh, pb, ident, s, k):
    pe.wait_ge(s["xh"], k + 1)
    pe.sem_inc(s["passed"])
    for g, (t0, t1) in enumerate(GROUPS):
        for t in range(t0, t1):
            last = pe.transpose(pb[0:C, g, (t - t0) * P:(t - t0 + 1) * P], xh[:, t, :], ident[:])
        last.then_inc(s["turned"], 1)


def turn_scalar(act, xT, pb, s, k):
    for g, (t0, t1) in enumerate(GROUPS):
        act.wait_ge(s["turned"], k * len(GROUPS) + g + 1)
        act.activation(xT[0:C, t0 * P:t1 * P], pb[0:C, g, 0:(t1 - t0) * P], ACT.Copy).then_inc(s["xT"], 1)


def phase_b(nc, io, h_cm, x_cm, h_tm):
    with ExitStack() as ctx:
        sb = lambda n, s, d=F32: ctx.enter_context(nc.sbuf_tensor("b_" + n, s, d))
        sem = lambda n: ctx.enter_context(nc.semaphore("b_s_" + n))
        xT = sb("xT", [C + 1, NP])
        H = sb("H", [P, NT, C])
        xh = sb("xh", [P, NT, C])
        sq = sb("sq", [P, NT, C])
        stat = sb("stat", [P, 4, NT])
        ident = sb("ident", [P, P])
        identh = sb("identh", [P, P], BF16)
        wqk = sb("wqk", [C + 1, P])
        wv = sb("wv", [C + 1, C])
        scale = sb("scale", [P, 1])
        V = sb("V", [P, NT, G0, 32])
        Qs = sb("Qs", [P, G0, N], BF16)
        Ks = sb("Ks", [P, G0, N], BF16)
        y = sb("y", [P, N])
        parts = sb("parts", [P, 3, N], BF16)
        prob = sb("prob", [P, 2, G0, QC])
        mx = sb("mx", [P, 3 * G0, NK])
        nm = sb("nm", [P, 2, 3 * G0])
        nsp = sb("nsp", [P, 3 * G0, 3], BF16)
        O = y
        wp = sb("wp", [P, C])
        bp = sb("bp", [1, C])
        one = sb("one", [1, P])
        selz = sb("selz", [P, P])
        zr = sb("zr", [P, 2, 512])
        pb = ctx.enter_context(nc.psum_tensor("b_ps", [P, 8, 512], F32))
        rw1 = sb("rw1", [C + 1, 32])
        rw2 = sb("rw2", [33, E0])
        ew1 = sb("ew1", [C + 1, 3, P])
        ew2 = sb("ew2", [P, 3, P])
        eb2 = sb("eb2", [P, 3])
        ew3 = sb("ew3", [P, 3, P])
        eb3 = sb("eb3", [1, 3 * P])
        iota = sb("iota", [P, NT, E0])
        rh = sb("rh", [33, NP])
        rt = sb("rt", [P, 8, NT, E0])
        rs = sb("rs", [P, 4, NT])
        W = sb("W", [P, NT, E0])
        h1 = sb("h1", [P, 3, QC])
        h2 = sb("h2", [P, 2, 3, QC])
        yw = sb("yw", [P, 2, E0, C])
        ya = sb("ya", [P, C])

        loaded = sem("loaded")
        pool_own = sem("pool_own")
        dve_own = [sem(f"dve_own{i}") for i in range(5)]
        h_in = sem("h_in")
        S = {n: sem(n) for n in ("var", "std", "xh", "turned", "xT")}
        S["passed"] = sem("passed")
        S["sp_passed"] = sem("sp_passed")
        h_turned = sem("h_turned")
        h_read = sem("h_read")
        v_done = sem("v_done")
        v_read = sem("v_read")
        qk_done = sem("qk_done")
        y_ready = sem("y_ready")
        part_ready = sem("part_ready")
        stacked = sem("stacked")
        mu_full = sem("mu_full")
        mu_free = sem("mu_free")
        n_ready = sem("n_ready")
        rows_full = sem("rows_full")
        rows_ready = sem("rows_ready")
        s_full = sem("s_full")
        p_full = sem("p_full")
        pv_done = sem("pv_done")
        o_read = sem("o_read")
        z_done = sem("z_done")
        zr_ready = sem("zr_ready")
        o_ready = sem("o_ready")
        pr_done = sem("pr_done")
        rh_done = sem("rh_done")
        rh_ready = sem("rh_ready")
        lg_done = sem("lg_done")
        lg_ready = sem("lg_ready")
        lg_exp = sem("lg_exp")
        two_ready = sem("two_ready")
        two_exp = sem("two_exp")
        h1_done = sem("h1_done")
        h1_ready = sem("h1_ready")
        h2_done = sem("h2_done")
        h2_ready = sem("h2_ready")
        ye_done = sem("ye_done")
        ye_read = sem("ye_read")
        stored = sem("stored")
        h_new = sem("h_new")

        with nc.Block() as block:
            @block.sync
            def _(sp):
                loads = ((ident, "ident"), (wqk, "wqk"), (wv, "wv"), (scale, "scale"), (wp, "wp"), (bp, "bp"),
                         (selz, "selz"), (rw1, "rw1"), (rw2, "rw2"), (ew1, "ew1"), (ew2, "ew2"), (eb2, "eb2"),
                         (ew3, "ew3"), (eb3, "eb3"), (iota, "iota"))
                for t, k in loads:
                    sp.dma_start(t[:], io[k]).then_inc(loaded, 16)
                sp.wait_ge(loaded, 16 * len(loads))

            @block.vector
            def _(dve):
                dve.memset(xT[0:C, N:NP], 0.0)
                dve.memset(xT[C:C + 1, :], 1.0)
                dve.memset(H[:], 0.0)
                dve.memset(one[:], 1.0)
                dve.memset(rh[32:33, :], 1.0)

            @block.gpsimd
            def _(pool):
                own = Chain(pool, pool_own)
                own.link(pool.memset(V[:], 0.0))
                own.link(pool.memset(V[:, :, :, D0:D0 + 1], 1.0))
                own.link(pool.memset(Ks[96:128, :, :], 1.0))
        with nc.Block() as block:
            @block.vector
            def _(dve):
                dve.tensor_copy(identh[:], ident[:])

        with nc.Fori(0, NB) as b:
            with nc.Block() as block:
                @block.sync
                def _(sp):
                    sp.dma_start(xT[0:C, 0:N], h_cm[:, bass.ds(b * N, N)]).then_inc(h_in, 16)
                    for part in range(3):
                        sp.wait_ge(part_ready, b * 3 + part + 1)
                        for r, (pq, pk) in enumerate(PARTS):
                            for h in range(G0):
                                rows = slice(r * D0, (r + 1) * D0)
                                if pq == part:
                                    sp.dma_start(Qs[rows, h, :], parts[h * D0:(h + 1) * D0, part, :]).then_inc(stacked, 16)
                                if pk == part:
                                    sp.dma_start(Ks[rows, h, :], parts[C + h * D0:C + (h + 1) * D0, part, :]).then_inc(stacked, 16)
                    sp.wait_ge(stacked, (b + 1) * 16 * 2 * G0 * len(PARTS))
                    sp.sem_inc(S["sp_passed"])

                @block.tensor
                def _(pe):
                    pe.wait_ge(h_in, (b + 1) * 16)
                    pe.sem_inc(S["passed"])
                    for t in range(NT):
                        w = P if t < NT - 1 else LAST
                        last = pe.transpose(pb[0:w, t // 8, t % 8 * C:(t % 8 + 1) * C], xT[0:C, t * P:t * P + w], ident[0:C, 0:C])
                    last.then_inc(h_turned, 1)
                    pe.wait_ge(h_read, b + 1)
                    turn_tensor(pe, xh, pb, ident, S, b * 3)
                    pe.wait_ge(S["xT"], (b * 3 + 1) * len(GROUPS))
                    for t in range(NT):
                        last = pe.matmul(pb[:, t // 8, t % 8 * C:(t % 8 + 1) * C], xT[:, t * P:(t + 1) * P], wv[:], start=True, stop=True)
                    last.then_inc(v_done, 1)
                    for c in range(NK):
                        bank = (c + 4) % 8
                        if c == 4:
                            pe.wait_ge(v_read, b + 1)
                        last = pe.matmul(pb[:, bank, 0:KC], wqk[:], xT[:, c * KC:(c + 1) * KC], start=True, stop=True)
                        if c % 4 == 3:
                            last.then_inc(qk_done, 1)

                @block.vector
                def _(dve):
                    own = Chain(dve, dve_own[0], b, 8)
                    dve.wait_ge(h_turned, b + 1)
                    for t0 in (0, 8, 16):
                        dve.tensor_copy(H[:, t0:t0 + 8, :], pb[:, t0 // 8, :].rearrange("p (t c) -> p t c", t=8))
                    dve.tensor_copy(H[0:LAST, NT - 1, :], pb[0:LAST, 3, 0:C]).then_inc(h_read, 1)
                    dve.wait_ge(h_read, b + 1)
                    ln_vector(dve, own, H, xh, sq, stat, S, b * 3)
                    dve.wait_ge(v_done, b + 1)
                    for g in range(4):
                        t0, t1 = 8 * g, min(8 * g + 8, NT)
                        last = dve.tensor_copy(V[:, t0:t1, :, 0:D0], pb[:, g, 0:(t1 - t0) * C].rearrange("p (t h e) -> p t h e", h=G0, e=D0))
                    last.then_inc(v_read, 1)
                    dve.wait_ge(y_ready, (b + 1) * 2)
                    dve.wait_ge(part_ready, b * 3 + 1)
                    own.link(dve.tensor_tensor(y[:], y[:], parts[:, 0, :], ALU.subtract))
                    dve.tensor_copy(parts[:, 1, :], y[:]).then_inc(part_ready, 1)
                    dve.wait_ge(part_ready, b * 3 + 2)
                    own.link(dve.tensor_tensor(y[:], y[:], parts[:, 1, :], ALU.subtract))
                    dve.tensor_copy(parts[:, 2, :], y[:]).then_inc(part_ready, 1)
                    own.end()

                @block.scalar
                def _(act):
                    ln_scalar(act, stat, S, b * 3)
                    turn_scalar(act, xT, pb, S, b * 3)
                    for g in range(2):
                        act.wait_ge(qk_done, b * 2 + g + 1)
                        src = pb[:, 4:8, 0:KC] if g == 0 else pb[:, 0:4, 0:KC]
                        cols = slice(g * 4 * KC, (g + 1) * 4 * KC)
                        act.activation(y[:, cols].rearrange("p (a n) -> p a n", a=4), src, ACT.Copy, scale=scale[:, 0:1]).then_inc(y_ready, 1)
                        last = act.activation(parts[:, 0, cols].rearrange("p (a n) -> p a n", a=4), src, ACT.Copy, scale=scale[:, 0:1])
                    last.then_inc(part_ready, 1)

            NU = 3 * G0 * NK
            UNITS = NQ * NU + G0 * NK
            nchunk = NQ + 1

            with nc.Block() as block:
                @block.tensor
                def _(pe):
                    u0 = b * UNITS

                    def unit(c, j, static=None):
                        w = P if static is None or static < NQ else LAST
                        t, h, k = j // (G0 * NK), j // NK % G0, j % NK
                        if static != 0 or j >= RING:
                            pe.wait_ge(mu_free, u0 + c * NU + (j - RING + 1))
                        if static != 0 and j < RING:
                            pe.wait_ge(rows_ready, b * nchunk + c)
                        q = Qs[0:ROWS, h, bass.ds(c * QC + t * P, w)] if static is None else Qs[0:ROWS, h, c * QC + t * P:c * QC + t * P + w]
                        pe.matmul(pb[0:w, j % RING, 0:KC], q, Ks[0:ROWS, h, k * KC:(k + 1) * KC],
                                  start=True, stop=True).then_inc(mu_full, 1)

                    def rows(c, tiles, w):
                        pe.wait_ge(n_ready, b * nchunk + c + 1)
                        for h in range(G0):
                            for t in range(tiles):
                                col = h * tiles * w + t * w
                                last = pe.matmul(pb[M0:M0 + 3, col // 512, col % 512:col % 512 + w],
                                                 nsp[0:w, t * G0 + h, :], identh[0:w, 0:w], start=True, stop=True)
                        last.then_inc(rows_full, 1)

                    def scores(c, s, w, whole):
                        m = P if s < NT - 1 else LAST
                        g = b * nchunk * STEPS + c * STEPS + s
                        for pair in range(2):
                            if s:
                                pe.wait_ge(p_full, g * 2 + pair - 1)
                            for h in (2 * pair, 2 * pair + 1):
                                q = Qs[0:M0 + 3, h, bass.ds(c * QC, w)] if whole is None else Qs[0:M0 + 3, h, c * QC:c * QC + w]
                                last = pe.matmul(pb[0:m, 4 + h, 0:w], Ks[0:M0 + 3, h, s * P:s * P + m], q, start=True, stop=True)
                            last.then_inc(s_full, 1)

                    def product(c, s, w):
                        m = P if s < NT - 1 else LAST
                        g = b * nchunk * STEPS + c * STEPS + s
                        pe.wait_ge(p_full, 2 * g + 2)
                        if s == 0:
                            pe.wait_ge(o_read, b * nchunk + c)
                        for h in range(G0):
                            last = pe.matmul(pb[32 * h:32 * h + 32, 3, 0:w], V[0:m, s, h, :], prob[0:m, s % 2, h, 0:w],
                                             start=(s == 0), stop=(s == NT - 1), tile_position=(0, 32 * h))
                        last.then_inc(pv_done, 1)

                    def both(c, w, static, ahead, n):
                        per = -(-n // (STEPS - 1))
                        pe.wait_ge(rows_ready, b * nchunk + c + 1)
                        for s in range(STEPS):
                            scores(c, s, w, static)
                            for j in range(s * per, min((s + 1) * per, n)):
                                unit(c + 1, j, ahead)
                            if s:
                                product(c, s - 1, w)
                        product(c, STEPS - 1, w)

                    for j in range(NU):
                        unit(0, j, 0)
                    rows(0, 3, P)
                    with pe.Fori(0, NQ - 1) as c:
                        both(c, QC, None, None, NU)
                        rows(c + 1, 3, P)
                    both(NQ - 1, QC, NQ - 1, NQ, G0 * NK)
                    rows(NQ, 1, LAST)
                    both(NQ, LAST, NQ, None, 0)

                @block.vector
                def _(dve):
                    def maxima(c, tiles, w):
                        for j in range(tiles * G0 * NK):
                            dve.wait_ge(mu_full, b * UNITS + c * NU + j + 1)
                            dve.tensor_reduce(mx[0:w, j // NK, j % NK:j % NK + 1], pb[0:w, j % RING, 0:KC],
                                              AX.X, ALU.max, negate=True).then_inc(mu_free, 1)
                        n = tiles * G0
                        dve.wait_ge(mu_free, b * UNITS + c * NU + tiles * G0 * NK)
                        own = Chain(dve, dve_own[1], b * nchunk + c, 5)
                        own.link(dve.tensor_reduce(nm[0:w, 0, 0:n], mx[0:w, 0:n, :], AX.X, ALU.min))
                        own.link(dve.tensor_copy(nsp[0:w, 0:n, 0], nm[0:w, 0, 0:n]))
                        own.link(dve.tensor_tensor(nm[0:w, 1, 0:n], nm[0:w, 0, 0:n], nsp[0:w, 0:n, 0], ALU.subtract))
                        own.link(dve.tensor_copy(nsp[0:w, 0:n, 1], nm[0:w, 1, 0:n]))
                        own.link(dve.tensor_tensor(nm[0:w, 0, 0:n], nm[0:w, 1, 0:n], nsp[0:w, 0:n, 1], ALU.subtract))
                        dve.tensor_copy(nsp[0:w, 0:n, 2], nm[0:w, 0, 0:n]).then_inc(n_ready, 1)
                        own.end()
                        dve.wait_ge(rows_full, b * nchunk + c + 1)
                        cols = tiles * w
                        dve.tensor_copy(Qs[M0:M0 + 3, :, bass.ds(c * QC, cols)],
                                        pb[M0:M0 + 3, 0:3, :].rearrange("p a n -> p (a n)")[:, 0:G0 * cols].rearrange(
                                            "p (h n) -> p h n", h=G0)).then_inc(rows_ready, 1)

                    with dve.Fori(0, NQ) as c:
                        maxima(c, 3, P)
                    maxima(NQ, 1, LAST)

                @block.scalar
                def _(act):
                    def exps(c, w):
                        for s in range(STEPS):
                            m = P if s < NT - 1 else LAST
                            g = b * nchunk * STEPS + c * STEPS + s
                            if s == 0:
                                act.wait_ge(pv_done, g)
                            elif s > 1:
                                act.wait_ge(pv_done, g - 1)
                            for pair in range(2):
                                act.wait_ge(s_full, g * 2 + pair + 1)
                                act.activation(prob[0:m, s % 2, 2 * pair:2 * pair + 2, 0:w],
                                               pb[0:m, 4 + 2 * pair:6 + 2 * pair, 0:w], ACT.Exp).then_inc(p_full, 1)
                        act.wait_ge(pv_done, b * nchunk * STEPS + c * STEPS + STEPS)
                        act.activation(O[:, bass.ds(c * QC, w)], pb[:, 3, 0:w], ACT.Copy).then_inc(o_read, 1)

                    with act.Fori(0, NQ) as c:
                        exps(c, QC)
                    exps(NQ, LAST)

            with nc.Block() as block:
                @block.tensor
                def _(pe):
                    for c in range(NK):
                        cols = slice(c * KC, (c + 1) * KC)
                        if c >= 2:
                            pe.wait_ge(zr_ready, b * NK + c - 1)
                        pe.matmul(pb[:, c % 2, 0:KC], selz[:], O[:, cols], start=True, stop=True).then_inc(z_done, 1)
                    pe.wait_ge(o_ready, (b + 1) * NK)
                    for t in range(NT):
                        w = P if t < NT - 1 else LAST
                        dst = pb[0:w, 2 + t // 8, t % 8 * C:(t % 8 + 1) * C]
                        pe.matmul(dst, O[:, t * P:t * P + w], wp[:], start=True, stop=False)
                        last = pe.matmul(dst, one[:, 0:w], bp[:], start=False, stop=True)
                    last.then_inc(pr_done, 1)
                    turn_tensor(pe, xh, pb, ident, S, b * 3 + 1)

                @block.vector
                def _(dve):
                    own = Chain(dve, dve_own[2], b, 7)
                    for c in range(NK):
                        cols = slice(c * KC, (c + 1) * KC)
                        dve.wait_ge(z_done, b * NK + c + 1)
                        if c >= 2:
                            dve.wait_ge(o_ready, b * NK + c - 1)
                        dve.reciprocal(zr[:, c % 2, 0:KC], pb[:, c % 2, 0:KC]).then_inc(zr_ready, 1)
                        dve.wait_ge(zr_ready, b * NK + c + 1)
                        dve.tensor_tensor(O[:, cols], O[:, cols], zr[:, c % 2, 0:KC], ALU.mult).then_inc(o_ready, 1)
                    dve.wait_ge(pr_done, b + 1)
                    for g in range(3):
                        dve.tensor_tensor(H[:, 8 * g:8 * g + 8, :], H[:, 8 * g:8 * g + 8, :],
                                          pb[:, 2 + g, :].rearrange("p (t c) -> p t c", t=8), ALU.add)
                    own.link(dve.tensor_tensor(H[0:LAST, NT - 1, :], H[0:LAST, NT - 1, :], pb[0:LAST, 5, 0:C], ALU.add))
                    ln_vector(dve, own, H, xh, sq, stat, S, b * 3 + 1)
                    own.end()

                @block.scalar
                def _(act):
                    ln_scalar(act, stat, S, b * 3 + 1)
                    turn_scalar(act, xT, pb, S, b * 3 + 1)

            CHUNKS = [(c * QC, QC) for c in range(NQ)] + [(NQ * QC, P)]
            with nc.Block() as block:
                @block.tensor
                def _(pe):
                    for c, (c0, w) in enumerate(CHUNKS):
                        if c >= 4:
                            pe.wait_ge(rh_ready, b * len(CHUNKS) + c - 3)
                        pe.matmul(pb[0:32, c % 4, 0:w], rw1[:], xT[:, c0:c0 + w], start=True, stop=True).then_inc(rh_done, 1)
                    pe.wait_ge(rh_ready, (b + 1) * len(CHUNKS))
                    for t in range(NT):
                        last = pe.matmul(pb[:, 4, t * E0:(t + 1) * E0], rh[:, t * P:(t + 1) * P], rw2[:], start=True, stop=True)
                    last.then_inc(lg_done, 1)

                @block.scalar
                def _(act):
                    for c, (c0, w) in enumerate(CHUNKS):
                        act.wait_ge(rh_done, b * len(CHUNKS) + c + 1)
                        act.activation(rh[0:32, c0:c0 + w], pb[0:32, c % 4, 0:w], ACT.Relu).then_inc(rh_ready, 1)
                    act.wait_ge(lg_ready, b + 1)
                    act.activation(rt[:, 0], rt[:, 0], ACT.Exp).then_inc(lg_exp, 1)
                    act.wait_ge(two_ready, b + 1)
                    act.activation(rs[:, 3], rs[:, 2], ACT.Exp).then_inc(two_exp, 1)

                @block.vector
                def _(dve):
                    own = Chain(dve, dve_own[3], b, 23)
                    wide = lambda a: a.unsqueeze(2).to_broadcast([P, NT, E0])
                    tt = lambda o, a, c, op: own.link(dve.tensor_tensor(o, a, c, op))
                    dve.wait_ge(lg_done, b + 1)
                    lg = pb[:, 4, 0:NT * E0].rearrange("p (t e) -> p t e", e=E0)
                    own.link(dve.tensor_reduce(rs[:, 0], lg, AX.X, ALU.max))
                    dve.tensor_tensor(rt[:, 0], lg, wide(rs[:, 0]), ALU.subtract).then_inc(lg_ready, 1)
                    dve.wait_ge(lg_exp, b + 1)
                    own.link(dve.tensor_reduce(rs[:, 0], rt[:, 0], AX.X, ALU.add))
                    own.link(dve.reciprocal(rs[:, 1], rs[:, 0]))
                    tt(rt[:, 0], rt[:, 0], wide(rs[:, 1]), ALU.mult)
                    for k in range(2):
                        own.link(dve.tensor_reduce(rs[:, k], rt[:, 0], AX.X, ALU.max))
                        tt(rt[:, 1], rt[:, 0], wide(rs[:, k]), ALU.is_equal)
                        own.link(dve.tensor_scalar(rt[:, 2], iota[:], float(E0), None, ALU.subtract))
                        tt(rt[:, 3], rt[:, 1], rt[:, 2], ALU.mult)
                        own.link(dve.tensor_reduce(rs[:, 2], rt[:, 3], AX.X, ALU.min))
                        tt(rt[:, 4 + k], rt[:, 2], wide(rs[:, 2]), ALU.is_equal)
                        if k == 0:
                            own.link(dve.tensor_scalar(rt[:, 6], rt[:, 4], 2.0, None, ALU.mult))
                            tt(rt[:, 0], rt[:, 0], rt[:, 6], ALU.subtract)
                    dve.tensor_tensor(rs[:, 2], rs[:, 1], rs[:, 0], ALU.subtract).then_inc(two_ready, 1)
                    dve.wait_ge(two_exp, b + 1)
                    own.link(dve.tensor_scalar(rs[:, 0], rs[:, 3], 1.0, None, ALU.add))
                    own.link(dve.reciprocal(rs[:, 1], rs[:, 0]))
                    tt(rs[:, 2], rs[:, 1], rs[:, 3], ALU.mult)
                    tt(rt[:, 4], rt[:, 4], wide(rs[:, 1]), ALU.mult)
                    tt(rt[:, 5], rt[:, 5], wide(rs[:, 2]), ALU.mult)
                    dve.tensor_tensor(W[:], rt[:, 4], rt[:, 5], ALU.add)
                    own.end()

            NC_ = len(CHUNKS)
            with nc.Block() as block:
                @block.tensor
                def _(pe):
                    def ups(c):
                        c0, w = CHUNKS[c]
                        for k in range(3):
                            n = b * NC_ * 3 + c * 3 + k
                            if c or k >= 2:
                                pe.wait_ge(h1_ready, n - 1)
                            pe.matmul(pb[:, (c * 3 + k) % 2, 0:w], ew1[:, k, :], xT[:, c0:c0 + w], start=True, stop=True).then_inc(h1_done, 1)

                    def mids(c):
                        c0, w = CHUNKS[c]
                        for k in range(3):
                            n = b * NC_ * 3 + c * 3 + k
                            pe.wait_ge(h1_ready, n + 1)
                            if c or k >= 2:
                                pe.wait_ge(h2_ready, n - 1)
                            pe.matmul(pb[:, 2 + (c * 3 + k) % 2, 0:w], ew2[:, k, :], h1[:, k, 0:w], start=True, stop=True).then_inc(h2_done, 1)

                    def downs(c):
                        c0, w = CHUNKS[c]
                        pe.wait_ge(h2_ready, b * NC_ * 3 + c * 3 + 3)
                        for t in range(w // P):
                            n = c * 3 + t
                            if n >= 2:
                                pe.wait_ge(ye_read, b * NT + n - 1)
                            dst = pb[:, 4 + n % 2, 0:3 * P]
                            pe.matmul(dst, one[:], eb3[:], start=True, stop=False)
                            for k in range(3):
                                last = pe.matmul(dst[:, k * P:(k + 1) * P], h2[:, c % 2, k, t * P:(t + 1) * P], ew3[:, k, :],
                                                 start=False, stop=(k == 2))
                            last.then_inc(ye_done, 1)

                    for c in range(NC_):
                        ups(c)
                        mids(c)
                        if c:
                            downs(c - 1)
                    downs(NC_ - 1)

                @block.scalar
                def _(act):
                    for c, (c0, w) in enumerate(CHUNKS):
                        for k in range(3):
                            n = b * NC_ * 3 + c * 3 + k
                            act.wait_ge(h1_done, n + 1)
                            if c:
                                act.wait_ge(h2_done, n - 2)
                            act.activation(h1[:, k, 0:w], pb[:, (c * 3 + k) % 2, 0:w], ACT.Relu).then_inc(h1_ready, 1)
                        for k in range(3):
                            n = b * NC_ * 3 + c * 3 + k
                            act.wait_ge(h2_done, n + 1)
                            if c >= 2:
                                act.wait_ge(ye_done, b * NT + (c - 1) * 3)
                            act.activation(h2[:, c % 2, k, 0:w], pb[:, 2 + (c * 3 + k) % 2, 0:w], ACT.Relu, bias=eb2[:, k:k + 1]).then_inc(h2_ready, 1)
                    ln_scalar(act, stat, S, b * 3 + 2)

                @block.vector
                def _(dve):
                    own = Chain(dve, dve_own[4], b, 2 * NT + 6)
                    for t in range(NT):
                        dve.wait_ge(ye_done, b * NT + t + 1)
                        dve.tensor_tensor(yw[:, t % 2], pb[:, 4 + t % 2, 0:3 * P].rearrange("p (e c) -> p e c", e=E0),
                                          W[:, t, :].unsqueeze(2).to_broadcast([P, E0, C]), ALU.mult).then_inc(ye_read, 1)
                        dve.wait_ge(ye_read, b * NT + t + 1)
                        own.link(dve.tensor_reduce(ya[:], yw[:, t % 2].rearrange("p e c -> p c e"), AX.X, ALU.add))
                        own.link(dve.tensor_tensor(H[:, t, :], H[:, t, :], ya[:], ALU.add))
                    ln_vector(dve, own, H, xh, sq, stat, S, b * 3 + 2)
                    own.end()

            with nc.Block() as block:
                @block.tensor
                def _(pe):
                    turn_tensor(pe, xh, pb, ident, S, b * 3 + 2)

                @block.sync
                def _(sp):
                    sp.dma_start(h_tm[bass.ds(b * N, (NT - 1) * P), :].rearrange("(t p) c -> p t c", p=P), H[:, 0:NT - 1, :]).then_inc(stored, 16)
                    sp.dma_start(h_tm[bass.ds(b * N + (NT - 1) * P, LAST), :], H[0:LAST, NT - 1, :]).then_inc(stored, 16)
                    sp.wait_ge(S["xT"], (b * 3 + 3) * len(GROUPS))
                    sp.sem_inc(S["sp_passed"])
                    sp.dma_start(x_cm[:, bass.ds(b * N, N)], xT[0:C, 0:N]).then_inc(stored, 16)
                    sp.wait_ge(stored, (b + 1) * 48)
                    sp.sem_inc(S["sp_passed"])

                @block.scalar
                def _(act):
                    turn_scalar(act, xT, pb, S, b * 3 + 2)


H1 = 8
NI = N // 3
PI = NI // 8
UC = 2 * KC
UT = N // UC
UH = NT * UT
RC = 3


def phase_c(nc, io, x_cm, nmx_all, es_all, diag_all):
    with ExitStack() as ctx:
        sb = lambda n, s, d=F32: ctx.enter_context(nc.sbuf_tensor("c_" + n, s, d))
        sem = lambda n: ctx.enter_context(nc.semaphore("c_s_" + n))
        xqk = sb("xqk", [C + 1, 2, 2, NI])
        wh = sb("wh", [C + 1, 2, 3, C])
        scale = sb("scale", [P, 1])
        ones = sb("ones", [C, 1])
        y = sb("y", [P, N])
        rest = sb("rest", [P, N])
        parts = sb("parts", [P, 3, N], BF16)
        kd = sb("kd", [C, N])
        prod = sb("prod", [C, N])
        stack = sb("stack", [P, 2, 5, N], BF16)
        nmx = sb("nmx", [P, 2, NT, UT])
        es = sb("es", [P, 2, NT, UT])
        diag = sb("diag", [P, 2, NT])
        pb = ctx.enter_context(nc.psum_tensor("c_ps", [P, 8, 512], F32))
        set_up = sem("set_up")
        x_in = sem("x_in")
        w_in = sem("w_in")
        pj_full = sem("pj_full")
        y_ready = sem("y_ready")
        part_ready = sem("part_ready")
        sub_done = sem("sub_done")
        kd_in = sem("kd_in")
        prod_ready = sem("prod_ready")
        stacked = sem("stacked")
        dg_full = sem("dg_full")
        dg_read = sem("dg_read")
        s_full = sem("s_full")
        max_done = sem("max_done")
        exp_done = sem("exp_done")
        results = sem("results")
        passed = {e: sem("passed_" + e) for e in ("sp", "pe", "dve", "act", "pool")}
        COPIES = ((0, 0, 0, 0), (0, 1, 0, 0), (2, 0, 0, 0), (3, 0, 1, 0), (4, 1, 1, 0),
                  (1, 0, 0, 1), (1, 1, 0, 1), (3, 1, 1, 1),
                  (2, 1, 0, 2), (4, 0, 1, 2))
        PAIRS = ((3, 0), (3, 1), (4, 2))
        HEADS = NB * H1

        def bodies(eng, front, main):
            front(0, 0)
            main(0, 0, lambda part: front(1, 1, part))
            main(1, 1, lambda part: front(2, 0, part))
            with eng.Fori(2, HEADS - 2, 2) as G:
                main(G, 0, lambda part: front(G + 1, 1, part))
                main(G + 1, 1, lambda part: front(G + 2, 0, part))
            main(HEADS - 2, 0, lambda part: front(HEADS - 1, 1, part))
            main(HEADS - 1, 1, None)

        with nc.Block() as block:
            @block.sync
            def _(sp):
                sp.dma_start(scale[:], io["scale1"]).then_inc(set_up, 16)
                sp.wait_ge(set_up, 16)

            @block.vector
            def _(dve):
                dve.memset(xqk[C:C + 1, :, :, :], 1.0)
                dve.memset(ones[:], 1.0)
                dve.memset(nmx[:], 0.0)
                dve.memset(es[:], 1.0)
                dve.memset(diag[:], 0.0)

        with nc.Block() as block:
            @block.sync
            def _(sp):
                def front(G, buf, part=None):
                    if part in (None, 0):
                        if not (isinstance(G, int) and G < 2):
                            sp.wait_ge(y_ready, (G - 1) * 8)
                        for s in range(2):
                            sp.dma_start(xqk[0:C, buf, s, :], x_cm[:, bass.ds((G // H1) * NI + s * NB * NI, NI)]).then_inc(x_in, 16)
                        sp.dma_start(wh[:, buf, :, :], io["w_qk"][bass.ds(G % H1, 1)].rearrange("o c j d -> (o c) j d")).then_inc(w_in, 16)
                    if part in (None, 1):
                        sp.wait_ge(prod_ready, G)
                        sp.wait_ge(y_ready, (G + 1) * 8)
                        sp.dma_start(kd[:], y[C:P, :]).then_inc(kd_in, 16)
                        if not (isinstance(G, int) and G < 2):
                            sp.wait_ge(s_full, (G - 1) * UH)
                        for n, (slot, half, s, p) in enumerate(COPIES):
                            if n in (0, 5, 8):
                                sp.wait_ge(part_ready, G * 3 + p + 1)
                            sp.dma_start(stack[half * C:(half + 1) * C, buf, slot, :], parts[s * C:(s + 1) * C, p, :]).then_inc(stacked, 16)

                def main(G, buf, nxt):
                    if nxt:
                        nxt(0)
                        nxt(1)
                    sp.wait_ge(exp_done, (G + 1) * UH)
                    sp.wait_ge(dg_read, G + 1)
                    for src, dst in ((nmx[:, buf].rearrange("p t u -> p (t u)"), nmx_all), (es[:, buf].rearrange("p t u -> p (t u)"), es_all),
                                     (diag[:, buf], diag_all)):
                        sp.dma_start(dst[:, bass.ds(G, 1), :].rearrange("p g n -> p (g n)"), src).then_inc(results, 16)

                bodies(sp, front, main)
                sp.wait_ge(results, HEADS * 48)

            @block.tensor
            def _(pe):
                pe.wait_ge(set_up, 16)

                def chunk(G, buf, c):
                    if c == 0:
                        pe.wait_ge(x_in, (G + 1) * 32)
                        pe.wait_ge(w_in, (G + 1) * 16)
                    pe.wait_ge(y_ready, G * 8 + c)
                    for s in range(2):
                        for j in range(3):
                            last = pe.matmul(pb[s * C:(s + 1) * C, 6, j * PI:(j + 1) * PI], wh[:, buf, j, :],
                                             xqk[:, buf, s, c * PI:(c + 1) * PI], start=True, stop=True)
                    last.then_inc(pj_full, 1)

                def front(G, buf, part=None):
                    for c in (range(8) if part is None else (part,) if part < 8 else ()):
                        chunk(G, buf, c)

                def main(G, buf, nxt):
                    base = G * UH
                    pe.wait_ge(stacked, (G + 1) * 16 * len(COPIES))
                    pe.wait_ge(prod_ready, G + 1)
                    pe.wait_ge(dg_read, G)
                    for t in range(NT):
                        w = P if t < NT - 1 else LAST
                        last = pe.matmul(pb[0:w, 7, t:t + 1], prod[:, t * P:t * P + w], ones[:], start=True, stop=True)
                    last.then_inc(dg_full, 1)
                    for t in range(NT):
                        w = P if t < NT - 1 else LAST
                        for u in range(UT):
                            j = t * UT + u
                            if j < RC:
                                if not (isinstance(G, int) and G == 0):
                                    pe.wait_ge(exp_done, base)
                            else:
                                pe.wait_ge(exp_done, base + j - RC + 1)
                            r = j % RC * 2
                            for n, (k, q) in enumerate(PAIRS):
                                for half in range(2):
                                    c0 = u * UC + half * KC
                                    last = pe.matmul(pb[0:w, r + half, 0:KC], stack[:, buf, k, t * P:t * P + w],
                                                     stack[:, buf, q, c0:c0 + KC], start=(n == 0), stop=(n == 2))
                            last.then_inc(s_full, 1)
                        if nxt and t < 8:
                            nxt(t)

                bodies(pe, front, main)

            @block.vector
            def _(dve):
                def front(G, buf, part=None):
                    for p in (range(3) if part is None else (part,)):
                        if p == 0:
                            dve.wait_ge(y_ready, (G + 1) * 8)
                            dve.wait_ge(stacked, G * 16 * len(COPIES))
                        else:
                            dve.wait_ge(sub_done, G * 2 + p)
                        dve.tensor_copy(parts[:, p, :], y[:] if p == 0 else rest[:]).then_inc(part_ready, 1)

                def main(G, buf, nxt):
                    if not (isinstance(G, int) and G < 2):
                        dve.wait_ge(results, (G - 1) * 48)
                    for t in range(NT):
                        w = P if t < NT - 1 else LAST
                        for u in range(UT):
                            j = t * UT + u
                            dve.wait_ge(s_full, G * UH + j + 1)
                            dve.tensor_reduce(nmx[0:w, buf, t, u:u + 1], pb[0:w, j % RC * 2:j % RC * 2 + 2, 0:KC],
                                              AX.XY, ALU.max, negate=True).then_inc(max_done, 1)
                        if t == 0:
                            dve.wait_ge(dg_full, G + 1)
                            dve.tensor_copy(diag[:, buf, 0:NT - 1], pb[:, 7, 0:NT - 1])
                            dve.tensor_copy(diag[0:LAST, buf, NT - 1:NT], pb[0:LAST, 7, NT - 1:NT]).then_inc(dg_read, 1)
                        if nxt and t in (9, 13, 17):
                            nxt((t - 9) // 4)

                bodies(dve, front, main)

            @block.gpsimd
            def _(pool):
                def front(G, buf, part=None):
                    pool.wait_ge(part_ready, G * 3 + 1)
                    pool.tensor_tensor(rest[:], y[:], parts[:, 0, :], ALU.subtract).then_inc(sub_done, 1)
                    pool.wait_ge(part_ready, G * 3 + 2)
                    pool.wait_ge(sub_done, G * 2 + 1)
                    pool.tensor_tensor(rest[:], rest[:], parts[:, 1, :], ALU.subtract).then_inc(sub_done, 1)
                    pool.wait_ge(kd_in, (G + 1) * 16)
                    pool.wait_ge(dg_full, G)
                    pool.tensor_tensor(prod[:], y[0:C, :], kd[:], ALU.mult).then_inc(prod_ready, 1)

                def main(G, buf, nxt):
                    if nxt:
                        nxt(0)

                bodies(pool, front, main)

            @block.scalar
            def _(act):
                def front(G, buf, part=None):
                    for c in (range(8) if part is None else (part,)):
                        if c == 0:
                            act.wait_ge(prod_ready, G)
                            act.wait_ge(kd_in, G * 16)
                        act.wait_ge(pj_full, G * 8 + c + 1)
                        act.activation(y[:].rearrange("p (j i) -> p j i", j=3)[:, :, c * PI:(c + 1) * PI],
                                       pb[:, 6, 0:KC].rearrange("p (j i) -> p j i", j=3), ACT.Copy,
                                       scale=scale[:, 0:1]).then_inc(y_ready, 1)

                def main(G, buf, nxt):
                    if not (isinstance(G, int) and G < 2):
                        act.wait_ge(results, (G - 1) * 48)
                    for t in range(NT):
                        w = P if t < NT - 1 else LAST
                        for u in range(UT):
                            j = t * UT + u
                            act.wait_ge(max_done, G * UH + j + 1)
                            unit = pb[0:w, j % RC * 2:j % RC * 2 + 2, 0:KC]
                            act.activation(unit, unit, ACT.Exp, bias=nmx[0:w, buf, t, u:u + 1],
                                           accum_out=es[0:w, buf, t, u:u + 1]).then_inc(exp_done, 1)
                        if nxt and t < 8:
                            nxt(t)

                bodies(act, front, main)


E1 = 8
HID = 256


def segments():
    found = []
    for j in range(3):
        at, end = j * NI, (j + 1) * NI
        while at < end:
            t, p = divmod(at, P)
            if p == 0 and end - at >= P:
                n = (end - at) // P
                found.append((t, t + n, 0, P, j, at - j * NI))
                at += n * P
            else:
                n = min(end - at, P - p)
                if p and p + n > 64 > p:
                    n = 64 - p
                found.append((t, t + 1, p, p + n, j, at - j * NI))
                at += n
    return found


def phase_d(nc, io, x_cm, h_tm, nmx_all, es_all, diag_all, out):
    with ExitStack() as ctx:
        sb = lambda n, s, d=F32: ctx.enter_context(nc.sbuf_tensor("d_" + n, s, d))
        sem = lambda n: ctx.enter_context(nc.semaphore("d_s_" + n))
        HEADS = NB * H1
        SEG = segments()
        a_all = sb("a_all", [P, HEADS, NT])
        m_all = sb("m_all", [P, HEADS, NT])
        ab = sb("ab", [P, H1, NT])
        xv = sb("xv", [C + 1, NI])
        wv = sb("wv", [C + 1, 3, C * H1])
        w0 = sb("w0", [P, 4, C])
        b0 = sb("b0", [1, C])
        one = sb("one", [1, P])
        ident = sb("ident", [P, P])
        av = sb("av", [P, 2, C * H1])
        avT = sb("avT", [P, 2, 4 * P])
        xT = sb("xT", [C + 1, NP])
        H = sb("H", [P, NT, C])
        xh = sb("xh", [P, NT, C])
        sq = sb("sq", [P, NT, C])
        stat = sb("stat", [P, 4, NT])
        w1 = sb("w1", [C + 1, 2, P])
        wg = sb("wg", [P, 2, E1])
        bg = sb("bg", [1, E1])
        wd = sb("wd", [P, 2, E1 * C])
        bd = sb("bd", [1, E1 * C])
        iota = sb("iota", [P, NT, E1])
        hg = sb("hg", [P, 2, NP])
        rt = sb("rt", [P, 3, NT, E1])
        rs = sb("rs", [P, 2, NT])
        yw = sb("yw", [P, 2, E1, C])
        ya = sb("ya", [P, C])
        pb = ctx.enter_context(nc.psum_tensor("d_ps", [P, 8, 512], F32))
        loaded = sem("loaded")
        dve_own = [sem(f"dve_own{i}") for i in range(4)]
        s_low = sem("s_low")
        s_exp = sem("s_exp")
        d_low = sem("d_low")
        d_exp = sem("d_exp")
        h_in = sem("h_in")
        v_done = sem("v_done")
        av_ready = sem("av_ready")
        t_done = sem("t_done")
        avT_ready = sem("avT_ready")
        pr_done = sem("pr_done")
        S = {n: sem(n) for n in ("var", "std", "xh", "turned", "xT", "passed", "sp_passed")}
        hg_done = sem("hg_done")
        hg_ready = sem("hg_ready")
        lg_done = sem("lg_done")
        lg_ready = sem("lg_ready")
        lg_exp = sem("lg_exp")
        ye_done = sem("ye_done")
        ye_read = sem("ye_read")
        stored = sem("stored")

        with nc.Block() as block:
            @block.sync
            def _(sp):
                loads = ((wv, "wv1"), (w0, "w0"), (b0, "b0"), (ident, "ident"), (w1, "w1"), (wg, "wg"), (bg, "bg"),
                         (wd, "wd"), (bd, "bd"), (iota, "iota8"))
                for t, k in loads:
                    sp.dma_start(t[:], io[k]).then_inc(loaded, 16)
                sp.wait_ge(loaded, 16 * len(loads))

            @block.gpsimd
            def _(pool):
                pool.memset(xv[C:C + 1, :], 1.0)
                pool.memset(one[:], 1.0)

            @block.vector
            def _(dve):
                dve.memset(xT[0:C, N:NP], 0.0)
                dve.memset(xT[C:C + 1, :], 1.0)
                dve.memset(H[:], 0.0)
                own = Chain(dve, dve_own[0], 0, 5)
                nmx = nmx_all[:].rearrange("p g (t u) -> p g t u", u=UT)
                es = es_all[:].rearrange("p g (t u) -> p g t u", u=UT)
                flat = lambda x: x[:].rearrange("p g n -> p (g n)")
                own.link(dve.tensor_reduce(m_all[:], nmx, AX.X, ALU.min))
                dve.tensor_tensor(nmx, m_all[:].unsqueeze(3).to_broadcast([P, HEADS, NT, UT]), nmx, ALU.subtract).then_inc(s_low, 1)
                own.link(dve.tensor_tensor(flat(diag_all), flat(diag_all), flat(m_all), ALU.add))
                dve.tensor_copy(flat(a_all), flat(diag_all)).then_inc(d_low, 1)
                dve.wait_ge(s_exp, 1)
                own.link(dve.tensor_tensor(flat(es_all), flat(es_all), flat(nmx_all), ALU.mult))
                own.link(dve.tensor_reduce(m_all[:], es, AX.X, ALU.add))
                own.link(dve.reciprocal(flat(m_all), flat(m_all)))
                dve.wait_ge(d_exp, 1)
                dve.tensor_tensor(flat(a_all), flat(a_all), flat(m_all), ALU.mult)
                own.end()

            @block.scalar
            def _(act):
                act.wait_ge(s_low, 1)
                act.activation(nmx_all[:], nmx_all[:], ACT.Exp).then_inc(s_exp, 1)
                act.wait_ge(d_low, 1)
                act.activation(a_all[:], a_all[:], ACT.Exp).then_inc(d_exp, 1)

        with nc.Fori(0, NB) as b:
            with nc.Block() as block:
                nload = 1 + len(SEG)

                @block.sync
                def _(sp):
                    sp.dma_start(xv[0:C, :], x_cm[:, bass.ds((b + 2 * NB) * NI, NI)]).then_inc(h_in, 16)
                    rows = h_tm.rearrange("(m q) c -> q m c", q=3)
                    for t0, t1, p0, p1, j, i0 in SEG:
                        n = (t1 - t0) * (p1 - p0)
                        sp.dma_start(H[p0:p1, t0:t1, :], rows[j, bass.ds(b * NI + i0, n), :].rearrange(
                            "(t p) c -> p t c", p=p1 - p0)).then_inc(h_in, 16)
                    sp.wait_ge(h_in, (b + 1) * 16 * nload)
                    sp.sem_inc(S["sp_passed"])

                @block.tensor
                def _(pe):
                    pe.wait_ge(h_in, (b + 1) * 16 * nload)

                    def values(t):
                        if t >= 2:
                            pe.wait_ge(av_ready, b * NT + t - 1)
                        for t0, t1, p0, p1, j, i0 in SEG:
                            if t0 <= t < t1:
                                i = i0 + (t - t0) * P
                                last = pe.matmul(pb[p0:p1, t % 2, :], xv[:, i:i + p1 - p0], wv[:, j, :], start=True, stop=True)
                        last.then_inc(v_done, 1)

                    def turn(t):
                        w = P if t < NT - 1 else LAST
                        pe.wait_ge(av_ready, b * NT + t + 1)
                        if t >= 2:
                            pe.wait_ge(avT_ready, b * NT + t - 1)
                        for k in range(4):
                            last = pe.transpose(pb[:, 2 + t % 2, k * P:k * P + w], av[0:w, t % 2, k * P:(k + 1) * P], ident[0:w, 0:w])
                        last.then_inc(t_done, 1)

                    def project(t):
                        w = P if t < NT - 1 else LAST
                        pe.wait_ge(avT_ready, b * NT + t + 1)
                        dst = pb[0:w, 4 + t // 8, t % 8 * C:(t % 8 + 1) * C]
                        pe.matmul(dst, one[:, 0:w], b0[:], start=True, stop=False)
                        for k in range(4):
                            last = pe.matmul(dst, avT[:, t % 2, k * P:k * P + w], w0[:, k, :], start=False, stop=(k == 3))
                        last.then_inc(pr_done, 1)

                    for t in range(NT + 2):
                        if t < NT:
                            values(t)
                        if 1 <= t <= NT:
                            turn(t - 1)
                        if t >= 2:
                            project(t - 2)
                    turn_tensor(pe, xh, pb, ident, S, b)

                @block.vector
                def _(dve):
                    own = Chain(dve, dve_own[1], b, 8)
                    own.link(dve.tensor_copy(ab[:], a_all[:, bass.ds(b * H1, H1), :]))
                    for t in range(NT):
                        w = P if t < NT - 1 else LAST
                        dve.wait_ge(v_done, b * NT + t + 1)
                        if t >= 2:
                            dve.wait_ge(t_done, b * NT + t - 1)
                        dve.tensor_tensor(av[0:w, t % 2, :].rearrange("p (d h) -> p d h", h=H1),
                                          pb[0:w, t % 2, :].rearrange("p (d h) -> p d h", h=H1),
                                          ab[0:w, :, t].unsqueeze(1).to_broadcast([w, C, H1]), ALU.mult).then_inc(av_ready, 1)
                    dve.wait_ge(pr_done, (b + 1) * NT)
                    for g in range(3):
                        last = dve.tensor_tensor(H[:, 8 * g:8 * g + 8, :], H[:, 8 * g:8 * g + 8, :],
                                                 pb[:, 4 + g, :].rearrange("p (t c) -> p t c", t=8), ALU.add)
                    own.link(dve.tensor_tensor(H[0:LAST, NT - 1, :], H[0:LAST, NT - 1, :], pb[0:LAST, 7, 0:C], ALU.add))
                    ln_vector(dve, own, H, xh, sq, stat, S, b)
                    own.end()

                @block.scalar
                def _(act):
                    for t in range(NT):
                        w = P if t < NT - 1 else LAST
                        act.wait_ge(t_done, b * NT + t + 1)
                        if t >= 2:
                            act.wait_ge(pr_done, b * NT + t - 1)
                        view = lambda x: x.rearrange("p (k n) -> p k n", k=4)[:, :, 0:w]
                        act.activation(view(avT[:, t % 2, :]), view(pb[:, 2 + t % 2, :]), ACT.Copy).then_inc(avT_ready, 1)
                    ln_scalar(act, stat, S, b)
                    turn_scalar(act, xT, pb, S, b)

            CHUNKS = [(c * QC, QC) for c in range(NQ)] + [(NQ * QC, P)]
            ND = 2 * len(CHUNKS)
            with nc.Block() as block:
                @block.tensor
                def _(pe):
                    for c, (c0, w) in enumerate(CHUNKS):
                        for k in range(2):
                            n = c * 2 + k
                            if n >= 4:
                                pe.wait_ge(hg_ready, b * ND + n - 3)
                            pe.matmul(pb[:, n % 4, 0:w], w1[:, k, :], xT[:, c0:c0 + w], start=True, stop=True).then_inc(hg_done, 1)
                    pe.wait_ge(hg_ready, (b + 1) * ND)
                    for t in range(NT):
                        dst = pb[:, 4, t * E1:(t + 1) * E1]
                        pe.matmul(dst, one[:], bg[:], start=True, stop=False)
                        for k in range(2):
                            last = pe.matmul(dst, hg[:, k, t * P:(t + 1) * P], wg[:, k, :], start=False, stop=(k == 1))
                    last.then_inc(lg_done, 1)
                    for t in range(NT):
                        if t >= 3:
                            pe.wait_ge(ye_read, b * NT + t - 2)
                        dst = pb[:, 5 + t % 3, :]
                        pe.matmul(dst, one[:], bd[:], start=True, stop=False)
                        for k in range(2):
                            last = pe.matmul(dst, hg[:, k, t * P:(t + 1) * P], wd[:, k, :], start=False, stop=(k == 1))
                        last.then_inc(ye_done, 1)

                @block.scalar
                def _(act):
                    for c, (c0, w) in enumerate(CHUNKS):
                        for k in range(2):
                            n = c * 2 + k
                            act.wait_ge(hg_done, b * ND + n + 1)
                            act.activation(hg[:, k, c0:c0 + w], pb[:, n % 4, 0:w], ACT.Gelu).then_inc(hg_ready, 1)
                    act.wait_ge(lg_ready, b + 1)
                    act.activation(rt[:, 0], rt[:, 0], ACT.Exp).then_inc(lg_exp, 1)

                @block.vector
                def _(dve):
                    own = Chain(dve, dve_own[2], b, 10 + 2 * NT - 1)
                    wide = lambda a: a.unsqueeze(2).to_broadcast([P, NT, E1])
                    tt = lambda o, a, c, op: own.link(dve.tensor_tensor(o, a, c, op))
                    dve.wait_ge(lg_done, b + 1)
                    lg = pb[:, 4, 0:NT * E1].rearrange("p (t e) -> p t e", e=E1)
                    own.link(dve.tensor_reduce(rs[:, 0], lg, AX.X, ALU.max))
                    dve.tensor_tensor(rt[:, 0], lg, wide(rs[:, 0]), ALU.subtract).then_inc(lg_ready, 1)
                    dve.wait_ge(lg_exp, b + 1)
                    own.link(dve.tensor_reduce(rs[:, 0], rt[:, 0], AX.X, ALU.add))
                    own.link(dve.reciprocal(rs[:, 1], rs[:, 0]))
                    tt(rt[:, 0], rt[:, 0], wide(rs[:, 1]), ALU.mult)
                    own.link(dve.tensor_reduce(rs[:, 0], rt[:, 0], AX.X, ALU.max))
                    tt(rt[:, 1], rt[:, 0], wide(rs[:, 0]), ALU.is_equal)
                    tt(rt[:, 2], rt[:, 1], iota[:], ALU.mult)
                    own.link(dve.tensor_reduce(rs[:, 1], rt[:, 2], AX.X, ALU.min))
                    tt(rt[:, 1], iota[:], wide(rs[:, 1]), ALU.is_equal)
                    tt(rt[:, 0], rt[:, 0], rt[:, 1], ALU.mult)
                    for t in range(NT):
                        dve.wait_ge(ye_done, b * NT + t + 1)
                        dve.tensor_tensor(yw[:, t % 2], pb[:, 5 + t % 3, :].rearrange("p (e c) -> p e c", e=E1),
                                          rt[:, 0, t, :].unsqueeze(2).to_broadcast([P, E1, C]), ALU.mult).then_inc(ye_read, 1)
                        dve.wait_ge(ye_read, b * NT + t + 1)
                        own.link(dve.tensor_reduce(ya[:], yw[:, t % 2].rearrange("p e c -> p c e"), AX.X, ALU.add))
                        last = dve.tensor_tensor(H[:, t, :], H[:, t, :], ya[:], ALU.add)
                        if t < NT - 1:
                            own.link(last)
                    own.end()

            with nc.Block() as block:
                @block.sync
                def _(sp):
                    rows = out.rearrange("b (i j) c -> (b i) j c", j=3)
                    for t0, t1, p0, p1, j, i0 in SEG:
                        n = (t1 - t0) * (p1 - p0)
                        sp.dma_start(rows[bass.ds(b * NI + i0, n), j, :].rearrange("(t p) c -> p t c", p=p1 - p0),
                                     H[p0:p1, t0:t1, :]).then_inc(stored, 16)
                    sp.wait_ge(stored, (b + 1) * 16 * len(SEG))
                    sp.sem_inc(S["sp_passed"])


def build(nc, out, **io):
    with ExitStack() as ctx:
        h_cm = nc.dram_tensor("h_cm", [C, NB * N], F32, kind="Internal").ap()
        x_cm = nc.dram_tensor("x_cm", [C, NB * N], F32, kind="Internal").ap()
        h_tm = nc.dram_tensor("h_tm", [NB * N, C], F32, kind="Internal").ap()
        phase_a(nc, io, h_cm)
        phase_b(nc, io, h_cm, x_cm, h_tm)
        nmx_all = ctx.enter_context(nc.sbuf_tensor("nmx_all", [P, NB * H1, UH], F32))
        es_all = ctx.enter_context(nc.sbuf_tensor("es_all", [P, NB * H1, UH], F32))
        diag_all = ctx.enter_context(nc.sbuf_tensor("diag_all", [P, NB * H1, NT], F32))
        phase_c(nc, io, x_cm, nmx_all, es_all, diag_all)
        phase_d(nc, io, x_cm, h_tm, nmx_all, es_all, diag_all, out)


def layout(a):
    import numpy as np

    d = {}
    half = lambda w: np.tile(w, (2, 1))
    with_bias = lambda w, b: np.concatenate([w, b[None]], 0)
    d["x"], d["txt"] = a["x"], a["txt"].transpose(2, 0, 1)
    d["tok_w1"] = np.tile(a["L0_tok_w1"].reshape(C, 3, C).transpose(2, 1, 0), (1, 1, 2))
    d["tok_b1"] = half(a["L0_tok_b1"].reshape(C, 3))
    d["tok_w2"] = half(a["L0_tok_w2"].T.reshape(NH, C // NH, C).transpose(1, 0, 2).reshape(C, C))
    d["tok_b2"] = a["L0_tok_b2"].reshape(C, 1)
    d["pos"] = a["L0_tok_pos_emb"].reshape(1, 2 * WS - 1, 2 * WS - 1)
    lane = np.arange(P)
    d["head_mask"] = (lane[:, None] % NH == np.arange(NH)).astype(np.float32)
    d["ident"] = np.eye(P, dtype=np.float32)
    token = np.arange(WT)
    row = (token[:, None] >= WT // 2) != (token[None] >= WT // 2)
    col = row.reshape(WS, WS, WS, WS).transpose(1, 0, 3, 2).reshape(WT, WT)
    unmet = np.zeros((HW, WT, WR, 2, WT), np.float32)
    unmet[:, :, WR - 1] += np.where(row, np.float32(MASKED), np.float32(0))[None, :, None]
    unmet[HW - 1, :, :, 1] += np.where(col, np.float32(MASKED), np.float32(0))[:, None]
    d["masks"] = unmet.reshape(HT, WR, 2, WT)
    wq, bq = a["L0_attn_W_qkv"], a["L0_attn_b_qkv"]
    d["wqk"] = with_bias(wq[:2 * C].T, bq[:2 * C])
    d["wv"] = with_bias(wq[2 * C:].T, bq[2 * C:])
    d["scale"] = np.where(lane[:, None] < C, D0 ** -0.5, 1.0).astype(np.float32)
    d["scale1"] = np.where(lane[:, None] < C, C ** -0.5, 1.0).astype(np.float32)
    wp = np.zeros((G0, 32, C), np.float32)
    wp[:, :D0] = a["L0_attn_W_proj"].T.reshape(G0, D0, C)
    d["wp"], d["bp"] = wp.reshape(P, C), a["L0_attn_b_proj"][None]
    d["selz"] = ((lane[:, None] % 32 == D0) & (lane[:, None] // 32 == lane[None] // 32)).astype(np.float32)
    d["rw1"] = with_bias(a["L0_ffn_router_w1"], a["L0_ffn_router_b1"])
    d["rw2"] = with_bias(a["L0_ffn_router_w2"], a["L0_ffn_router_b2"])
    w = a["L0_ffn_expert_w1"].reshape(3, 2, C, C).transpose(2, 0, 1, 3).reshape(C, 3, P)
    d["ew1"] = np.concatenate([w, a["L0_ffn_expert_b1"].reshape(1, 3, P)], 0)
    for k, n in (("ew2", "L0_ffn_expert_w2"), ("ew3", "L0_ffn_expert_w3")):
        z = np.zeros((2, C, 3, 2, C), np.float32)
        for e in range(2):
            z[e, :, :, e, :] = a[n].reshape(3, 2, C, C)[:, e].transpose(1, 0, 2)
        d[k] = z.reshape(P, 3, P)
    d["eb2"] = a["L0_ffn_expert_b2"].reshape(3, P).T
    d["eb3"] = a["L0_ffn_expert_b3"].reshape(1, 3 * P)
    d["iota"] = np.broadcast_to(np.arange(E0, dtype=np.float32), (P, NT, E0))
    d["iota8"] = np.broadcast_to(np.arange(E1, dtype=np.float32) - E1, (P, NT, E1))
    w = np.concatenate([a["L1_attn_Wqkv"], a["L1_attn_bqkv"][None]], 0)
    d["w_qk"] = w.reshape(C + 1, 3, C, H1).transpose(3, 0, 1, 2)
    d["wv1"] = w.reshape(C + 1, 3, C * H1)
    d["w0"] = a["L1_attn_W0"].reshape(4, P, C).transpose(1, 0, 2)
    d["b0"] = a["L1_attn_b0"][None]
    d["w1"] = with_bias(a["L1_ffn_W1"], a["L1_ffn_b1"]).reshape(C + 1, 2, P)
    d["wg"] = a["L1_ffn_Wg"].reshape(2, P, E1).transpose(1, 0, 2)
    d["bg"] = a["L1_ffn_bg"][None]
    d["wd"] = a["L1_ffn_Wd"].transpose(1, 0, 2).reshape(2, P, E1 * C).transpose(1, 0, 2)
    d["bd"] = a["L1_ffn_bd"].reshape(1, E1 * C)
    return {k: np.ascontiguousarray(v) for k, v in d.items()}


def kernel(**inputs):
    import numpy as _np
    import concourse.bacc as _bacc
    from concourse.bass_utils import run_bass_kernel_spmd as _run

    nc = _bacc.Bacc("TRN2", target_bir_lowering=False, num_devices=1)
    arrays, io = {}, {}
    for name, a in layout({k: _np.asarray(v) for k, v in inputs.items()}).items():
        arrays["in_" + name] = a
        io[name] = nc.dram_tensor("in_" + name, a.shape, mybir.dt.from_np(a.dtype), kind="ExternalInput").ap()
    out = nc.dram_tensor("out_0", (NB, N, C), F32, kind="ExternalOutput").ap()
    build(nc, out, **io)
    r = _run(nc, [arrays], core_ids=[0])
    return r.results[0]["out_0"]
```

```python
from contextlib import ExitStack

import concourse.bass as bass
from concourse import mybir

F32 = mybir.dt.float32
BF16 = mybir.dt.bfloat16
F32R = mybir.dt.float32r
ALU = mybir.AluOpType
ACT = mybir.ActivationFunctionType
AX = mybir.AxisListType

NB = 4
C = 64
SIDE = 56
IMG = SIDE * SIDE
TXT = 32
N = IMG + TXT
P = 128
NT = 25
LAST = N - (NT - 1) * P
WS = 4
WT = WS * WS
NH = 8
WR = SIDE // WS
HW = WR // 2
HT = HW * WT
ROWS_A = NB * WR
MASKED = -1e30
EPS = 1e-5


class Chain:

    def __init__(self, eng, sem, i=0, per=0):
        self.eng, self.sem, self.base, self.n, self.per = eng, sem, i * per, 0, per

    def link(self, ins):
        self.n += 1
        ins.then_inc(self.sem, 1)
        self.eng.wait_ge(self.sem, self.base + self.n)

    def end(self):
        assert self.n == self.per, self.n


def wait(eng, sem, value):
    if not (isinstance(value, int) and value <= 0):
        eng.wait_ge(sem, value)


def phase_a(nc, io, h_cm):
    with ExitStack() as ctx:
        sb = lambda n, s, d=F32: ctx.enter_context(nc.sbuf_tensor("a_" + n, s, d))
        ps = lambda n, s, d=F32: ctx.enter_context(nc.psum_tensor("a_p_" + n, s, d))
        sem = lambda n: ctx.enter_context(nc.semaphore("a_s_" + n))
        X = sb("x", [C, NB * IMG])
        w1 = sb("w1", [C, 3, P])
        b1 = sb("b1", [P, 3])
        w2 = sb("w2", [P, 2, C])
        b2 = sb("b2", [P, 1])
        mask = sb("mask", [P, NH])
        ident = sb("ident", [P, P])
        bias = sb("bias", [P, WR, 2, WT])
        unmet = sb("unmet", [P, WR, 2, WT])
        q = sb("q", [P, HW, 2, WT])
        kv = sb("kv", [P, 2, HT])
        kexp = sb("kexp", [P, HW, NH, WT])
        vexp = sb("vexp", [P, HW, NH, WT])
        prob = sb("prob", [P, 2, NH, WT])
        stat = sb("stat", [P, 3, 2 * NH])
        vw = sb("vw", [P, 2, HW, P])
        pt = sb("pt", [P, 2 * P])
        yrow = sb("yrow", [C, WS * SIDE])
        p_proj = ps("proj", [P, 2, 512])
        p_s = ps("s", [P, 512])
        p_pty = ps("pty", [P, 512])
        p_pt = p_pty[:, 0:2 * P]
        p_y = p_pty[:, 2 * P:2 * P + HW * 2 * WT]
        p_vw = ps("vw", [P, 8 * P])

        w2_zeroed = sem("w2_zeroed")
        s_zeroed = sem("s_zeroed")
        first_in = sem("first_in")
        loaded = sem("loaded")
        bias_in = sem("bias_in")
        bias_ok = sem("bias_ok")
        txt_in = sem("txt_in")
        proj_done = sem("proj_done")
        kv_ready = sem("kv_ready")
        kexp_ready = sem("kexp_ready")
        vexp_ready = sem("vexp_ready")
        s_done = sem("s_done")
        s_read = sem("s_read")
        shifted = sem("shifted")
        exp_done = sem("exp_done")
        p_ready = sem("p_ready")
        vw_done = sem("vw_done")
        vw_ready = sem("vw_ready")
        pt_done = sem("pt_done")
        pt_ready = sem("pt_ready")
        y_done = sem("y_done")
        y_read = sem("y_read")
        y_out = sem("y_out")
        dve_own = sem("dve_own")
        dve_low = sem("dve_low")
        dve_set = sem("dve_set")

        Xv = X[:].rearrange("c (b h w) -> c b h w", b=NB, h=SIDE)
        x = io["x"]
        R = SIDE - 2
        FIRST = 4 + 5 + 2
        with nc.Block() as block:
            def picture(eng, b, sem):
                for i0, i1, s0 in ((0, R, 2), (R, SIDE, 0)):
                    for j0, j1, t0 in ((0, R, 2), (R, SIDE, 0)):
                        eng.dma_start(Xv[:, b, i0:i1, j0:j1],
                                      x[b, :, s0:s0 + i1 - i0, t0:t0 + j1 - j0]).then_inc(sem, 16)

            @block.sync
            def _(sp):
                picture(sp, 0, first_in)
                for t, k in ((w1, "tok_w1"), (b1, "tok_b1"), (b2, "tok_b2"), (mask, "head_mask"), (ident, "ident")):
                    sp.dma_start(t[:], io[k]).then_inc(first_in, 16)
                sp.wait_ge(w2_zeroed, 1)
                for half in range(2):
                    lanes = slice(half * C, half * C + C)
                    sp.dma_start(w2[lanes, half, :], io["tok_w2"][lanes, :]).then_inc(first_in, 16)
                for b in range(1, NB):
                    picture(sp, b, loaded)
                sp.dma_start(h_cm.rearrange("c (b n) -> c b n", b=NB)[:, :, IMG:N], io["txt"]).then_inc(txt_in, 16)
                with sp.Fori(0, ROWS_A) as g:
                    sp.wait_ge(y_read, g + 1)
                    sp.dma_start(h_cm[:, bass.ds(g // WR * N + g % WR * (WS * SIDE), WS * SIDE)], yrow[:]).then_inc(y_out, 16)
                sp.wait_ge(y_out, NB * WR * 16)
                sp.wait_ge(txt_in, 16)

            @block.tensor
            def _(pe):
                pe.wait_ge(first_in, 16 * FIRST)
                pe.wait_ge(s_zeroed, 1)

                def project(g):
                    wait(pe, kv_ready, g)
                    for s in range(3):
                        rows = X[:, bass.ds(g * WS * SIDE, WS * SIDE)].rearrange("c (r w s) -> c w r s", r=WS, s=WS)
                        bank, c0 = ((1, 0), (0, 0), (0, 2 * HT))[s]
                        last = pe.matmul(p_proj[:, bank, c0:c0 + 2 * HT], w1[:, s, :], rows,
                                         start=True, stop=True)
                    last.then_inc(proj_done, 1)

                def scores(g):
                    wait(pe, kexp_ready, g + 1)
                    wait(pe, s_read, g)
                    for w in range(HW):
                        r0, c0 = w % 4 * 2 * WT, w // 4 * P
                        last = pe.matmul(p_s[r0:r0 + 2 * WT, c0:c0 + P], q[:, w, :, :].rearrange("p t q -> p (t q)"),
                                         kexp[:, w, :, :].rearrange("p h k -> p (h k)"), start=True, stop=True)
                    last.then_inc(s_done, 1)

                def values(g):
                    wait(pe, vexp_ready, g + 1)
                    wait(pe, vw_ready, g)
                    for w in range(HW):
                        last = pe.matmul(p_vw[:, w * P:(w + 1) * P],
                                         vexp[:, w, :, :].rearrange("p h k -> p (h k)"),
                                         w2[:].rearrange("p t o -> p (t o)"), start=True, stop=True)
                    last.then_inc(vw_done, 1)

                def turn(g):
                    wait(pe, p_ready, g + 1)
                    wait(pe, y_read, g)
                    for group in range(2):
                        last = pe.transpose(p_pt[:, group * P:(group + 1) * P],
                                            prob[:, group, :, :].rearrange("q h k -> q (h k)"), ident[:])
                    last.then_inc(pt_done, 1)

                def result(g, buf):
                    wait(pe, pt_ready, g + 1)
                    wait(pe, vw_ready, g + 1)
                    for w in range(HW):
                        last = pe.matmul(p_y[:, w * 2 * WT:(w + 1) * 2 * WT], vw[:, buf, w, :],
                                         pt[:, w * 2 * WT:(w + 1) * 2 * WT], start=True, stop=True)
                    last.then_inc(y_done, 1)

                def step(i, buf):
                    scores(i - 1)
                    turn(i - 2)
                    values(i - 1)
                    result(i - 2, buf)

                project(0)
                project(1)
                scores(0)
                values(0)
                project(2)
                step(2, 0)
                project(3)
                step(3, 1)
                project(4)
                pe.wait_ge(loaded, 16 * 4 * (NB - 1))
                with pe.Fori(4, ROWS_A - 3, 2) as i:
                    step(i, 0)
                    project(i + 1)
                    step(i + 1, 1)
                    project(i + 2)
                step(ROWS_A - 2, 0)
                project(ROWS_A - 1)
                step(ROWS_A - 1, 1)
                step(ROWS_A, 0)
                turn(ROWS_A - 1)
                result(ROWS_A - 1, 1)

            @block.vector
            def _(dve):
                own = Chain(dve, dve_set)
                dve.memset(w2[:], 0.0).then_inc(w2_zeroed, 1)
                own.link(dve.memset(q[:], 0.0))
                dve.memset(p_s[:, P:2 * P], 0.0).then_inc(s_zeroed, 1)
                dve.wait_ge(bias_in, 16 * WT)
                own.link(dve.tensor_copy(bias[:, 0, 1, :], bias[:, 0, 0, :]))
                for r in range(1, WR):
                    last = dve.tensor_copy(bias[:, r, :, :], bias[:, 0, :, :])
                own.link(last)
                dve.wait_ge(bias_ok, 16)
                own.link(dve.tensor_tensor(bias[:], bias[:], unmet[:], ALU.add))
                dve.wait_ge(first_in, 16 * FIRST)
                flat = prob[:].rearrange("q t h k -> q (t h) k")
                wide = lambda i: stat[:, i, :].unsqueeze(2).to_broadcast([P, 2 * NH, WT])

                def inputs(g):
                    wait(dve, proj_done, g + 1)
                    wait(dve, vexp_ready, g)
                    wait(dve, s_done, g)
                    for half in range(2):
                        lanes = slice(half * C, half * C + C)
                        dve.tensor_scalar(q[lanes, :, half, :], p_proj[lanes, 1, half * HT:(half + 1) * HT].rearrange(
                            "p (w q) -> p w q", q=WT), b1[lanes, 0:1], float((C / NH) ** -0.5), ALU.add, ALU.mult)
                        last = dve.tensor_tensor(kv[lanes, :, :], p_proj[lanes, 0, 0:4 * HT].rearrange(
                            "p (s t) -> p s t", s=2)[:, :, half * HT:(half + 1) * HT],
                            b1[lanes, 1:3].unsqueeze(2).to_broadcast([C, 2, HT]), ALU.add)
                    last.then_inc(kv_ready, 1)
                    wait(dve, kv_ready, g + 1)
                    dve.tensor_tensor(kexp[:],
                                      kv[:, 0, :].rearrange("p (w k) -> p w k", k=WT).unsqueeze(2).to_broadcast([P, HW, NH, WT]),
                                      mask[:].unsqueeze(1).unsqueeze(3).to_broadcast([P, HW, NH, WT]), ALU.mult).then_inc(kexp_ready, 1)

                def shift(g):
                    own = Chain(dve, dve_low, g, 1)
                    wait(dve, s_done, g + 1)
                    wait(dve, pt_done, g)
                    dve.tensor_tensor(prob[:],
                                      p_s[:, 0:2 * P].rearrange("q (t h k) -> q t h k", t=2, h=NH),
                                      bias[:, bass.ds(g % WR, 1), :, :].rearrange("q r t k -> q (r t) k").unsqueeze(2).to_broadcast([P, 2, NH, WT]),
                                      ALU.add).then_inc(s_read, 1)
                    wait(dve, s_read, g + 1)
                    own.link(dve.tensor_reduce(stat[:, 0, :], flat, AX.X, ALU.max))
                    dve.tensor_tensor(flat, flat, wide(0), ALU.subtract).then_inc(shifted, 1)
                    own.end()

                def norm(g):
                    own = Chain(dve, dve_own, g, 2)
                    wait(dve, exp_done, g + 1)
                    own.link(dve.tensor_reduce(stat[:, 1, :], flat, AX.X, ALU.add))
                    own.link(dve.reciprocal(stat[:, 2, :], stat[:, 1, :]))
                    dve.tensor_tensor(flat, flat, wide(2), ALU.mult).then_inc(p_ready, 1)
                    own.end()

                def step(i):
                    inputs(i)
                    shift(i - 1)
                    norm(i - 1)
                    wait(dve, p_ready, i)

                inputs(0)
                step(1)
                with dve.Fori(2, ROWS_A) as i:
                    step(i)
                shift(ROWS_A - 1)
                norm(ROWS_A - 1)

            @block.gpsimd
            def _(pool):
                pool.dma_start(unmet[:], io["masks"]).then_inc(bias_ok, 16)
                pool.wait_ge(first_in, 16 * FIRST)

                def spread(g):
                    wait(pool, kv_ready, g + 1)
                    wait(pool, vw_done, g)
                    pool.tensor_tensor(vexp[:],
                                       kv[:, 1, :].rearrange("p (w k) -> p w k", k=WT).unsqueeze(2).to_broadcast([P, HW, NH, WT]),
                                       mask[:].unsqueeze(1).unsqueeze(3).to_broadcast([P, HW, NH, WT]), ALU.mult).then_inc(vexp_ready, 1)

                spread(0)
                with pool.Fori(1, ROWS_A) as g:
                    spread(g)

            @block.scalar
            def _(act):
                for p in range(WT):
                    pi, pj = divmod(p, WS)
                    act.dma_start(bias[p:P:WT, 0, 0, :].rearrange("p (a c) -> p a c", a=WS),
                                  io["pos"][:, 3 - pi:7 - pi, 3 - pj:7 - pj].to_broadcast([P // WT, WS, WS])).then_inc(bias_in, 16)
                act.wait_ge(first_in, 16 * FIRST)

                def values(g, buf):
                    wait(act, vw_done, g + 1)
                    wait(act, y_done, g - 1)
                    act.activation(vw[:, buf].rearrange("p w o -> p (w o)"), p_vw[:, 0:HW * P], ACT.Copy).then_inc(vw_ready, 1)

                def exps(g):
                    wait(act, shifted, g + 1)
                    act.activation(prob[:], prob[:], ACT.Exp).then_inc(exp_done, 1)

                def probs(g):
                    wait(act, pt_done, g + 1)
                    wait(act, y_done, g)
                    act.activation(pt[:], p_pt, ACT.Copy).then_inc(pt_ready, 1)

                def out(g):
                    wait(act, y_done, g + 1)
                    wait(act, y_out, g * 16)
                    for half in range(2):
                        last = act.activation(yrow[:].rearrange("c (r t w s) -> c t w r s", r=WS, t=2, s=WS)[:, half],
                                              p_y[half * C:half * C + C, :].rearrange("c (w t r s) -> c t w r s", t=2, r=WS, s=WS)[:, half],
                                              ACT.Identity, bias=b2[half * C:half * C + C, 0:1])
                    last.then_inc(y_read, 1)

                def step(i, buf):
                    probs(i - 2)
                    values(i - 1, 1 - buf)
                    out(i - 2)
                    exps(i - 1)

                values(0, 0)
                exps(0)
                step(2, 0)
                step(3, 1)
                with act.Fori(4, ROWS_A - 1, 2) as i:
                    step(i, 0)
                    step(i + 1, 1)
                step(ROWS_A, 0)
                probs(ROWS_A - 1)
                out(ROWS_A - 1)


NP = NT * P
G0 = 4
D0 = C // G0
QC = 3 * P
NQ = N // QC
KC = 396
NK = N // KC
KU = 1
NKU = NK // KU
RING = 3
STEPS = NT
ROWS = 6 * D0
M0 = ROWS
E0 = 6
PARTS = ((0, 0), (0, 1), (1, 0), (1, 1), (0, 2), (2, 0))


def ln_vector(dve, own, H, xh, sq, stat, s, k):
    wide = lambda i: stat[:, i, :].unsqueeze(2).to_broadcast([P, NT, C])
    own.link(dve.tensor_reduce(stat[:, 0, :], H[:], AX.X, ALU.add))
    own.link(dve.tensor_scalar(stat[:, 0, :], stat[:, 0, :], 1.0 / C, None, ALU.mult))
    own.link(dve.tensor_tensor(xh[:], H[:], wide(0), ALU.subtract))
    own.link(dve.tensor_tensor(sq[:], xh[:], xh[:], ALU.mult))
    own.link(dve.tensor_reduce(stat[:, 1, :], sq[:], AX.X, ALU.add))
    dve.tensor_scalar(stat[:, 1, :], stat[:, 1, :], 1.0 / C, EPS, ALU.mult, ALU.add).then_inc(s["var"], 1)
    dve.wait_ge(s["std"], k + 1)
    own.link(dve.reciprocal(stat[:, 3, :], stat[:, 2, :]))
    dve.tensor_tensor(xh[:], xh[:], wide(3), ALU.mult).then_inc(s["xh"], 1)


def ln_scalar(act, stat, s, k):
    act.wait_ge(s["var"], k + 1)
    act.activation(stat[:, 2, :], stat[:, 1, :], ACT.Sqrt).then_inc(s["std"], 1)


GROUPS = [(4 * g, min(4 * g + 4, NT)) for g in range((NT + 3) // 4)]


def turn_tensor(pe, xh, pb, ident, s, k):
    pe.wait_ge(s["xh"], k + 1)
    pe.sem_inc(s["passed"])
    for g, (t0, t1) in enumerate(GROUPS):
        for t in range(t0, t1):
            last = pe.transpose(pb[0:C, g, (t - t0) * P:(t - t0 + 1) * P], xh[:, t, :], ident[:])
        last.then_inc(s["turned"], 1)


def turn_scalar(act, xT, pb, s, k):
    for g, (t0, t1) in enumerate(GROUPS):
        act.wait_ge(s["turned"], k * len(GROUPS) + g + 1)
        act.activation(xT[0:C, t0 * P:t1 * P], pb[0:C, g, 0:(t1 - t0) * P], ACT.Copy).then_inc(s["xT"], 1)


def split_row(pool, s, row, parts):
    own = Chain(pool, s["own"])
    for part in range(3):
        own.link(pool.tensor_copy(parts[:, part, :], row[:]))
        if part < 2:
            own.link(pool.tensor_tensor(row[:], row[:], parts[:, part, :], ALU.subtract))


def stack_parts(sp, s, parts, dst):
    for part in range(3):
        sp.wait_ge(s["own"], 2 * part + 1)
        sp.dma_start(dst[part:part + 1, :], parts[:, part, :]).then_inc(s["in"], 16)
    sp.wait_ge(s["in"], 48)


def phase_b(nc, io, h_cm, x_cm, h_tm):
    with ExitStack() as ctx:
        sb = lambda n, s, d=F32: ctx.enter_context(nc.sbuf_tensor("b_" + n, s, d))
        sem = lambda n: ctx.enter_context(nc.semaphore("b_s_" + n))
        xT = sb("xT", [C + 1, NP])
        H = sb("H", [P, NT, C])
        xh = sb("xh", [P, NT, C])
        sq = sb("sq", [P, NT, C])
        stat = sb("stat", [P, 4, NT])
        ident = sb("ident", [P, P])
        identh = sb("identh", [P, P], BF16)
        wqk = sb("wqk", [C + 1, P])
        wv = sb("wv", [C + 1, C])
        scale = sb("scale", [P, 1])
        V = sb("V", [P, NT, G0, 32])
        Qs = sb("Qs", [P, G0, N], BF16)
        Ks = sb("Ks", [P, G0, N], BF16)
        y = sb("y", [P, N])
        parts = sb("parts", [P, 3, N], BF16)
        prob = sb("prob", [P, 2, G0, QC])
        mx = sb("mx", [P, 3 * G0, NKU])
        nm = sb("nm", [P, 2, 3 * G0])
        nsp = sb("nsp", [P, 3 * G0, 3], BF16)
        O = y
        wp = sb("wp", [P, C])
        bp = sb("bp", [P, C])
        selz = sb("selz", [P, P])
        zr = sb("zr", [P, 2, 512])
        pb = ctx.enter_context(nc.psum_tensor("b_ps", [P, 8, 512], F32))
        rw1 = sb("rw1", [C + 1, 32])
        rw2 = sb("rw2", [33, E0])
        ew1 = sb("ew1", [C + 1, 3, P])
        ew2 = sb("ew2", [P, 3, P])
        eb2 = sb("eb2", [P, 3])
        ew3 = sb("ew3", [P, 3, P])
        eb3 = sb("eb3", [1, 3 * P])
        eb3p = sb("eb3p", [1, 3, 3 * P], BF16)
        eb33 = sb("eb33", [3, 3 * P], BF16)
        ones3 = sb("ones3", [3, P], BF16)
        iota = sb("iota", [P, NT, E0])
        rh = sb("rh", [33, NP])
        rt = sb("rt", [P, 8, NT, E0])
        rs = sb("rs", [P, 4, NT])
        W = sb("W", [P, NT, E0])
        h1 = sb("h1", [P, 3, QC])
        h2 = sb("h2", [P, 2, 3, QC])
        yw = sb("yw", [P, 2, E0, C])
        ya = sb("ya", [P, C])

        loaded = sem("loaded")
        pool_own = sem("pool_own")
        b_split = {n: sem("b_" + n) for n in ("own", "in")}
        dve_own = [sem(f"dve_own{i}") for i in range(5)]
        h_in = sem("h_in")
        S = {n: sem(n) for n in ("var", "std", "xh", "turned", "xT")}
        S["passed"] = sem("passed")
        S["sp_passed"] = sem("sp_passed")
        S["spread0"], S["spread2"] = sem("spread0"), sem("spread2")
        h_turned = sem("h_turned")
        h_read = sem("h_read")
        v_done = sem("v_done")
        v_read = sem("v_read")
        qk_done = sem("qk_done")
        y_ready = sem("y_ready")
        part_ready = sem("part_ready")
        stacked = sem("stacked")
        pool_stacked = sem("pool_stacked")
        mu_full = sem("mu_full")
        mu_free = sem("mu_free")
        n_ready = sem("n_ready")
        rows_full = sem("rows_full")
        rows_ready = sem("rows_ready")
        s_full = sem("s_full")
        p_full = sem("p_full")
        pv_done = sem("pv_done")
        o_read = sem("o_read")
        z_done = sem("z_done")
        zr_ready = sem("zr_ready")
        o_ready = sem("o_ready")
        pr_done = sem("pr_done")
        rh_done = sem("rh_done")
        rh_ready = sem("rh_ready")
        lg_done = sem("lg_done")
        lg_ready = sem("lg_ready")
        lg_exp = sem("lg_exp")
        two_ready = sem("two_ready")
        two_exp = sem("two_exp")
        h1_done = sem("h1_done")
        h1_ready = sem("h1_ready")
        h2_done = sem("h2_done")
        h2_ready = sem("h2_ready")
        ye_done = sem("ye_done")
        ye_read = sem("ye_read")
        stored = sem("stored")
        h_new = sem("h_new")

        with nc.Block() as block:
            @block.sync
            def _(sp):
                loads = ((ident, "ident"), (wqk, "wqk"), (wv, "wv"), (scale, "scale"), (wp, "wp"), (bp, "bp"),
                         (selz, "selz"), (rw1, "rw1"), (rw2, "rw2"), (ew1, "ew1"), (ew2, "ew2"), (eb2, "eb2"),
                         (ew3, "ew3"), (eb3, "eb3"), (iota, "iota"))
                for t, k in loads:
                    sp.dma_start(t[:], io[k]).then_inc(loaded, 16)
                sp.wait_ge(loaded, 16 * len(loads))
                stack_parts(sp, b_split, eb3p, eb33)

            @block.vector
            def _(dve):
                dve.memset(xT[0:C, N:NP], 0.0)
                dve.memset(xT[C:C + 1, :], 1.0)
                dve.memset(H[:], 0.0)
                dve.memset(ones3[:], 1.0)
                dve.memset(rh[32:33, :], 1.0)

            @block.tensor
            def _(pe):
                pe.sem_inc(pv_done)

            @block.scalar
            def _(act):
                act.sem_inc(o_read)

            @block.gpsimd
            def _(pool):
                own = Chain(pool, pool_own)
                own.link(pool.memset(V[:], 0.0))
                own.link(pool.memset(V[:, :, :, D0:D0 + 1], 1.0))
                own.link(pool.memset(Ks[96:128, :, :], 1.0))
                pool.wait_ge(loaded, 16 * 15)
                split_row(pool, b_split, eb3, eb3p)
        with nc.Block() as block:
            @block.vector
            def _(dve):
                dve.tensor_copy(identh[:], ident[:])

        with nc.Fori(0, NB) as b:
            def spread(eng, stacked, heads):
                for part in range(3):
                    eng.wait_ge(part_ready, b * 3 + part + 1)
                    eng.sem_inc(S[f"spread{heads[0]}"])
                    for r, (pq, pk) in enumerate(PARTS):
                        for h in heads:
                            rows = slice(r * D0, (r + 1) * D0)
                            if pq == part:
                                eng.dma_start(Qs[rows, h, :], parts[h * D0:(h + 1) * D0, part, :]).then_inc(stacked, 16)
                            if pk == part:
                                eng.dma_start(Ks[rows, h, :], parts[C + h * D0:C + (h + 1) * D0, part, :]).then_inc(stacked, 16)

            with nc.Block() as block:
                @block.sync
                def _(sp):
                    sp.dma_start(xT[0:C, 0:N], h_cm[:, bass.ds(b * N, N)]).then_inc(h_in, 16)
                    spread(sp, stacked, (0, 1))
                    sp.wait_ge(stacked, (b + 1) * 16 * G0 * len(PARTS))
                    sp.sem_inc(S["sp_passed"])

                @block.tensor
                def _(pe):
                    pe.wait_ge(h_in, (b + 1) * 16)
                    pe.sem_inc(S["passed"])
                    for t in range(NT):
                        w = P if t < NT - 1 else LAST
                        last = pe.transpose(pb[0:w, t // 8, t % 8 * C:(t % 8 + 1) * C], xT[0:C, t * P:t * P + w], ident[0:C, 0:C])
                    last.then_inc(h_turned, 1)
                    pe.wait_ge(h_read, b + 1)
                    turn_tensor(pe, xh, pb, ident, S, b * 3)
                    pe.wait_ge(S["xT"], (b * 3 + 1) * len(GROUPS))
                    for t in range(NT):
                        last = pe.matmul(pb[:, t // 8, t % 8 * C:(t % 8 + 1) * C], xT[:, t * P:(t + 1) * P], wv[:], start=True, stop=True)
                    last.then_inc(v_done, 1)
                    for c in range(NK):
                        bank = (c + 4) % 8
                        if c == 4:
                            pe.wait_ge(v_read, b + 1)
                        last = pe.matmul(pb[:, bank, 0:KC], wqk[:], xT[:, c * KC:(c + 1) * KC], start=True, stop=True)
                        if c % 4 == 3:
                            last.then_inc(qk_done, 1)

                @block.vector
                def _(dve):
                    own = Chain(dve, dve_own[0], b, 8)
                    dve.wait_ge(h_turned, b + 1)
                    for t0 in (0, 8, 16):
                        dve.tensor_copy(H[:, t0:t0 + 8, :], pb[:, t0 // 8, :].rearrange("p (t c) -> p t c", t=8))
                    dve.tensor_copy(H[0:LAST, NT - 1, :], pb[0:LAST, 3, 0:C]).then_inc(h_read, 1)
                    dve.wait_ge(h_read, b + 1)
                    ln_vector(dve, own, H, xh, sq, stat, S, b * 3)
                    dve.wait_ge(v_done, b + 1)
                    for g in range(4):
                        t0, t1 = 8 * g, min(8 * g + 8, NT)
                        last = dve.tensor_copy(V[:, t0:t1, :, 0:D0], pb[:, g, 0:(t1 - t0) * C].rearrange("p (t h e) -> p t h e", h=G0, e=D0))
                    last.then_inc(v_read, 1)
                    dve.wait_ge(y_ready, (b + 1) * 2)
                    dve.wait_ge(part_ready, b * 3 + 1)
                    own.link(dve.tensor_tensor(y[:], y[:], parts[:, 0, :], ALU.subtract))
                    dve.tensor_copy(parts[:, 1, :], y[:]).then_inc(part_ready, 1)
                    dve.wait_ge(part_ready, b * 3 + 2)
                    own.link(dve.tensor_tensor(y[:], y[:], parts[:, 1, :], ALU.subtract))
                    dve.tensor_copy(parts[:, 2, :], y[:]).then_inc(part_ready, 1)
                    own.end()

                @block.scalar
                def _(act):
                    ln_scalar(act, stat, S, b * 3)
                    turn_scalar(act, xT, pb, S, b * 3)
                    for g in range(2):
                        act.wait_ge(qk_done, b * 2 + g + 1)
                        src = pb[:, 4:8, 0:KC] if g == 0 else pb[:, 0:4, 0:KC]
                        cols = slice(g * 4 * KC, (g + 1) * 4 * KC)
                        act.activation(y[:, cols].rearrange("p (a n) -> p a n", a=4), src, ACT.Copy, scale=scale[:, 0:1]).then_inc(y_ready, 1)
                        last = act.activation(parts[:, 0, cols].rearrange("p (a n) -> p a n", a=4), src, ACT.Copy, scale=scale[:, 0:1])
                    last.then_inc(part_ready, 1)

                @block.gpsimd
                def _(pool):
                    spread(pool, pool_stacked, (2, 3))
                    pool.wait_ge(pool_stacked, (b + 1) * 16 * G0 * len(PARTS))
                    pool.sem_inc(S["spread2"])

            NU = 3 * G0 * NKU
            UNITS = NQ * NU + G0 * NKU
            nchunk = NQ + 1
            flat = pb[:].rearrange("p a n -> p (a n)")
            top = flat[:, 5 * 512:8 * 512]

            with nc.Block() as block:
                @block.tensor
                def _(pe):
                    u0 = b * UNITS

                    def unit(c, j, static=None):
                        w = P if static is None or static < NQ else LAST
                        t, h, k = j // (G0 * NKU), j // NKU % G0, j % NKU
                        if static != 0 or j >= RING:
                            pe.wait_ge(mu_free, u0 + c * NU + (j - RING + 1))
                        if static != 0 and j < RING:
                            pe.wait_ge(rows_ready, b * nchunk + c)
                        q = Qs[0:ROWS, h, bass.ds(c * QC + t * P, w)] if static is None else Qs[0:ROWS, h, c * QC + t * P:c * QC + t * P + w]
                        for half in range(KU):
                            c0 = (k * KU + half) * KC
                            last = pe.matmul(pb[0:w, 5 + j % RING * KU + half, 0:KC], q, Ks[0:ROWS, h, c0:c0 + KC],
                                             start=True, stop=True)
                        last.then_inc(mu_full, 1)

                    def rows(c, tiles, w):
                        pe.wait_ge(n_ready, b * nchunk + c + 1)
                        for h in range(G0):
                            for t in range(tiles):
                                col = h * tiles * w + t * w
                                last = pe.matmul(top[M0:M0 + 3, col:col + w],
                                                 nsp[0:w, t * G0 + h, :], identh[0:w, 0:w], start=True, stop=True)
                        last.then_inc(rows_full, 1)

                    def scores(c, s, pair, w, whole):
                        m = P if s < NT - 1 else LAST
                        g = b * nchunk * STEPS + c * STEPS + s
                        if s:
                            pe.wait_ge(p_full, g * 2 + pair - 1)
                        for h in (2 * pair, 2 * pair + 1):
                            c0 = c * QC
                            q = Qs[0:M0 + 3, h, bass.ds(c0, w)] if whole is None else Qs[0:M0 + 3, h, c0:c0 + w]
                            last = pe.matmul(pb[0:m, h, 0:w], Ks[0:M0 + 3, h, s * P:s * P + m], q, start=True, stop=True)
                        last.then_inc(s_full, 1)

                    def product(c, s, w):
                        m = P if s < NT - 1 else LAST
                        g = b * nchunk * STEPS + c * STEPS + s
                        pe.wait_ge(p_full, 2 * g + 2)
                        if s == 0:
                            pe.wait_ge(o_read, b * nchunk + c + 1)
                        for h in range(G0):
                            last = pe.matmul(pb[32 * h:32 * h + 32, 4, 0:w], V[0:m, s, h, :], prob[0:m, s % 2, h, 0:w],
                                             start=(s == 0), stop=(s == NT - 1), tile_position=(0, 32 * h))
                        last.then_inc(pv_done, 1)

                    def both(c, w, static, ahead, n):
                        per = -(-n // (STEPS - 1))
                        pe.wait_ge(rows_ready, b * nchunk + c + 1)
                        for s in range(STEPS):
                            units = iter(range(s * per, min((s + 1) * per, n)))
                            scores(c, s, 0, w, static)
                            for j in units:
                                unit(c + 1, j, ahead)
                                break
                            scores(c, s, 1, w, static)
                            for j in units:
                                unit(c + 1, j, ahead)
                                break
                            if s:
                                product(c, s - 1, w)
                            for j in units:
                                unit(c + 1, j, ahead)
                        product(c, STEPS - 1, w)

                    for j in range(NU):
                        unit(0, j, 0)
                    rows(0, 3, P)
                    with pe.Fori(0, NQ - 1) as c:
                        both(c, QC, None, None, NU)
                        rows(c + 1, 3, P)
                    both(NQ - 1, QC, NQ - 1, NQ, G0 * NKU)
                    rows(NQ, 1, LAST)
                    both(NQ, LAST, NQ, None, 0)

                @block.vector
                def _(dve):
                    def maxima(c, tiles, w):
                        for j in range(tiles * G0 * NKU):
                            r = 5 + j % RING * KU
                            dve.wait_ge(mu_full, b * UNITS + c * NU + j + 1)
                            dve.tensor_reduce(mx[0:w, j // NKU, j % NKU:j % NKU + 1], pb[0:w, r:r + KU, 0:KC],
                                              AX.XY, ALU.max, negate=True).then_inc(mu_free, 1)
                        n = tiles * G0
                        dve.wait_ge(mu_free, b * UNITS + c * NU + tiles * G0 * NKU)
                        own = Chain(dve, dve_own[1], b * nchunk + c, 5)
                        own.link(dve.tensor_reduce(nm[0:w, 0, 0:n], mx[0:w, 0:n, :], AX.X, ALU.min))
                        own.link(dve.tensor_copy(nsp[0:w, 0:n, 0], nm[0:w, 0, 0:n]))
                        own.link(dve.tensor_tensor(nm[0:w, 1, 0:n], nm[0:w, 0, 0:n], nsp[0:w, 0:n, 0], ALU.subtract))
                        own.link(dve.tensor_copy(nsp[0:w, 0:n, 1], nm[0:w, 1, 0:n]))
                        own.link(dve.tensor_tensor(nm[0:w, 0, 0:n], nm[0:w, 1, 0:n], nsp[0:w, 0:n, 1], ALU.subtract))
                        dve.tensor_copy(nsp[0:w, 0:n, 2], nm[0:w, 0, 0:n]).then_inc(n_ready, 1)
                        own.end()
                        dve.wait_ge(rows_full, b * nchunk + c + 1)
                        cols = tiles * w
                        dve.tensor_copy(Qs[M0:M0 + 3, :, bass.ds(c * QC, cols)],
                                        top[M0:M0 + 3, 0:G0 * cols].rearrange("p (h n) -> p h n", h=G0)).then_inc(rows_ready, 1)

                    with dve.Fori(0, NQ) as c:
                        maxima(c, 3, P)
                    maxima(NQ, 1, LAST)

                @block.scalar
                def _(act):
                    def exps(c, w):
                        for s in range(STEPS):
                            m = P if s < NT - 1 else LAST
                            g = b * nchunk * STEPS + c * STEPS + s
                            if s == 0:
                                act.wait_ge(pv_done, g + 1)
                            elif s > 1:
                                act.wait_ge(pv_done, g)
                            for pair in range(2):
                                act.wait_ge(s_full, g * 2 + pair + 1)
                                act.activation(prob[0:m, s % 2, 2 * pair:2 * pair + 2, 0:w],
                                               pb[0:m, 2 * pair:2 * pair + 2, 0:w],
                                               ACT.Exp).then_inc(p_full, 1)
                        act.wait_ge(pv_done, b * nchunk * STEPS + c * STEPS + STEPS + 1)
                        act.activation(O[:, bass.ds(c * QC, w)], pb[:, 4, 0:w], ACT.Copy).then_inc(o_read, 1)

                    with act.Fori(0, NQ) as c:
                        exps(c, QC)
                    exps(NQ, LAST)

            with nc.Block() as block:
                @block.tensor
                def _(pe):
                    for c in range(NK):
                        cols = slice(c * KC, (c + 1) * KC)
                        if c >= 2:
                            pe.wait_ge(zr_ready, b * NK + c - 1)
                        pe.matmul(pb[:, c % 2, 0:KC], selz[:], O[:, cols], start=True, stop=True).then_inc(z_done, 1)
                    pe.wait_ge(o_ready, (b + 1) * NK)
                    for t in range(NT):
                        w = P if t < NT - 1 else LAST
                        dst = pb[0:w, 2 + t // 8, t % 8 * C:(t % 8 + 1) * C]
                        last = pe.matmul(dst, O[:, t * P:t * P + w], wp[:], start=True, stop=True)
                    last.then_inc(pr_done, 1)
                    turn_tensor(pe, xh, pb, ident, S, b * 3 + 1)

                @block.vector
                def _(dve):
                    own = Chain(dve, dve_own[2], b, 8)
                    own.link(dve.tensor_tensor(H[:], H[:], bp[:].unsqueeze(1).to_broadcast([P, NT, C]), ALU.add))
                    for c in range(NK):
                        cols = slice(c * KC, (c + 1) * KC)
                        dve.wait_ge(z_done, b * NK + c + 1)
                        if c >= 2:
                            dve.wait_ge(o_ready, b * NK + c - 1)
                        dve.reciprocal(zr[:, c % 2, 0:KC], pb[:, c % 2, 0:KC]).then_inc(zr_ready, 1)
                        dve.wait_ge(zr_ready, b * NK + c + 1)
                        dve.tensor_tensor(O[:, cols], O[:, cols], zr[:, c % 2, 0:KC], ALU.mult).then_inc(o_ready, 1)
                    dve.wait_ge(pr_done, b + 1)
                    for g in range(3):
                        dve.tensor_tensor(H[:, 8 * g:8 * g + 8, :], H[:, 8 * g:8 * g + 8, :],
                                          pb[:, 2 + g, :].rearrange("p (t c) -> p t c", t=8), ALU.add)
                    own.link(dve.tensor_tensor(H[0:LAST, NT - 1, :], H[0:LAST, NT - 1, :], pb[0:LAST, 5, 0:C], ALU.add))
                    ln_vector(dve, own, H, xh, sq, stat, S, b * 3 + 1)
                    own.end()

                @block.scalar
                def _(act):
                    ln_scalar(act, stat, S, b * 3 + 1)
                    turn_scalar(act, xT, pb, S, b * 3 + 1)

            CHUNKS = [(c * QC, QC) for c in range(NQ)] + [(NQ * QC, P)]
            with nc.Block() as block:
                @block.tensor
                def _(pe):
                    for c, (c0, w) in enumerate(CHUNKS):
                        if c >= 4:
                            pe.wait_ge(rh_ready, b * len(CHUNKS) + c - 3)
                        pe.matmul(pb[0:32, c % 4, 0:w], rw1[:], xT[:, c0:c0 + w], start=True, stop=True).then_inc(rh_done, 1)
                    pe.wait_ge(rh_ready, (b + 1) * len(CHUNKS))
                    for t in range(NT):
                        last = pe.matmul(pb[:, 4, t * E0:(t + 1) * E0], rh[:, t * P:(t + 1) * P], rw2[:], start=True, stop=True)
                    last.then_inc(lg_done, 1)

                @block.scalar
                def _(act):
                    for c, (c0, w) in enumerate(CHUNKS):
                        act.wait_ge(rh_done, b * len(CHUNKS) + c + 1)
                        act.activation(rh[0:32, c0:c0 + w], pb[0:32, c % 4, 0:w], ACT.Relu).then_inc(rh_ready, 1)
                    act.wait_ge(lg_ready, b + 1)
                    act.activation(rt[:, 0], rt[:, 0], ACT.Exp).then_inc(lg_exp, 1)
                    act.wait_ge(two_ready, b + 1)
                    act.activation(rs[:, 3], rs[:, 2], ACT.Exp).then_inc(two_exp, 1)

                @block.vector
                def _(dve):
                    own = Chain(dve, dve_own[3], b, 23)
                    wide = lambda a: a.unsqueeze(2).to_broadcast([P, NT, E0])
                    tt = lambda o, a, c, op: own.link(dve.tensor_tensor(o, a, c, op))
                    dve.wait_ge(lg_done, b + 1)
                    lg = pb[:, 4, 0:NT * E0].rearrange("p (t e) -> p t e", e=E0)
                    own.link(dve.tensor_reduce(rs[:, 0], lg, AX.X, ALU.max))
                    dve.tensor_tensor(rt[:, 0], lg, wide(rs[:, 0]), ALU.subtract).then_inc(lg_ready, 1)
                    dve.wait_ge(lg_exp, b + 1)
                    own.link(dve.tensor_reduce(rs[:, 0], rt[:, 0], AX.X, ALU.add))
                    own.link(dve.reciprocal(rs[:, 1], rs[:, 0]))
                    tt(rt[:, 0], rt[:, 0], wide(rs[:, 1]), ALU.mult)
                    for k in range(2):
                        own.link(dve.tensor_reduce(rs[:, k], rt[:, 0], AX.X, ALU.max))
                        tt(rt[:, 1], rt[:, 0], wide(rs[:, k]), ALU.is_equal)
                        own.link(dve.tensor_scalar(rt[:, 2], iota[:], float(E0), None, ALU.subtract))
                        tt(rt[:, 3], rt[:, 1], rt[:, 2], ALU.mult)
                        own.link(dve.tensor_reduce(rs[:, 2], rt[:, 3], AX.X, ALU.min))
                        tt(rt[:, 4 + k], rt[:, 2], wide(rs[:, 2]), ALU.is_equal)
                        if k == 0:
                            own.link(dve.tensor_scalar(rt[:, 6], rt[:, 4], 2.0, None, ALU.mult))
                            tt(rt[:, 0], rt[:, 0], rt[:, 6], ALU.subtract)
                    dve.tensor_tensor(rs[:, 2], rs[:, 1], rs[:, 0], ALU.subtract).then_inc(two_ready, 1)
                    dve.wait_ge(two_exp, b + 1)
                    own.link(dve.tensor_scalar(rs[:, 0], rs[:, 3], 1.0, None, ALU.add))
                    own.link(dve.reciprocal(rs[:, 1], rs[:, 0]))
                    tt(rs[:, 2], rs[:, 1], rs[:, 3], ALU.mult)
                    tt(rt[:, 4], rt[:, 4], wide(rs[:, 1]), ALU.mult)
                    tt(rt[:, 5], rt[:, 5], wide(rs[:, 2]), ALU.mult)
                    dve.tensor_tensor(W[:], rt[:, 4], rt[:, 5], ALU.add)
                    own.end()

            NC_ = len(CHUNKS)
            with nc.Block() as block:
                @block.tensor
                def _(pe):
                    def ups(c):
                        c0, w = CHUNKS[c]
                        for k in range(3):
                            n = b * NC_ * 3 + c * 3 + k
                            if c or k >= 2:
                                pe.wait_ge(h1_ready, n - 1)
                            pe.matmul(pb[:, (c * 3 + k) % 2, 0:w], ew1[:, k, :], xT[:, c0:c0 + w], start=True, stop=True).then_inc(h1_done, 1)

                    def mids(c):
                        c0, w = CHUNKS[c]
                        for k in range(3):
                            n = b * NC_ * 3 + c * 3 + k
                            pe.wait_ge(h1_ready, n + 1)
                            if c or k >= 2:
                                pe.wait_ge(h2_ready, n - 1)
                            pe.matmul(pb[:, 2 + (c * 3 + k) % 2, 0:w], ew2[:, k, :], h1[:, k, 0:w], start=True, stop=True).then_inc(h2_done, 1)

                    def downs(c):
                        c0, w = CHUNKS[c]
                        pe.wait_ge(h2_ready, b * NC_ * 3 + c * 3 + 3)
                        for t in range(w // P):
                            n = c * 3 + t
                            if n >= 2:
                                pe.wait_ge(ye_read, b * NT + n - 1)
                            dst = pb[:, 4 + n % 2, 0:3 * P]
                            pe.matmul(dst, ones3[:], eb33[:], start=True, stop=False)
                            for k in range(3):
                                last = pe.matmul(dst[:, k * P:(k + 1) * P], h2[:, c % 2, k, t * P:(t + 1) * P], ew3[:, k, :],
                                                 start=False, stop=(k == 2))
                            last.then_inc(ye_done, 1)

                    for c in range(NC_):
                        ups(c)
                        mids(c)
                        if c:
                            downs(c - 1)
                    downs(NC_ - 1)

                @block.scalar
                def _(act):
                    for c, (c0, w) in enumerate(CHUNKS):
                        for k in range(3):
                            n = b * NC_ * 3 + c * 3 + k
                            act.wait_ge(h1_done, n + 1)
                            if c:
                                act.wait_ge(h2_done, n - 2)
                            act.activation(h1[:, k, 0:w], pb[:, (c * 3 + k) % 2, 0:w], ACT.Relu).then_inc(h1_ready, 1)
                        for k in range(3):
                            n = b * NC_ * 3 + c * 3 + k
                            act.wait_ge(h2_done, n + 1)
                            if c >= 2:
                                act.wait_ge(ye_done, b * NT + (c - 1) * 3)
                            act.activation(h2[:, c % 2, k, 0:w], pb[:, 2 + (c * 3 + k) % 2, 0:w], ACT.Relu, bias=eb2[:, k:k + 1]).then_inc(h2_ready, 1)
                    ln_scalar(act, stat, S, b * 3 + 2)

                @block.vector
                def _(dve):
                    own = Chain(dve, dve_own[4], b, 2 * NT + 6)
                    for t in range(NT):
                        dve.wait_ge(ye_done, b * NT + t + 1)
                        dve.tensor_tensor(yw[:, t % 2], pb[:, 4 + t % 2, 0:3 * P].rearrange("p (e c) -> p e c", e=E0),
                                          W[:, t, :].unsqueeze(2).to_broadcast([P, E0, C]), ALU.mult).then_inc(ye_read, 1)
                        dve.wait_ge(ye_read, b * NT + t + 1)
                        own.link(dve.tensor_reduce(ya[:], yw[:, t % 2].rearrange("p e c -> p c e"), AX.X, ALU.add))
                        own.link(dve.tensor_tensor(H[:, t, :], H[:, t, :], ya[:], ALU.add))
                    ln_vector(dve, own, H, xh, sq, stat, S, b * 3 + 2)
                    own.end()

            with nc.Block() as block:
                @block.tensor
                def _(pe):
                    turn_tensor(pe, xh, pb, ident, S, b * 3 + 2)

                @block.sync
                def _(sp):
                    sp.dma_start(h_tm[bass.ds(b * N, (NT - 1) * P), :].rearrange("(t p) c -> p t c", p=P), H[:, 0:NT - 1, :]).then_inc(stored, 16)
                    sp.dma_start(h_tm[bass.ds(b * N + (NT - 1) * P, LAST), :], H[0:LAST, NT - 1, :]).then_inc(stored, 16)
                    sp.wait_ge(S["xT"], (b * 3 + 3) * len(GROUPS))
                    sp.sem_inc(S["sp_passed"])
                    sp.dma_start(x_cm[:, bass.ds(b * N, N)], xT[0:C, 0:N]).then_inc(stored, 16)
                    sp.wait_ge(stored, (b + 1) * 48)
                    sp.sem_inc(S["sp_passed"])

                @block.scalar
                def _(act):
                    turn_scalar(act, xT, pb, S, b * 3 + 2)


H1 = 8
NI = N // 3
PI = NI // 8
UC = 2 * KC
UT = N // UC
UH = NT * UT
RC = 3


def phase_c(nc, io, x_cm, nmx_all, es_all, diag_all):
    with ExitStack() as ctx:
        sb = lambda n, s, d=F32: ctx.enter_context(nc.sbuf_tensor("c_" + n, s, d))
        sem = lambda n: ctx.enter_context(nc.semaphore("c_s_" + n))
        xqk = sb("xqk", [C + 1, 2, 2, NI])
        wh = sb("wh", [C + 1, 2, 3, C])
        scale = sb("scale", [P, 1])
        ones = sb("ones", [C, 1])
        y = sb("y", [P, N])
        kd = sb("kd", [C, N])
        prod = sb("prod", [C, N])
        stack = sb("stack", [P, 2, 3, N], F32R)
        nmx = sb("nmx", [P, 2, NT, UT])
        es = sb("es", [P, 2, NT, UT])
        diag = sb("diag", [P, 2, NT])
        pb = ctx.enter_context(nc.psum_tensor("c_ps", [P, 8, 512], F32))
        set_up = sem("set_up")
        x_in = sem("x_in")
        w_in = sem("w_in")
        pj_full = sem("pj_full")
        y_ready = sem("y_ready")
        part_ready = sem("part_ready")
        sub_done = sem("sub_done")
        kd_in = sem("kd_in")
        prod_ready = sem("prod_ready")
        k_stacked = sem("k_stacked")
        stacked = sem("stacked")
        dg_full = sem("dg_full")
        dg_read = sem("dg_read")
        s_full = sem("s_full")
        max_done = sem("max_done")
        exp_done = sem("exp_done")
        results = sem("results")
        passed = {e: sem("passed_" + e) for e in ("sp", "pe", "dve", "act", "pool")}
        HEADS = NB * H1
        place = lambda buf, j: (j + buf) % RC * 2
        DG = 2
        T0 = 7

        def bodies(eng, front, main):
            front(0, 0)
            main(0, 0, lambda part: front(1, 1, part))
            main(1, 1, lambda part: front(2, 0, part))
            with eng.Fori(2, HEADS - 2, 2) as G:
                main(G, 0, lambda part: front(G + 1, 1, part))
                main(G + 1, 1, lambda part: front(G + 2, 0, part))
            main(HEADS - 2, 0, lambda part: front(HEADS - 1, 1, part))
            main(HEADS - 1, 1, None)

        with nc.Block() as block:
            @block.sync
            def _(sp):
                sp.dma_start(scale[:], io["scale1"]).then_inc(set_up, 16)
                sp.wait_ge(set_up, 16)

            @block.vector
            def _(dve):
                dve.memset(xqk[C:C + 1, :, :, :], 1.0)
                dve.memset(ones[:], 1.0)
                dve.memset(nmx[:], 0.0)
                dve.memset(es[:], 1.0)
                dve.memset(diag[:], 0.0)

        with nc.Block() as block:
            @block.sync
            def _(sp):
                def front(G, buf, part=None):
                    if part in (None, 0):
                        if not (isinstance(G, int) and G < 2):
                            sp.wait_ge(y_ready, (G - 1) * 8)
                        for s in range(2):
                            sp.dma_start(xqk[0:C, buf, s, :], x_cm[:, bass.ds((G // H1) * NI + s * NB * NI, NI)]).then_inc(x_in, 16)
                        sp.dma_start(wh[:, buf, :, :], io["w_qk"][bass.ds(G % H1, 1)].rearrange("o c j d -> (o c) j d")).then_inc(w_in, 16)
                    if part in (None, 1):
                        sp.wait_ge(prod_ready, G)
                        sp.wait_ge(y_ready, (G + 1) * 8)
                        sp.dma_start(kd[:], y[C:P, :]).then_inc(kd_in, 16)
                        sp.wait_ge(sub_done, G + 1)
                        for p in range(2):
                            sp.dma_start(stack[p * C:(p + 1) * C, buf, 2, :].bitcast(F32), stack[C:P, buf, p, :].bitcast(F32)).then_inc(k_stacked, 16)
                        sp.wait_ge(k_stacked, (G + 1) * 32)
                        for p in range(2):
                            sp.dma_start(stack[C:P, buf, p, :].bitcast(F32), stack[0:C, buf, p, :].bitcast(F32)).then_inc(stacked, 16)

                def main(G, buf, nxt):
                    if nxt:
                        nxt(0)
                        nxt(1)
                    sp.wait_ge(exp_done, (G + 1) * UH)
                    sp.wait_ge(dg_read, G + 1)
                    for src, dst in ((nmx[:, buf].rearrange("p t u -> p (t u)"), nmx_all), (es[:, buf].rearrange("p t u -> p (t u)"), es_all),
                                     (diag[:, buf], diag_all)):
                        sp.dma_start(dst[:, bass.ds(G, 1), :].rearrange("p g n -> p (g n)"), src).then_inc(results, 16)

                bodies(sp, front, main)
                sp.wait_ge(results, HEADS * 48)

            @block.tensor
            def _(pe):
                pe.wait_ge(set_up, 16)

                def chunk(G, buf, c, j):
                    if j == 0:
                        if c == 0:
                            pe.wait_ge(x_in, (G + 1) * 32)
                            pe.wait_ge(w_in, (G + 1) * 16)
                        pe.wait_ge(y_ready, G * 8 + c)
                    for s in range(2):
                        last = pe.matmul(pb[s * C:(s + 1) * C, 6, j * PI:(j + 1) * PI], wh[:, buf, j, :],
                                         xqk[:, buf, s, c * PI:(c + 1) * PI], start=True, stop=True)
                    if j == 2:
                        last.then_inc(pj_full, 1)

                def front(G, buf, part=None):
                    if part is None:
                        for i in range(24):
                            chunk(G, buf, i // 3, i % 3)
                    else:
                        chunk(G, buf, *part)

                def diagonal(G, t):
                    if t == 0:
                        pe.wait_ge(prod_ready, G + 1)
                        if not (isinstance(G, int) and G == 0):
                            pe.wait_ge(dg_read, G)
                    w = P if t < NT - 1 else LAST
                    last = pe.matmul(pb[0:w, 7, t:t + 1], prod[:, t * P:t * P + w], ones[:], start=True, stop=True)
                    if t == NT - 1:
                        last.then_inc(dg_full, 1)

                def main(G, buf, nxt):
                    base = G * UH
                    pe.wait_ge(stacked, (G + 1) * 32)
                    for t in range(NT):
                        w = P if t < NT - 1 else LAST
                        for u in range(UT):
                            j = t * UT + u
                            r = place(buf, j)
                            if j < RC:
                                before = max(i for i in range(UH) if place(1 - buf, i) == r)
                                if not (isinstance(G, int) and G == 0):
                                    pe.wait_ge(exp_done, base - UH + before + 1)
                            else:
                                pe.wait_ge(exp_done, base + j - RC + 1)
                            for q in range(2):
                                for half in range(2):
                                    c0 = u * UC + half * KC
                                    last = pe.matmul(pb[0:w, r + half, 0:KC], stack[:, buf, 2, t * P:t * P + w],
                                                     stack[:, buf, q, c0:c0 + KC], start=(q == 0), stop=(q == 1))
                            last.then_inc(s_full, 1)
                            if DG <= j < DG + NT:
                                diagonal(G, j - DG)
                            if nxt and T0 <= t < T0 + 8 and u < 3:
                                nxt((t - T0, u))

                bodies(pe, front, main)

            @block.vector
            def _(dve):
                def front(G, buf, part=None):
                    dve.wait_ge(y_ready, (G + 1) * 8)
                    if not (isinstance(G, int) and G < 2):
                        dve.wait_ge(s_full, (G - 1) * UH)
                    dve.tensor_copy(stack[:, buf, 0, :], y[:]).then_inc(part_ready, 1)

                def main(G, buf, nxt):
                    if not (isinstance(G, int) and G < 2):
                        dve.wait_ge(results, (G - 1) * 48)
                    for t in range(NT):
                        w = P if t < NT - 1 else LAST
                        for u in range(UT):
                            j = t * UT + u
                            dve.wait_ge(s_full, G * UH + j + 1)
                            r = place(buf, j)
                            dve.tensor_reduce(nmx[0:w, buf, t, u:u + 1], pb[0:w, r:r + 2, 0:KC],
                                              AX.XY, ALU.max, negate=True).then_inc(max_done, 1)
                        if t == (DG + NT) // UT + 1:
                            dve.wait_ge(dg_full, G + 1)
                            dve.tensor_copy(diag[:, buf, 0:NT - 1], pb[:, 7, 0:NT - 1])
                            dve.tensor_copy(diag[0:LAST, buf, NT - 1:NT], pb[0:LAST, 7, NT - 1:NT]).then_inc(dg_read, 1)
                        if nxt and t == T0 + 9:
                            nxt(None)

                bodies(dve, front, main)

            @block.gpsimd
            def _(pool):
                def front(G, buf, part=None):
                    pool.wait_ge(part_ready, G + 1)
                    pool.tensor_tensor(stack[:, buf, 1, :], y[:], stack[:, buf, 0, :].bitcast(F32), ALU.subtract).then_inc(sub_done, 1)
                    pool.wait_ge(kd_in, (G + 1) * 16)
                    pool.wait_ge(dg_full, G)
                    pool.tensor_tensor(prod[:], y[0:C, :], kd[:], ALU.mult).then_inc(prod_ready, 1)

                def main(G, buf, nxt):
                    if nxt:
                        nxt(0)

                bodies(pool, front, main)

            @block.scalar
            def _(act):
                def front(G, buf, part=None):
                    for c in (range(8) if part is None else (part,)):
                        if c == 0:
                            act.wait_ge(prod_ready, G)
                            act.wait_ge(kd_in, G * 16)
                        act.wait_ge(pj_full, G * 8 + c + 1)
                        act.activation(y[:].rearrange("p (j i) -> p j i", j=3)[:, :, c * PI:(c + 1) * PI],
                                       pb[:, 6, 0:KC].rearrange("p (j i) -> p j i", j=3), ACT.Copy,
                                       scale=scale[:, 0:1]).then_inc(y_ready, 1)

                def main(G, buf, nxt):
                    if not (isinstance(G, int) and G < 2):
                        act.wait_ge(results, (G - 1) * 48)
                    for t in range(NT):
                        w = P if t < NT - 1 else LAST
                        for u in range(UT):
                            j = t * UT + u
                            act.wait_ge(max_done, G * UH + j + 1)
                            r = place(buf, j)
                            unit = pb[0:w, r:r + 2, 0:KC]
                            act.activation(unit, unit, ACT.Exp, bias=nmx[0:w, buf, t, u:u + 1],
                                           accum_out=es[0:w, buf, t, u:u + 1]).then_inc(exp_done, 1)
                            if nxt and T0 <= t < T0 + 8 and u == 1:
                                nxt(t - T0)

                bodies(act, front, main)


E1 = 8
HID = 256


def segments():
    found = []
    for j in range(3):
        at, end = j * NI, (j + 1) * NI
        while at < end:
            t, p = divmod(at, P)
            if p == 0 and end - at >= P:
                n = (end - at) // P
                found.append((t, t + n, 0, P, j, at - j * NI))
                at += n * P
            else:
                n = min(end - at, P - p)
                if p and p + n > 64 > p:
                    n = 64 - p
                found.append((t, t + 1, p, p + n, j, at - j * NI))
                at += n
    return found


def phase_d(nc, io, x_cm, h_tm, nmx_all, es_all, diag_all, out):
    with ExitStack() as ctx:
        sb = lambda n, s, d=F32: ctx.enter_context(nc.sbuf_tensor("d_" + n, s, d))
        sem = lambda n: ctx.enter_context(nc.semaphore("d_s_" + n))
        HEADS = NB * H1
        SEG = segments()
        a_all = sb("a_all", [P, HEADS, NT])
        m_all = sb("m_all", [P, HEADS, NT])
        ab = sb("ab", [P, H1, NT])
        xv = sb("xv", [C + 1, NI])
        wvT = sb("wvT", [C, 3, H1, C + 1])
        w0 = sb("w0", [C, H1, C])
        wv = sb("wv", [C + 1, 3, H1, C])
        b0 = sb("b0", [P, C])
        one = sb("one", [1, P])
        ident = sb("ident", [P, P])
        av = sb("av", [P, 2, H1, C])
        parts = sb("parts", [1, 3, E1 * C], BF16)
        xT = sb("xT", [C + 1, NP])
        H = sb("H", [P, NT, C])
        xh = sb("xh", [P, NT, C])
        sq = sb("sq", [P, NT, C])
        stat = sb("stat", [P, 4, NT])
        w1 = sb("w1", [C + 1, 2, P])
        wg = sb("wg", [P, 2, E1])
        bg = sb("bg", [1, E1])
        wd = sb("wd", [P, 2, E1 * C])
        bd = sb("bd", [1, E1 * C])
        bd3 = sb("bd3", [3, E1 * C], BF16)
        ones3 = sb("ones3", [3, P], BF16)
        iota = sb("iota", [P, NT, E1])
        hg = sb("hg", [P, 2, NP])
        rt = sb("rt", [P, 3, NT, E1])
        rs = sb("rs", [P, 2, NT])
        yw = sb("yw", [P, 2, E1, C])
        ya = sb("ya", [P, C])
        pb = ctx.enter_context(nc.psum_tensor("d_ps", [P, 8, 512], F32))
        loaded = sem("loaded")
        dve_own = [sem(f"dve_own{i}") for i in range(4)]
        s_low = sem("s_low")
        s_exp = sem("s_exp")
        d_low = sem("d_low")
        d_exp = sem("d_exp")
        h_in = sem("h_in")
        v_done = sem("v_done")
        av_ready = sem("av_ready")
        av_read = sem("av_read")
        w_full = sem("w_full")
        w_ready = sem("w_ready")
        b_split = {n: sem("b_" + n) for n in ("own", "in")}
        S = {n: sem(n) for n in ("var", "std", "xh", "turned", "xT", "passed", "sp_passed")}
        hg_done = sem("hg_done")
        hg_ready = sem("hg_ready")
        lg_done = sem("lg_done")
        lg_ready = sem("lg_ready")
        lg_exp = sem("lg_exp")
        ye_done = sem("ye_done")
        ye_read = sem("ye_read")
        stored = sem("stored")

        with nc.Block() as block:
            @block.sync
            def _(sp):
                loads = ((wvT, "wv1T"), (w0, "w0"), (b0, "b0"), (ident, "ident"), (w1, "w1"), (wg, "wg"), (bg, "bg"),
                         (wd, "wd"), (bd, "bd"), (iota, "iota8"))
                for t, k in loads:
                    sp.dma_start(t[:], io[k]).then_inc(loaded, 16)
                sp.wait_ge(loaded, 16 * len(loads))
                stack_parts(sp, b_split, parts, bd3)

            @block.tensor
            def _(pe):
                pe.wait_ge(loaded, 16 * 10)
                for j in range(3):
                    for h in range(H1):
                        last = pe.matmul(pb[0:C + 1, j, h * C:(h + 1) * C], wvT[:, j, h, :], w0[:, h, :], start=True, stop=True)
                last.then_inc(w_full, 1)

            @block.gpsimd
            def _(pool):
                pool.memset(xv[C:C + 1, :], 1.0)
                pool.memset(one[:], 1.0)
                pool.memset(ones3[:], 1.0)
                pool.wait_ge(loaded, 16 * 10)
                split_row(pool, b_split, bd, parts)

            @block.vector
            def _(dve):
                dve.memset(xT[0:C, N:NP], 0.0)
                dve.memset(xT[C:C + 1, :], 1.0)
                dve.memset(H[:], 0.0)
                own = Chain(dve, dve_own[0], 0, 5)
                nmx = nmx_all[:].rearrange("p g (t u) -> p g t u", u=UT)
                es = es_all[:].rearrange("p g (t u) -> p g t u", u=UT)
                flat = lambda x: x[:].rearrange("p g n -> p (g n)")
                own.link(dve.tensor_reduce(m_all[:], nmx, AX.X, ALU.min))
                dve.tensor_tensor(nmx, m_all[:].unsqueeze(3).to_broadcast([P, HEADS, NT, UT]), nmx, ALU.subtract).then_inc(s_low, 1)
                own.link(dve.tensor_tensor(flat(diag_all), flat(diag_all), flat(m_all), ALU.add))
                dve.tensor_copy(flat(a_all), flat(diag_all)).then_inc(d_low, 1)
                dve.wait_ge(s_exp, 1)
                own.link(dve.tensor_tensor(flat(es_all), flat(es_all), flat(nmx_all), ALU.mult))
                own.link(dve.tensor_reduce(m_all[:], es, AX.X, ALU.add))
                own.link(dve.reciprocal(flat(m_all), flat(m_all)))
                dve.wait_ge(d_exp, 1)
                dve.tensor_tensor(flat(a_all), flat(a_all), flat(m_all), ALU.mult)
                own.end()

            @block.scalar
            def _(act):
                act.wait_ge(s_low, 1)
                act.activation(nmx_all[:], nmx_all[:], ACT.Exp).then_inc(s_exp, 1)
                act.wait_ge(d_low, 1)
                act.activation(a_all[:], a_all[:], ACT.Exp).then_inc(d_exp, 1)
                act.wait_ge(w_full, 1)
                act.activation(wv[:].rearrange("c j h o -> c j (h o)"), pb[0:C + 1, 0:3, :], ACT.Copy)

        with nc.Fori(0, NB) as b:
            RV = 4
            with nc.Block() as block:
                nload = 1 + len(SEG)

                @block.sync
                def _(sp):
                    sp.dma_start(xv[0:C, :], x_cm[:, bass.ds((b + 2 * NB) * NI, NI)]).then_inc(h_in, 16)
                    rows = h_tm.rearrange("(m q) c -> q m c", q=3)
                    for t0, t1, p0, p1, j, i0 in SEG:
                        n = (t1 - t0) * (p1 - p0)
                        sp.dma_start(H[p0:p1, t0:t1, :], rows[j, bass.ds(b * NI + i0, n), :].rearrange(
                            "(t p) c -> p t c", p=p1 - p0)).then_inc(h_in, 16)
                    sp.wait_ge(h_in, (b + 1) * 16 * nload)
                    sp.sem_inc(S["sp_passed"])


                @block.tensor
                def _(pe):
                    pe.wait_ge(h_in, (b + 1) * 16 * nload)

                    for t in range(NT):
                        if t >= RV:
                            pe.wait_ge(av_ready, b * NT + t - RV + 1)
                        for t0, t1, p0, p1, j, i0 in SEG:
                            if t0 <= t < t1:
                                i = i0 + (t - t0) * P
                                last = pe.matmul(pb[p0:p1, t % RV, :], xv[:, i:i + p1 - p0],
                                                 wv[:, j, :, :].rearrange("c h o -> c (h o)"), start=True, stop=True)
                        last.then_inc(v_done, 1)
                    turn_tensor(pe, xh, pb, ident, S, b)

                @block.vector
                def _(dve):
                    own = Chain(dve, dve_own[1], b, 9 + NT)
                    dve.wait_ge(h_in, (b + 1) * 16 * nload)
                    own.link(dve.tensor_copy(ab[:], a_all[:, bass.ds(b * H1, H1), :]))
                    own.link(dve.tensor_tensor(H[:], H[:], b0[:].unsqueeze(1).to_broadcast([P, NT, C]), ALU.add))
                    for t in range(NT):
                        w = P if t < NT - 1 else LAST
                        dve.wait_ge(v_done, b * NT + t + 1)
                        dve.tensor_tensor(av[0:w, t % 2], pb[0:w, t % RV, :].rearrange("p (h o) -> p h o", h=H1),
                                          ab[0:w, :, t].unsqueeze(2).to_broadcast([w, H1, C]), ALU.mult).then_inc(av_ready, 1)
                        dve.wait_ge(av_ready, b * NT + t + 1)
                        own.link(dve.tensor_reduce(xh[0:w, t, :], av[0:w, t % 2].rearrange("p h o -> p o h"), AX.X, ALU.add))
                    dve.tensor_tensor(H[:, 0:NT - 1, :], H[:, 0:NT - 1, :], xh[:, 0:NT - 1, :], ALU.add)
                    own.link(dve.tensor_tensor(H[0:LAST, NT - 1, :], H[0:LAST, NT - 1, :], xh[0:LAST, NT - 1, :], ALU.add))
                    ln_vector(dve, own, H, xh, sq, stat, S, b)
                    own.end()

                @block.scalar
                def _(act):
                    ln_scalar(act, stat, S, b)
                    turn_scalar(act, xT, pb, S, b)

            CHUNKS = [(c * QC, QC) for c in range(NQ)] + [(NQ * QC, P)]
            ND = 2 * len(CHUNKS)
            with nc.Block() as block:
                @block.tensor
                def _(pe):
                    for c, (c0, w) in enumerate(CHUNKS):
                        for k in range(2):
                            n = c * 2 + k
                            if n >= 4:
                                pe.wait_ge(hg_ready, b * ND + n - 3)
                            pe.matmul(pb[:, n % 4, 0:w], w1[:, k, :], xT[:, c0:c0 + w], start=True, stop=True).then_inc(hg_done, 1)
                    pe.wait_ge(hg_ready, (b + 1) * ND)
                    for t in range(NT):
                        dst = pb[:, 4, t * E1:(t + 1) * E1]
                        pe.matmul(dst, one[:], bg[:], start=True, stop=False)
                        for k in range(2):
                            last = pe.matmul(dst, hg[:, k, t * P:(t + 1) * P], wg[:, k, :], start=False, stop=(k == 1))
                    last.then_inc(lg_done, 1)
                    for t in range(NT):
                        if t >= 3:
                            pe.wait_ge(ye_read, b * NT + t - 2)
                        dst = pb[:, 5 + t % 3, :]
                        pe.matmul(dst, ones3[:], bd3[:], start=True, stop=False)
                        for k in range(2):
                            last = pe.matmul(dst, hg[:, k, t * P:(t + 1) * P], wd[:, k, :], start=False, stop=(k == 1))
                        last.then_inc(ye_done, 1)

                @block.scalar
                def _(act):
                    for c, (c0, w) in enumerate(CHUNKS):
                        for k in range(2):
                            n = c * 2 + k
                            act.wait_ge(hg_done, b * ND + n + 1)
                            act.activation(hg[:, k, c0:c0 + w], pb[:, n % 4, 0:w], ACT.Gelu).then_inc(hg_ready, 1)
                    act.wait_ge(lg_ready, b + 1)
                    act.activation(rt[:, 0], rt[:, 0], ACT.Exp).then_inc(lg_exp, 1)

                @block.vector
                def _(dve):
                    own = Chain(dve, dve_own[2], b, 10 + 2 * NT - 1)
                    wide = lambda a: a.unsqueeze(2).to_broadcast([P, NT, E1])
                    tt = lambda o, a, c, op: own.link(dve.tensor_tensor(o, a, c, op))
                    dve.wait_ge(lg_done, b + 1)
                    lg = pb[:, 4, 0:NT * E1].rearrange("p (t e) -> p t e", e=E1)
                    own.link(dve.tensor_reduce(rs[:, 0], lg, AX.X, ALU.max))
                    dve.tensor_tensor(rt[:, 0], lg, wide(rs[:, 0]), ALU.subtract).then_inc(lg_ready, 1)
                    dve.wait_ge(lg_exp, b + 1)
                    own.link(dve.tensor_reduce(rs[:, 0], rt[:, 0], AX.X, ALU.add))
                    own.link(dve.reciprocal(rs[:, 1], rs[:, 0]))
                    tt(rt[:, 0], rt[:, 0], wide(rs[:, 1]), ALU.mult)
                    own.link(dve.tensor_reduce(rs[:, 0], rt[:, 0], AX.X, ALU.max))
                    tt(rt[:, 1], rt[:, 0], wide(rs[:, 0]), ALU.is_equal)
                    tt(rt[:, 2], rt[:, 1], iota[:], ALU.mult)
                    own.link(dve.tensor_reduce(rs[:, 1], rt[:, 2], AX.X, ALU.min))
                    tt(rt[:, 1], iota[:], wide(rs[:, 1]), ALU.is_equal)
                    tt(rt[:, 0], rt[:, 0], rt[:, 1], ALU.mult)
                    for t in range(NT):
                        dve.wait_ge(ye_done, b * NT + t + 1)
                        dve.tensor_tensor(yw[:, t % 2], pb[:, 5 + t % 3, :].rearrange("p (e c) -> p e c", e=E1),
                                          rt[:, 0, t, :].unsqueeze(2).to_broadcast([P, E1, C]), ALU.mult).then_inc(ye_read, 1)
                        dve.wait_ge(ye_read, b * NT + t + 1)
                        own.link(dve.tensor_reduce(ya[:], yw[:, t % 2].rearrange("p e c -> p c e"), AX.X, ALU.add))
                        last = dve.tensor_tensor(H[:, t, :], H[:, t, :], ya[:], ALU.add)
                        if t < NT - 1:
                            own.link(last)
                    own.end()

            with nc.Block() as block:
                @block.sync
                def _(sp):
                    rows = out.rearrange("b (i j) c -> (b i) j c", j=3)
                    for t0, t1, p0, p1, j, i0 in SEG:
                        n = (t1 - t0) * (p1 - p0)
                        sp.dma_start(rows[bass.ds(b * NI + i0, n), j, :].rearrange("(t p) c -> p t c", p=p1 - p0),
                                     H[p0:p1, t0:t1, :]).then_inc(stored, 16)
                    sp.wait_ge(stored, (b + 1) * 16 * len(SEG))
                    sp.sem_inc(S["sp_passed"])


def build(nc, out, **io):
    with ExitStack() as ctx:
        h_cm = nc.dram_tensor("h_cm", [C, NB * N], F32, kind="Internal").ap()
        x_cm = nc.dram_tensor("x_cm", [C, NB * N], F32, kind="Internal").ap()
        h_tm = nc.dram_tensor("h_tm", [NB * N, C], F32, kind="Internal").ap()
        phase_a(nc, io, h_cm)
        phase_b(nc, io, h_cm, x_cm, h_tm)
        nmx_all = ctx.enter_context(nc.sbuf_tensor("nmx_all", [P, NB * H1, UH], F32))
        es_all = ctx.enter_context(nc.sbuf_tensor("es_all", [P, NB * H1, UH], F32))
        diag_all = ctx.enter_context(nc.sbuf_tensor("diag_all", [P, NB * H1, NT], F32))
        phase_c(nc, io, x_cm, nmx_all, es_all, diag_all)
        phase_d(nc, io, x_cm, h_tm, nmx_all, es_all, diag_all, out)


def layout(a):
    import numpy as np

    d = {}
    half = lambda w: np.tile(w, (2, 1))
    with_bias = lambda w, b: np.concatenate([w, b[None]], 0)
    d["x"], d["txt"] = a["x"], a["txt"].transpose(2, 0, 1)
    d["tok_w1"] = np.tile(a["L0_tok_w1"].reshape(C, 3, C).transpose(2, 1, 0), (1, 1, 2))
    d["tok_b1"] = half(a["L0_tok_b1"].reshape(C, 3))
    d["tok_w2"] = half(a["L0_tok_w2"].T.reshape(NH, C // NH, C).transpose(1, 0, 2).reshape(C, C))
    d["tok_b2"] = half(a["L0_tok_b2"].reshape(C, 1))
    d["pos"] = a["L0_tok_pos_emb"].reshape(1, 2 * WS - 1, 2 * WS - 1)
    lane = np.arange(P)
    d["head_mask"] = (lane[:, None] % NH == np.arange(NH)).astype(np.float32)
    d["ident"] = np.eye(P, dtype=np.float32)
    token = np.arange(WT)
    row = (token[:, None] >= WT // 2) != (token[None] >= WT // 2)
    col = row.reshape(WS, WS, WS, WS).transpose(1, 0, 3, 2).reshape(WT, WT)
    unmet = np.zeros((4, 2, WT, WR, 2, WT), np.float32)
    unmet[:, :, :, WR - 1] += np.where(row, np.float32(MASKED), np.float32(0))[None, None, :, None]
    unmet[(HW - 1) % 4, 1, :, :, (HW - 1) // 4] += np.where(col, np.float32(MASKED), np.float32(0))[:, None]
    d["masks"] = unmet.reshape(P, WR, 2, WT)
    wq, bq = a["L0_attn_W_qkv"], a["L0_attn_b_qkv"]
    d["wqk"] = with_bias(wq[:2 * C].T, bq[:2 * C])
    d["wv"] = with_bias(wq[2 * C:].T, bq[2 * C:])
    d["scale"] = np.where(lane[:, None] < C, D0 ** -0.5, 1.0).astype(np.float32)
    d["scale1"] = np.where(lane[:, None] < C, C ** -0.5, 1.0).astype(np.float32)
    wp = np.zeros((G0, 32, C), np.float32)
    wp[:, :D0] = a["L0_attn_W_proj"].T.reshape(G0, D0, C)
    d["wp"], d["bp"] = wp.reshape(P, C), np.broadcast_to(a["L0_attn_b_proj"], (P, C))
    d["selz"] = ((lane[:, None] % 32 == D0) & (lane[:, None] // 32 == lane[None] // 32)).astype(np.float32)
    d["rw1"] = with_bias(a["L0_ffn_router_w1"], a["L0_ffn_router_b1"])
    d["rw2"] = with_bias(a["L0_ffn_router_w2"], a["L0_ffn_router_b2"])
    w = a["L0_ffn_expert_w1"].reshape(3, 2, C, C).transpose(2, 0, 1, 3).reshape(C, 3, P)
    d["ew1"] = np.concatenate([w, a["L0_ffn_expert_b1"].reshape(1, 3, P)], 0)
    for k, n in (("ew2", "L0_ffn_expert_w2"), ("ew3", "L0_ffn_expert_w3")):
        z = np.zeros((2, C, 3, 2, C), np.float32)
        for e in range(2):
            z[e, :, :, e, :] = a[n].reshape(3, 2, C, C)[:, e].transpose(1, 0, 2)
        d[k] = z.reshape(P, 3, P)
    d["eb2"] = a["L0_ffn_expert_b2"].reshape(3, P).T
    d["eb3"] = a["L0_ffn_expert_b3"].reshape(1, 3 * P)
    d["iota"] = np.broadcast_to(np.arange(E0, dtype=np.float32), (P, NT, E0))
    d["iota8"] = np.broadcast_to(np.arange(E1, dtype=np.float32) - E1, (P, NT, E1))
    w = np.concatenate([a["L1_attn_Wqkv"], a["L1_attn_bqkv"][None]], 0)
    d["w_qk"] = w.reshape(C + 1, 3, C, H1).transpose(3, 0, 1, 2)
    d["wv1T"] = w.reshape(C + 1, 3, C, H1).transpose(2, 1, 3, 0)
    d["w0"] = a["L1_attn_W0"].reshape(C, H1, C)
    d["b0"] = np.broadcast_to(a["L1_attn_b0"], (P, C))
    d["w1"] = with_bias(a["L1_ffn_W1"], a["L1_ffn_b1"]).reshape(C + 1, 2, P)
    d["wg"] = a["L1_ffn_Wg"].reshape(2, P, E1).transpose(1, 0, 2)
    d["bg"] = a["L1_ffn_bg"][None]
    d["wd"] = a["L1_ffn_Wd"].transpose(1, 0, 2).reshape(2, P, E1 * C).transpose(1, 0, 2)
    d["bd"] = a["L1_ffn_bd"].reshape(1, E1 * C)
    return {k: np.ascontiguousarray(v) for k, v in d.items()}


def kernel(**inputs):
    import numpy as _np
    import concourse.bacc as _bacc
    from concourse.bass_utils import run_bass_kernel_spmd as _run

    nc = _bacc.Bacc("TRN2", target_bir_lowering=False, num_devices=1)
    arrays, io = {}, {}
    for name, a in layout({k: _np.asarray(v) for k, v in inputs.items()}).items():
        arrays["in_" + name] = a
        io[name] = nc.dram_tensor("in_" + name, a.shape, mybir.dt.from_np(a.dtype), kind="ExternalInput").ap()
    out = nc.dram_tensor("out_0", (NB, N, C), F32, kind="ExternalOutput").ap()
    build(nc, out, **io)
    r = _run(nc, [arrays], core_ids=[0])
    return r.results[0]["out_0"]
```

```python
from contextlib import ExitStack

import concourse.bass as bass
from concourse import mybir

F32 = mybir.dt.float32
BF16 = mybir.dt.bfloat16
F32R = mybir.dt.float32r
ALU = mybir.AluOpType
ACT = mybir.ActivationFunctionType
AX = mybir.AxisListType

NB = 4
C = 64
SIDE = 56
IMG = SIDE * SIDE
TXT = 32
N = IMG + TXT
P = 128
NT = 25
LAST = N - (NT - 1) * P
WS = 4
WT = WS * WS
NH = 8
WR = SIDE // WS
HW = WR // 2
HT = HW * WT
ROWS_A = NB * WR
MASKED = -1e30
EPS = 1e-5


class Chain:

    def __init__(self, eng, sem, i=0, per=0):
        self.eng, self.sem, self.base, self.n, self.per = eng, sem, i * per, 0, per

    def link(self, ins):
        self.n += 1
        ins.then_inc(self.sem, 1)
        self.eng.wait_ge(self.sem, self.base + self.n)

    def end(self):
        assert self.n == self.per, self.n


def wait(eng, sem, value):
    if not (isinstance(value, int) and value <= 0):
        eng.wait_ge(sem, value)


def phase_a(nc, io, h_cm):
    with ExitStack() as ctx:
        sb = lambda n, s, d=F32: ctx.enter_context(nc.sbuf_tensor("a_" + n, s, d))
        ps = lambda n, s, d=F32: ctx.enter_context(nc.psum_tensor("a_p_" + n, s, d))
        sem = lambda n: ctx.enter_context(nc.semaphore("a_s_" + n))
        X = sb("x", [C, NB * IMG])
        w1 = sb("w1", [C, 3, P])
        b1 = sb("b1", [P, 3])
        w2 = sb("w2", [P, 2, C])
        b2 = sb("b2", [P, 1])
        mask = sb("mask", [P, NH])
        ident = sb("ident", [P, P])
        bias = sb("bias", [P, WR, 2, WT])
        unmet = sb("unmet", [P, WR, 2, WT])
        q = sb("q", [P, HW, 2, WT])
        kv = sb("kv", [P, 2, HT])
        kexp = sb("kexp", [P, HW, NH, WT])
        vexp = sb("vexp", [P, HW, NH, WT])
        prob = sb("prob", [P, 2, NH, WT])
        stat = sb("stat", [P, 3, 2 * NH])
        vw = sb("vw", [P, 2, HW, P])
        pt = sb("pt", [P, 2 * P])
        yrow = sb("yrow", [C, WS * SIDE])
        p_proj = ps("proj", [P, 2, 512])
        p_s = ps("s", [P, 512])
        p_pty = ps("pty", [P, 512])
        p_pt = p_pty[:, 0:2 * P]
        p_y = p_pty[:, 2 * P:2 * P + HW * 2 * WT]
        p_vw = ps("vw", [P, 8 * P])

        w2_zeroed = sem("w2_zeroed")
        s_zeroed = sem("s_zeroed")
        first_in = sem("first_in")
        loaded = sem("loaded")
        bias_in = sem("bias_in")
        bias_ok = sem("bias_ok")
        txt_in = sem("txt_in")
        proj_done = sem("proj_done")
        kv_ready = sem("kv_ready")
        kexp_ready = sem("kexp_ready")
        vexp_ready = sem("vexp_ready")
        s_done = sem("s_done")
        s_read = sem("s_read")
        shifted = sem("shifted")
        exp_done = sem("exp_done")
        p_ready = sem("p_ready")
        vw_done = sem("vw_done")
        vw_ready = sem("vw_ready")
        pt_done = sem("pt_done")
        pt_ready = sem("pt_ready")
        y_done = sem("y_done")
        y_read = sem("y_read")
        y_out = sem("y_out")
        dve_own = sem("dve_own")
        dve_low = sem("dve_low")
        dve_set = sem("dve_set")

        Xv = X[:].rearrange("c (b h w) -> c b h w", b=NB, h=SIDE)
        x = io["x"]
        R = SIDE - 2
        FIRST = 4 + 5 + 2
        with nc.Block() as block:
            def picture(eng, b, sem):
                for i0, i1, s0 in ((0, R, 2), (R, SIDE, 0)):
                    for j0, j1, t0 in ((0, R, 2), (R, SIDE, 0)):
                        eng.dma_start(Xv[:, b, i0:i1, j0:j1],
                                      x[b, :, s0:s0 + i1 - i0, t0:t0 + j1 - j0]).then_inc(sem, 16)

            @block.sync
            def _(sp):
                picture(sp, 0, first_in)
                for t, k in ((w1, "tok_w1"), (b1, "tok_b1"), (b2, "tok_b2"), (mask, "head_mask"), (ident, "ident")):
                    sp.dma_start(t[:], io[k]).then_inc(first_in, 16)
                sp.wait_ge(w2_zeroed, 1)
                for half in range(2):
                    lanes = slice(half * C, half * C + C)
                    sp.dma_start(w2[lanes, half, :], io["tok_w2"][lanes, :]).then_inc(first_in, 16)
                for b in range(1, NB):
                    picture(sp, b, loaded)
                sp.dma_start(h_cm.rearrange("c (b n) -> c b n", b=NB)[:, :, IMG:N], io["txt"]).then_inc(txt_in, 16)
                with sp.Fori(0, ROWS_A) as g:
                    sp.wait_ge(y_read, g + 1)
                    sp.dma_start(h_cm[:, bass.ds(g // WR * N + g % WR * (WS * SIDE), WS * SIDE)], yrow[:]).then_inc(y_out, 16)
                sp.wait_ge(y_out, NB * WR * 16)
                sp.wait_ge(txt_in, 16)

            @block.tensor
            def _(pe):
                pe.wait_ge(first_in, 16 * FIRST)
                pe.wait_ge(s_zeroed, 1)

                def project(g):
                    wait(pe, kv_ready, g)
                    for s in range(3):
                        rows = X[:, bass.ds(g * WS * SIDE, WS * SIDE)].rearrange("c (r w s) -> c w r s", r=WS, s=WS)
                        bank, c0 = ((1, 0), (0, 0), (0, 2 * HT))[s]
                        last = pe.matmul(p_proj[:, bank, c0:c0 + 2 * HT], w1[:, s, :], rows,
                                         start=True, stop=True)
                    last.then_inc(proj_done, 1)

                def scores(g):
                    wait(pe, kexp_ready, g + 1)
                    wait(pe, s_read, g)
                    for w in range(HW):
                        r0, c0 = w % 4 * 2 * WT, w // 4 * P
                        last = pe.matmul(p_s[r0:r0 + 2 * WT, c0:c0 + P], q[:, w, :, :].rearrange("p t q -> p (t q)"),
                                         kexp[:, w, :, :].rearrange("p h k -> p (h k)"), start=True, stop=True)
                    last.then_inc(s_done, 1)

                def values(g):
                    wait(pe, vexp_ready, g + 1)
                    wait(pe, vw_ready, g)
                    for w in range(HW):
                        last = pe.matmul(p_vw[:, w * P:(w + 1) * P],
                                         vexp[:, w, :, :].rearrange("p h k -> p (h k)"),
                                         w2[:].rearrange("p t o -> p (t o)"), start=True, stop=True)
                    last.then_inc(vw_done, 1)

                def turn(g):
                    wait(pe, p_ready, g + 1)
                    wait(pe, y_read, g)
                    for group in range(2):
                        last = pe.transpose(p_pt[:, group * P:(group + 1) * P],
                                            prob[:, group, :, :].rearrange("q h k -> q (h k)"), ident[:])
                    last.then_inc(pt_done, 1)

                def result(g, buf):
                    wait(pe, pt_ready, g + 1)
                    wait(pe, vw_ready, g + 1)
                    for w in range(HW):
                        last = pe.matmul(p_y[:, w * 2 * WT:(w + 1) * 2 * WT], vw[:, buf, w, :],
                                         pt[:, w * 2 * WT:(w + 1) * 2 * WT], start=True, stop=True)
                    last.then_inc(y_done, 1)

                def step(i, buf):
                    scores(i - 1)
                    turn(i - 2)
                    values(i - 1)
                    result(i - 2, buf)

                project(0)
                project(1)
                scores(0)
                values(0)
                project(2)
                step(2, 0)
                project(3)
                step(3, 1)
                project(4)
                pe.wait_ge(loaded, 16 * 4 * (NB - 1))
                with pe.Fori(4, ROWS_A - 3, 2) as i:
                    step(i, 0)
                    project(i + 1)
                    step(i + 1, 1)
                    project(i + 2)
                step(ROWS_A - 2, 0)
                project(ROWS_A - 1)
                step(ROWS_A - 1, 1)
                step(ROWS_A, 0)
                turn(ROWS_A - 1)
                result(ROWS_A - 1, 1)

            @block.vector
            def _(dve):
                own = Chain(dve, dve_set)
                dve.memset(w2[:], 0.0).then_inc(w2_zeroed, 1)
                own.link(dve.memset(q[:], 0.0))
                dve.memset(p_s[:, P:2 * P], 0.0).then_inc(s_zeroed, 1)
                dve.wait_ge(bias_in, 16 * WT)
                own.link(dve.tensor_copy(bias[:, 0, 1, :], bias[:, 0, 0, :]))
                for r in range(1, WR):
                    last = dve.tensor_copy(bias[:, r, :, :], bias[:, 0, :, :])
                own.link(last)
                dve.wait_ge(bias_ok, 16)
                own.link(dve.tensor_tensor(bias[:], bias[:], unmet[:], ALU.add))
                dve.wait_ge(first_in, 16 * FIRST)
                flat = prob[:].rearrange("q t h k -> q (t h) k")
                wide = lambda i: stat[:, i, :].unsqueeze(2).to_broadcast([P, 2 * NH, WT])

                def inputs(g):
                    wait(dve, proj_done, g + 1)
                    wait(dve, vexp_ready, g)
                    wait(dve, s_done, g)
                    for half in range(2):
                        lanes = slice(half * C, half * C + C)
                        dve.tensor_scalar(q[lanes, :, half, :], p_proj[lanes, 1, half * HT:(half + 1) * HT].rearrange(
                            "p (w q) -> p w q", q=WT), b1[lanes, 0:1], float((C / NH) ** -0.5), ALU.add, ALU.mult)
                        last = dve.tensor_tensor(kv[lanes, :, :], p_proj[lanes, 0, 0:4 * HT].rearrange(
                            "p (s t) -> p s t", s=2)[:, :, half * HT:(half + 1) * HT],
                            b1[lanes, 1:3].unsqueeze(2).to_broadcast([C, 2, HT]), ALU.add)
                    last.then_inc(kv_ready, 1)
                    wait(dve, kv_ready, g + 1)
                    dve.tensor_tensor(kexp[:],
                                      kv[:, 0, :].rearrange("p (w k) -> p w k", k=WT).unsqueeze(2).to_broadcast([P, HW, NH, WT]),
                                      mask[:].unsqueeze(1).unsqueeze(3).to_broadcast([P, HW, NH, WT]), ALU.mult).then_inc(kexp_ready, 1)

                def shift(g):
                    own = Chain(dve, dve_low, g, 1)
                    wait(dve, s_done, g + 1)
                    wait(dve, pt_done, g)
                    dve.tensor_tensor(prob[:],
                                      p_s[:, 0:2 * P].rearrange("q (t h k) -> q t h k", t=2, h=NH),
                                      bias[:, bass.ds(g % WR, 1), :, :].rearrange("q r t k -> q (r t) k").unsqueeze(2).to_broadcast([P, 2, NH, WT]),
                                      ALU.add).then_inc(s_read, 1)
                    wait(dve, s_read, g + 1)
                    own.link(dve.tensor_reduce(stat[:, 0, :], flat, AX.X, ALU.max))
                    dve.tensor_tensor(flat, flat, wide(0), ALU.subtract).then_inc(shifted, 1)
                    own.end()

                def norm(g):
                    own = Chain(dve, dve_own, g, 2)
                    wait(dve, exp_done, g + 1)
                    own.link(dve.tensor_reduce(stat[:, 1, :], flat, AX.X, ALU.add))
                    own.link(dve.reciprocal(stat[:, 2, :], stat[:, 1, :]))
                    dve.tensor_tensor(flat, flat, wide(2), ALU.mult).then_inc(p_ready, 1)
                    own.end()

                def step(i):
                    inputs(i)
                    shift(i - 1)
                    norm(i - 1)
                    wait(dve, p_ready, i)

                inputs(0)
                step(1)
                with dve.Fori(2, ROWS_A) as i:
                    step(i)
                shift(ROWS_A - 1)
                norm(ROWS_A - 1)

            @block.gpsimd
            def _(pool):
                pool.dma_start(unmet[:], io["masks"]).then_inc(bias_ok, 16)
                pool.wait_ge(first_in, 16 * FIRST)

                def spread(g):
                    wait(pool, kv_ready, g + 1)
                    wait(pool, vw_done, g)
                    pool.tensor_tensor(vexp[:],
                                       kv[:, 1, :].rearrange("p (w k) -> p w k", k=WT).unsqueeze(2).to_broadcast([P, HW, NH, WT]),
                                       mask[:].unsqueeze(1).unsqueeze(3).to_broadcast([P, HW, NH, WT]), ALU.mult).then_inc(vexp_ready, 1)

                spread(0)
                with pool.Fori(1, ROWS_A) as g:
                    spread(g)

            @block.scalar
            def _(act):
                for p in range(WT):
                    pi, pj = divmod(p, WS)
                    act.dma_start(bias[p:P:WT, 0, 0, :].rearrange("p (a c) -> p a c", a=WS),
                                  io["pos"][:, 3 - pi:7 - pi, 3 - pj:7 - pj].to_broadcast([P // WT, WS, WS])).then_inc(bias_in, 16)
                act.wait_ge(first_in, 16 * FIRST)

                def values(g, buf):
                    wait(act, vw_done, g + 1)
                    wait(act, y_done, g - 1)
                    act.activation(vw[:, buf].rearrange("p w o -> p (w o)"), p_vw[:, 0:HW * P], ACT.Copy).then_inc(vw_ready, 1)

                def exps(g):
                    wait(act, shifted, g + 1)
                    act.activation(prob[:], prob[:], ACT.Exp).then_inc(exp_done, 1)

                def probs(g):
                    wait(act, pt_done, g + 1)
                    wait(act, y_done, g)
                    act.activation(pt[:], p_pt, ACT.Copy).then_inc(pt_ready, 1)

                def out(g):
                    wait(act, y_done, g + 1)
                    wait(act, y_out, g * 16)
                    for half in range(2):
                        last = act.activation(yrow[:].rearrange("c (r t w s) -> c t w r s", r=WS, t=2, s=WS)[:, half],
                                              p_y[half * C:half * C + C, :].rearrange("c (w t r s) -> c t w r s", t=2, r=WS, s=WS)[:, half],
                                              ACT.Identity, bias=b2[half * C:half * C + C, 0:1])
                    last.then_inc(y_read, 1)

                def step(i, buf):
                    probs(i - 2)
                    values(i - 1, 1 - buf)
                    out(i - 2)
                    exps(i - 1)

                values(0, 0)
                exps(0)
                step(2, 0)
                step(3, 1)
                with act.Fori(4, ROWS_A - 1, 2) as i:
                    step(i, 0)
                    step(i + 1, 1)
                step(ROWS_A, 0)
                probs(ROWS_A - 1)
                out(ROWS_A - 1)


NP = NT * P
G0 = 4
D0 = C // G0
QC = 3 * P
NQ = N // QC
KC = 396
NK = N // KC
KU = 1
NKU = NK // KU
RING = 3
MSTEPS = 23
STEPS = NT
ROWS = 6 * D0
M0 = ROWS
E0 = 6
PARTS = ((0, 0), (0, 1), (1, 0), (1, 1), (0, 2), (2, 0))


def ln_vector(dve, own, H, xh, sq, stat, s, k):
    wide = lambda i: stat[:, i, :].unsqueeze(2).to_broadcast([P, NT, C])
    own.link(dve.tensor_reduce(stat[:, 0, :], H[:], AX.X, ALU.add))
    own.link(dve.tensor_scalar(stat[:, 0, :], stat[:, 0, :], 1.0 / C, None, ALU.mult))
    own.link(dve.tensor_tensor(xh[:], H[:], wide(0), ALU.subtract))
    own.link(dve.tensor_tensor(sq[:], xh[:], xh[:], ALU.mult))
    own.link(dve.tensor_reduce(stat[:, 1, :], sq[:], AX.X, ALU.add))
    dve.tensor_scalar(stat[:, 1, :], stat[:, 1, :], 1.0 / C, EPS, ALU.mult, ALU.add).then_inc(s["var"], 1)
    dve.wait_ge(s["std"], k + 1)
    own.link(dve.reciprocal(stat[:, 3, :], stat[:, 2, :]))
    dve.tensor_tensor(xh[:], xh[:], wide(3), ALU.mult).then_inc(s["xh"], 1)


def ln_scalar(act, stat, s, k):
    act.wait_ge(s["var"], k + 1)
    act.activation(stat[:, 2, :], stat[:, 1, :], ACT.Sqrt).then_inc(s["std"], 1)


GROUPS = [(4 * g, min(4 * g + 4, NT)) for g in range((NT + 3) // 4)]


def turn_tensor(pe, xh, pb, ident, s, k):
    pe.wait_ge(s["xh"], k + 1)
    pe.sem_inc(s["passed"])
    for g, (t0, t1) in enumerate(GROUPS):
        for t in range(t0, t1):
            last = pe.transpose(pb[0:C, g, (t - t0) * P:(t - t0 + 1) * P], xh[:, t, :], ident[:])
        last.then_inc(s["turned"], 1)


def turn_scalar(act, xT, pb, s, k):
    for g, (t0, t1) in enumerate(GROUPS):
        act.wait_ge(s["turned"], k * len(GROUPS) + g + 1)
        act.activation(xT[0:C, t0 * P:t1 * P], pb[0:C, g, 0:(t1 - t0) * P], ACT.Copy).then_inc(s["xT"], 1)


def weigh(dve, b, products, weights, dst, buf, full, read, summed, last=P):
    width = lambda t: P if t < NT - 1 else last
    for t in range(NT + 1):
        if t < NT:
            w = width(t)
            dve.wait_ge(full, b * NT + t + 1)
            if t >= 3:
                dve.wait_ge(summed, b * NT + t - 2)
            dve.tensor_tensor(buf[0:w, t % 3], products(t)[0:w], weights(t)[0:w].unsqueeze(2).to_broadcast([w] + list(buf.shape[2:])),
                              ALU.mult).then_inc(read, 1)
        if t:
            w = width(t - 1)
            dve.wait_ge(read, b * NT + t)
            dve.tensor_reduce(dst[0:w, t - 1, :], buf[0:w, (t - 1) % 3].rearrange("p e c -> p c e"), AX.X, ALU.add).then_inc(summed, 1)
    dve.wait_ge(summed, (b + 1) * NT)


def split_row(pool, s, row, parts):
    own = Chain(pool, s["own"])
    for part in range(3):
        own.link(pool.tensor_copy(parts[:, part, :], row[:]))
        if part < 2:
            own.link(pool.tensor_tensor(row[:], row[:], parts[:, part, :], ALU.subtract))


def stack_parts(sp, s, parts, dst):
    for part in range(3):
        sp.wait_ge(s["own"], 2 * part + 1)
        sp.dma_start(dst[part:part + 1, :], parts[:, part, :]).then_inc(s["in"], 16)
    sp.wait_ge(s["in"], 48)


def phase_b(nc, io, h_cm, x_cm, h_tm):
    with ExitStack() as ctx:
        sb = lambda n, s, d=F32: ctx.enter_context(nc.sbuf_tensor("b_" + n, s, d))
        sem = lambda n: ctx.enter_context(nc.semaphore("b_s_" + n))
        xT = sb("xT", [C + 1, NP])
        H = sb("H", [P, NT, C])
        xh = sb("xh", [P, NT, C])
        sq = sb("sq", [P, NT, C])
        stat = sb("stat", [P, 4, NT])
        ident = sb("ident", [P, P])
        identh = sb("identh", [P, P], BF16)
        wqk = sb("wqk", [C + 1, P])
        wv = sb("wv", [C + 1, C])
        scale = sb("scale", [P, 1])
        V = sb("V", [P, NT, G0, 32])
        Qs = sb("Qs", [P, G0, N], BF16)
        Ks = sb("Ks", [P, G0, N], BF16)
        y = sb("y", [P, N])
        parts = sb("parts", [P, 3, N], BF16)
        prob = sb("prob", [P, 2, G0, QC])
        mx = sb("mx", [P, 3 * G0, NKU])
        nm = sb("nm", [P, 2, 3 * G0])
        nsp = sb("nsp", [P, 3 * G0, 3], BF16)
        O = y
        wp = sb("wp", [P, G0 * C + G0])
        bp = sb("bp", [P, C])
        rz = sb("rz", [P, 4, G0])
        oh = sb("oh", [P, 4, G0, C])
        pb = ctx.enter_context(nc.psum_tensor("b_ps", [P, 8, 512], F32))
        rw1 = sb("rw1", [C + 1, 32])
        rw2 = sb("rw2", [33, E0])
        ew1 = sb("ew1", [C + 1, 3, P])
        ew2 = sb("ew2", [P, 3, P])
        eb2 = sb("eb2", [P, 3])
        ew3 = sb("ew3", [P, 3, P])
        eb3 = sb("eb3", [1, 3 * P])
        eb3p = sb("eb3p", [1, 3, 3 * P], BF16)
        eb33 = sb("eb33", [3, 3 * P], BF16)
        ones3 = sb("ones3", [3, P], BF16)
        iota = sb("iota", [P, NT, E0])
        rh = sb("rh", [33, NP])
        rt = sb("rt", [P, 8, NT, E0])
        rs = sb("rs", [P, 4, NT])
        W = sb("W", [P, NT, E0])
        h1 = sb("h1", [P, 3, QC])
        h2 = sb("h2", [P, 2, 3, QC])
        yw = sb("yw", [P, 3, E0, C])

        loaded = sem("loaded")
        pool_own = sem("pool_own")
        b_split = {n: sem("b_" + n) for n in ("own", "in")}
        dve_own = [sem(f"dve_own{i}") for i in range(5)]
        h_in = sem("h_in")
        S = {n: sem(n) for n in ("var", "std", "xh", "turned", "xT")}
        S["passed"] = sem("passed")
        S["sp_passed"] = sem("sp_passed")
        S["spread0"], S["spread3"] = sem("spread0"), sem("spread3")
        h_turned = sem("h_turned")
        h_read = sem("h_read")
        v_done = sem("v_done")
        qk_done = sem("qk_done")
        y_ready = sem("y_ready")
        part_ready = sem("part_ready")
        stacked = sem("stacked")
        pool_stacked = sem("pool_stacked")
        mu_full = sem("mu_full")
        mu_free = sem("mu_free")
        n_ready = sem("n_ready")
        rows_full = sem("rows_full")
        rows_ready = sem("rows_ready")
        s_full = sem("s_full")
        p_full = sem("p_full")
        pv_done = sem("pv_done")
        o_read = sem("o_read")
        pr_done = sem("pr_done")
        pr_read = sem("pr_read")
        rh_done = sem("rh_done")
        rh_ready = sem("rh_ready")
        lg_done = sem("lg_done")
        lg_ready = sem("lg_ready")
        lg_exp = sem("lg_exp")
        two_ready = sem("two_ready")
        two_exp = sem("two_exp")
        h1_done = sem("h1_done")
        h1_ready = sem("h1_ready")
        h2_done = sem("h2_done")
        h2_ready = sem("h2_ready")
        ye_done = sem("ye_done")
        ye_read = sem("ye_read")
        ye_summed = sem("ye_summed")
        stored = sem("stored")

        with nc.Block() as block:
            @block.sync
            def _(sp):
                loads = ((ident, "ident"), (wqk, "wqk"), (wv, "wv"), (scale, "scale"), (wp, "wp"), (bp, "bp"),
                         (rw1, "rw1"), (rw2, "rw2"), (ew1, "ew1"), (ew2, "ew2"), (eb2, "eb2"),
                         (ew3, "ew3"), (eb3, "eb3"), (iota, "iota"))
                for t, k in loads:
                    sp.dma_start(t[:], io[k]).then_inc(loaded, 16)
                sp.wait_ge(loaded, 16 * len(loads))
                stack_parts(sp, b_split, eb3p, eb33)

            @block.vector
            def _(dve):
                dve.memset(xT[0:C, N:NP], 0.0)
                dve.memset(xT[C:C + 1, :], 1.0)
                dve.memset(H[:], 0.0)
                dve.memset(ones3[:], 1.0)
                dve.memset(rh[32:33, :], 1.0)

            @block.tensor
            def _(pe):
                pe.sem_inc(pv_done)

            @block.scalar
            def _(act):
                act.sem_inc(o_read)

            @block.gpsimd
            def _(pool):
                own = Chain(pool, pool_own)
                own.link(pool.memset(V[:], 0.0))
                own.link(pool.memset(V[:, :, :, D0:D0 + 1], 1.0))
                own.link(pool.memset(Ks[96:128, :, :], 1.0))
                pool.wait_ge(loaded, 16 * 14)
                split_row(pool, b_split, eb3, eb3p)
        with nc.Block() as block:
            @block.vector
            def _(dve):
                dve.tensor_copy(identh[:], ident[:])

        with nc.Fori(0, NB) as b:
            def spread(eng, stacked, heads):
                for part in range(3):
                    eng.wait_ge(part_ready, b * 3 + part + 1)
                    eng.sem_inc(S[f"spread{heads[0]}"])
                    for r, (pq, pk) in enumerate(PARTS):
                        for h in heads:
                            rows = slice(r * D0, (r + 1) * D0)
                            if pq == part:
                                eng.dma_start(Qs[rows, h, :], parts[h * D0:(h + 1) * D0, part, :]).then_inc(stacked, 16)
                            if pk == part:
                                eng.dma_start(Ks[rows, h, :], parts[C + h * D0:C + (h + 1) * D0, part, :]).then_inc(stacked, 16)

            with nc.Block() as block:
                @block.sync
                def _(sp):
                    sp.dma_start(xT[0:C, 0:N], h_cm[:, bass.ds(b * N, N)]).then_inc(h_in, 16)
                    spread(sp, stacked, (0, 1, 2))
                    sp.wait_ge(stacked, (b + 1) * 16 * 6 * len(PARTS))
                    sp.sem_inc(S["sp_passed"])

                @block.tensor
                def _(pe):
                    pe.wait_ge(h_in, (b + 1) * 16)
                    pe.sem_inc(S["passed"])
                    for t in range(NT):
                        w = P if t < NT - 1 else LAST
                        last = pe.transpose(pb[0:w, t // 8, t % 8 * C:(t % 8 + 1) * C], xT[0:C, t * P:t * P + w], ident[0:C, 0:C])
                    last.then_inc(h_turned, 1)
                    pe.wait_ge(h_read, b + 1)
                    turn_tensor(pe, xh, pb, ident, S, b * 3)
                    pe.wait_ge(S["xT"], (b * 3 + 1) * len(GROUPS))
                    for c in range(NK):
                        last = pe.matmul(pb[:, c, 0:KC], wqk[:], xT[:, c * KC:(c + 1) * KC], start=True, stop=True)
                        if c % 4 == 3:
                            last.then_inc(qk_done, 1)
                    pe.wait_ge(y_ready, b * 2 + 1)
                    for t in range(NT):
                        last = pe.matmul(pb[:, t // 8, t % 8 * C:(t % 8 + 1) * C], xT[:, t * P:(t + 1) * P], wv[:], start=True, stop=True)
                    last.then_inc(v_done, 1)

                @block.vector
                def _(dve):
                    own = Chain(dve, dve_own[0], b, 8)
                    dve.wait_ge(h_turned, b + 1)
                    for t0 in (0, 8, 16):
                        dve.tensor_copy(H[:, t0:t0 + 8, :], pb[:, t0 // 8, :].rearrange("p (t c) -> p t c", t=8))
                    dve.tensor_copy(H[0:LAST, NT - 1, :], pb[0:LAST, 3, 0:C]).then_inc(h_read, 1)
                    dve.wait_ge(h_read, b + 1)
                    ln_vector(dve, own, H, xh, sq, stat, S, b * 3)
                    dve.wait_ge(y_ready, (b + 1) * 2)
                    dve.wait_ge(part_ready, b * 3 + 1)
                    own.link(dve.tensor_tensor(y[:], y[:], parts[:, 0, :], ALU.subtract))
                    dve.tensor_copy(parts[:, 1, :], y[:]).then_inc(part_ready, 1)
                    dve.wait_ge(part_ready, b * 3 + 2)
                    own.link(dve.tensor_tensor(y[:], y[:], parts[:, 1, :], ALU.subtract))
                    dve.tensor_copy(parts[:, 2, :], y[:]).then_inc(part_ready, 1)
                    dve.wait_ge(v_done, b + 1)
                    for g in range(4):
                        t0, t1 = 8 * g, min(8 * g + 8, NT)
                        last = dve.tensor_copy(V[:, t0:t1, :, 0:D0], pb[:, g, 0:(t1 - t0) * C].rearrange("p (t h e) -> p t h e", h=G0, e=D0))
                    own.end()

                @block.scalar
                def _(act):
                    ln_scalar(act, stat, S, b * 3)
                    turn_scalar(act, xT, pb, S, b * 3)
                    for g in range(2):
                        act.wait_ge(qk_done, b * 2 + g + 1)
                        src = pb[:, 4 * g:4 * g + 4, 0:KC]
                        cols = slice(g * 4 * KC, (g + 1) * 4 * KC)
                        last = act.activation(parts[:, 0, cols].rearrange("p (a n) -> p a n", a=4), src, ACT.Copy, scale=scale[:, 0:1])
                    last.then_inc(part_ready, 1)
                    for g in range(2):
                        src = pb[:, 4 * g:4 * g + 4, 0:KC]
                        cols = slice(g * 4 * KC, (g + 1) * 4 * KC)
                        act.activation(y[:, cols].rearrange("p (a n) -> p a n", a=4), src, ACT.Copy, scale=scale[:, 0:1]).then_inc(y_ready, 1)

                @block.gpsimd
                def _(pool):
                    spread(pool, pool_stacked, (3,))
                    pool.wait_ge(pool_stacked, (b + 1) * 16 * 2 * len(PARTS))
                    pool.sem_inc(S["spread3"])

            NU = 3 * G0 * NKU
            UNITS = NQ * NU + G0 * NKU
            nchunk = NQ + 1
            flat = pb[:].rearrange("p a n -> p (a n)")
            top = flat[:, 5 * 512:8 * 512]

            with nc.Block() as block:
                @block.tensor
                def _(pe):
                    u0 = b * UNITS

                    def unit(c, j, static=None):
                        w = P if static is None or static < NQ else LAST
                        t, h, k = j // (G0 * NKU), j // NKU % G0, j % NKU
                        if static != 0 or j >= RING:
                            pe.wait_ge(mu_free, u0 + c * NU + (j - RING + 1))
                        if static != 0 and j < RING:
                            pe.wait_ge(rows_ready, b * nchunk + c)
                        q = Qs[0:ROWS, h, bass.ds(c * QC + t * P, w)] if static is None else Qs[0:ROWS, h, c * QC + t * P:c * QC + t * P + w]
                        for half in range(KU):
                            c0 = (k * KU + half) * KC
                            last = pe.matmul(pb[0:w, 5 + j % RING * KU + half, 0:KC], q, Ks[0:ROWS, h, c0:c0 + KC],
                                             start=True, stop=True)
                        last.then_inc(mu_full, 1)

                    def rows(c, tiles, w):
                        pe.wait_ge(n_ready, b * nchunk + c + 1)
                        for h in range(G0):
                            for t in range(tiles):
                                col = h * tiles * w + t * w
                                last = pe.matmul(top[M0:M0 + 3, col:col + w],
                                                 nsp[0:w, t * G0 + h, :], identh[0:w, 0:w], start=True, stop=True)
                        last.then_inc(rows_full, 1)

                    def scores(c, s, pair, w, whole):
                        m = P if s < NT - 1 else LAST
                        g = b * nchunk * STEPS + c * STEPS + s
                        if s:
                            pe.wait_ge(p_full, g * 2 + pair - 1)
                        for h in (2 * pair, 2 * pair + 1):
                            c0 = c * QC
                            q = Qs[0:M0 + 3, h, bass.ds(c0, w)] if whole is None else Qs[0:M0 + 3, h, c0:c0 + w]
                            last = pe.matmul(pb[0:m, h, 0:w], Ks[0:M0 + 3, h, s * P:s * P + m], q, start=True, stop=True)
                        last.then_inc(s_full, 1)

                    def product(c, s, w):
                        m = P if s < NT - 1 else LAST
                        g = b * nchunk * STEPS + c * STEPS + s
                        pe.wait_ge(p_full, 2 * g + 2)
                        if s == 0:
                            pe.wait_ge(o_read, b * nchunk + c + 1)
                        for h in range(G0):
                            last = pe.matmul(pb[32 * h:32 * h + 32, 4, 0:w], V[0:m, s, h, :], prob[0:m, s % 2, h, 0:w],
                                             start=(s == 0), stop=(s == NT - 1), tile_position=(0, 32 * h))
                        last.then_inc(pv_done, 1)

                    def both(c, w, static, ahead, n, tiles, lanes):
                        pe.wait_ge(rows_ready, b * nchunk + c + 1)
                        for s in range(STEPS):
                            units = iter(range(min(s, MSTEPS) * n // MSTEPS, min(s + 1, MSTEPS) * n // MSTEPS))
                            scores(c, s, 0, w, static)
                            for j in units:
                                unit(c + 1, j, ahead)
                                break
                            scores(c, s, 1, w, static)
                            for j in units:
                                unit(c + 1, j, ahead)
                                break
                            if s:
                                product(c, s - 1, w)
                            for j in units:
                                unit(c + 1, j, ahead)
                        if n:
                            rows(c + 1, tiles, lanes)
                        product(c, STEPS - 1, w)

                    for j in range(NU):
                        unit(0, j, 0)
                    rows(0, 3, P)
                    with pe.Fori(0, NQ - 1) as c:
                        both(c, QC, None, None, NU, 3, P)
                    both(NQ - 1, QC, NQ - 1, NQ, G0 * NKU, 1, LAST)
                    both(NQ, LAST, NQ, None, 0, 0, 0)

                @block.vector
                def _(dve):
                    def maxima(c, tiles, w):
                        for j in range(tiles * G0 * NKU):
                            r = 5 + j % RING * KU
                            dve.wait_ge(mu_full, b * UNITS + c * NU + j + 1)
                            dve.tensor_reduce(mx[0:w, j // NKU, j % NKU:j % NKU + 1], pb[0:w, r:r + KU, 0:KC],
                                              AX.XY, ALU.max, negate=True).then_inc(mu_free, 1)
                        n = tiles * G0
                        dve.wait_ge(mu_free, b * UNITS + c * NU + tiles * G0 * NKU)
                        own = Chain(dve, dve_own[1], b * nchunk + c, 5)
                        own.link(dve.tensor_reduce(nm[0:w, 0, 0:n], mx[0:w, 0:n, :], AX.X, ALU.min))
                        own.link(dve.tensor_copy(nsp[0:w, 0:n, 0], nm[0:w, 0, 0:n]))
                        own.link(dve.tensor_tensor(nm[0:w, 1, 0:n], nm[0:w, 0, 0:n], nsp[0:w, 0:n, 0], ALU.subtract))
                        own.link(dve.tensor_copy(nsp[0:w, 0:n, 1], nm[0:w, 1, 0:n]))
                        own.link(dve.tensor_tensor(nm[0:w, 0, 0:n], nm[0:w, 1, 0:n], nsp[0:w, 0:n, 1], ALU.subtract))
                        dve.tensor_copy(nsp[0:w, 0:n, 2], nm[0:w, 0, 0:n]).then_inc(n_ready, 1)
                        own.end()
                        dve.wait_ge(rows_full, b * nchunk + c + 1)
                        cols = tiles * w
                        dve.tensor_copy(Qs[M0:M0 + 3, :, bass.ds(c * QC, cols)],
                                        top[M0:M0 + 3, 0:G0 * cols].rearrange("p (h n) -> p h n", h=G0)).then_inc(rows_ready, 1)

                    with dve.Fori(0, NQ) as c:
                        maxima(c, 3, P)
                    maxima(NQ, 1, LAST)

                @block.scalar
                def _(act):
                    def exps(c, w):
                        for s in range(STEPS):
                            m = P if s < NT - 1 else LAST
                            g = b * nchunk * STEPS + c * STEPS + s
                            if s == 0:
                                act.wait_ge(pv_done, g + 1)
                            elif s > 1:
                                act.wait_ge(pv_done, g)
                            for pair in range(2):
                                act.wait_ge(s_full, g * 2 + pair + 1)
                                act.activation(prob[0:m, s % 2, 2 * pair:2 * pair + 2, 0:w],
                                               pb[0:m, 2 * pair:2 * pair + 2, 0:w],
                                               ACT.Exp).then_inc(p_full, 1)
                        act.wait_ge(pv_done, b * nchunk * STEPS + c * STEPS + STEPS + 1)
                        act.activation(O[:, bass.ds(c * QC, w)], pb[:, 4, 0:w], ACT.Copy).then_inc(o_read, 1)

                    with act.Fori(0, NQ) as c:
                        exps(c, QC)
                    exps(NQ, LAST)

            with nc.Block() as block:
                @block.tensor
                def _(pe):
                    for g, (t0, t1) in enumerate(GROUPS):
                        if g >= 2:
                            pe.wait_ge(pr_read, b * len(GROUPS) + g - 1)
                        for t in range(t0, t1):
                            w = P if t < NT - 1 else LAST
                            last = pe.matmul(pb[0:w, g % 2 * 4 + t - t0, 0:G0 * C + G0], O[:, t * P:t * P + w], wp[:], start=True, stop=True)
                        last.then_inc(pr_done, 1)
                    turn_tensor(pe, xh, pb, ident, S, b * 3 + 1)

                @block.vector
                def _(dve):
                    own = Chain(dve, dve_own[2], b, 2 * len(GROUPS) + 9)
                    own.link(dve.tensor_tensor(H[:], H[:], bp[:].unsqueeze(1).to_broadcast([P, NT, C]), ALU.add))
                    for g, (t0, t1) in enumerate(GROUPS):
                        n, w, bank = t1 - t0, P if t1 < NT else LAST, g % 2 * 4
                        dve.wait_ge(pr_done, b * len(GROUPS) + g + 1)
                        own.link(dve.reciprocal(rz[0:w, 0:n, :], pb[0:w, bank:bank + n, G0 * C:G0 * C + G0]))
                        dve.tensor_tensor(oh[0:w, 0:n], pb[0:w, bank:bank + n, 0:G0 * C].rearrange("p t (h o) -> p t h o", h=G0),
                                          rz[0:w, 0:n, :].unsqueeze(3).to_broadcast([w, n, G0, C]), ALU.mult).then_inc(pr_read, 1)
                        dve.wait_ge(pr_read, b * len(GROUPS) + g + 1)
                        own.link(dve.tensor_reduce(sq[0:w, t0:t1, :], oh[0:w, 0:n].rearrange("p t h o -> p t o h"), AX.X, ALU.add))
                    own.link(dve.tensor_tensor(H[:, 0:NT - 1, :], H[:, 0:NT - 1, :], sq[:, 0:NT - 1, :], ALU.add))
                    own.link(dve.tensor_tensor(H[0:LAST, NT - 1, :], H[0:LAST, NT - 1, :], sq[0:LAST, NT - 1, :], ALU.add))
                    ln_vector(dve, own, H, xh, sq, stat, S, b * 3 + 1)
                    own.end()

                @block.scalar
                def _(act):
                    ln_scalar(act, stat, S, b * 3 + 1)
                    turn_scalar(act, xT, pb, S, b * 3 + 1)

            CHUNKS = [(c * QC, QC) for c in range(NQ)] + [(NQ * QC, P)]
            NC_ = len(CHUNKS)
            YB = (4, 5, 7)
            with nc.Block() as block:
                @block.tensor
                def _(pe):
                    for c, (c0, w) in enumerate(CHUNKS):
                        if c >= 3:
                            pe.wait_ge(rh_ready, b * len(CHUNKS) + c - 2)
                        pe.matmul(pb[0:32, YB[c % 3], 0:w], rw1[:], xT[:, c0:c0 + w], start=True, stop=True).then_inc(rh_done, 1)
                    pe.wait_ge(rh_ready, (b + 1) * len(CHUNKS))
                    for t in range(NT):
                        last = pe.matmul(pb[:, 6, t * E0:(t + 1) * E0], rh[:, t * P:(t + 1) * P], rw2[:], start=True, stop=True)
                    last.then_inc(lg_done, 1)

                    def ups(c):
                        c0, w = CHUNKS[c]
                        for k in range(3):
                            n = b * NC_ * 3 + c * 3 + k
                            if c or k >= 2:
                                pe.wait_ge(h1_ready, n - 1)
                            pe.matmul(pb[:, (c * 3 + k) % 2, 0:w], ew1[:, k, :], xT[:, c0:c0 + w], start=True, stop=True).then_inc(h1_done, 1)

                    def mids(c):
                        c0, w = CHUNKS[c]
                        for k in range(3):
                            n = b * NC_ * 3 + c * 3 + k
                            pe.wait_ge(h1_ready, n + 1)
                            if c or k >= 2:
                                pe.wait_ge(h2_ready, n - 1)
                            pe.matmul(pb[:, 2 + (c * 3 + k) % 2, 0:w], ew2[:, k, :], h1[:, k, 0:w], start=True, stop=True).then_inc(h2_done, 1)

                    def downs(c):
                        c0, w = CHUNKS[c]
                        pe.wait_ge(h2_ready, b * NC_ * 3 + c * 3 + 3)
                        for t in range(w // P):
                            n = c * 3 + t
                            if n >= 3:
                                pe.wait_ge(ye_read, b * NT + n - 2)
                            dst = pb[:, YB[n % 3], 0:3 * P]
                            pe.matmul(dst, ones3[:], eb33[:], start=True, stop=False)
                            for k in range(3):
                                last = pe.matmul(dst[:, k * P:(k + 1) * P], h2[:, c % 2, k, t * P:(t + 1) * P], ew3[:, k, :],
                                                 start=False, stop=(k == 2))
                            last.then_inc(ye_done, 1)

                    for c in range(NC_):
                        ups(c)
                        mids(c)
                        if c:
                            downs(c - 1)
                    downs(NC_ - 1)

                @block.vector
                def _(dve):
                    own = Chain(dve, dve_own[3], b, 24)
                    wide = lambda a: a.unsqueeze(2).to_broadcast([P, NT, E0])
                    tt = lambda o, a, c, op: own.link(dve.tensor_tensor(o, a, c, op))
                    dve.wait_ge(lg_done, b + 1)
                    lg = pb[:, 6, 0:NT * E0].rearrange("p (t e) -> p t e", e=E0)
                    own.link(dve.tensor_reduce(rs[:, 0], lg, AX.X, ALU.max))
                    dve.tensor_tensor(rt[:, 0], lg, wide(rs[:, 0]), ALU.subtract).then_inc(lg_ready, 1)
                    dve.wait_ge(lg_exp, b + 1)
                    own.link(dve.tensor_reduce(rs[:, 0], rt[:, 0], AX.X, ALU.add))
                    own.link(dve.reciprocal(rs[:, 1], rs[:, 0]))
                    tt(rt[:, 0], rt[:, 0], wide(rs[:, 1]), ALU.mult)
                    for k in range(2):
                        own.link(dve.tensor_reduce(rs[:, k], rt[:, 0], AX.X, ALU.max))
                        tt(rt[:, 1], rt[:, 0], wide(rs[:, k]), ALU.is_equal)
                        own.link(dve.tensor_scalar(rt[:, 2], iota[:], float(E0), None, ALU.subtract))
                        tt(rt[:, 3], rt[:, 1], rt[:, 2], ALU.mult)
                        own.link(dve.tensor_reduce(rs[:, 2], rt[:, 3], AX.X, ALU.min))
                        tt(rt[:, 4 + k], rt[:, 2], wide(rs[:, 2]), ALU.is_equal)
                        if k == 0:
                            own.link(dve.tensor_scalar(rt[:, 6], rt[:, 4], 2.0, None, ALU.mult))
                            tt(rt[:, 0], rt[:, 0], rt[:, 6], ALU.subtract)
                    dve.tensor_tensor(rs[:, 2], rs[:, 1], rs[:, 0], ALU.subtract).then_inc(two_ready, 1)
                    dve.wait_ge(two_exp, b + 1)
                    own.link(dve.tensor_scalar(rs[:, 0], rs[:, 3], 1.0, None, ALU.add))
                    own.link(dve.reciprocal(rs[:, 1], rs[:, 0]))
                    tt(rs[:, 2], rs[:, 1], rs[:, 3], ALU.mult)
                    tt(rt[:, 4], rt[:, 4], wide(rs[:, 1]), ALU.mult)
                    tt(rt[:, 5], rt[:, 5], wide(rs[:, 2]), ALU.mult)
                    own.link(dve.tensor_tensor(W[:], rt[:, 4], rt[:, 5], ALU.add))
                    own.end()
                    own = Chain(dve, dve_own[4], b, 7)
                    weigh(dve, b, lambda t: pb[:, YB[t % 3], 0:3 * P].rearrange("p (e c) -> p e c", e=E0), lambda t: W[:, t, :],
                          sq, yw, ye_done, ye_read, ye_summed)
                    own.link(dve.tensor_tensor(H[:], H[:], sq[:], ALU.add))
                    ln_vector(dve, own, H, xh, sq, stat, S, b * 3 + 2)
                    own.end()

                @block.scalar
                def _(act):
                    for c, (c0, w) in enumerate(CHUNKS):
                        act.wait_ge(rh_done, b * len(CHUNKS) + c + 1)
                        act.activation(rh[0:32, c0:c0 + w], pb[0:32, YB[c % 3], 0:w], ACT.Relu).then_inc(rh_ready, 1)
                    for c, (c0, w) in enumerate(CHUNKS):
                        if c == 1:
                            act.wait_ge(lg_ready, b + 1)
                            act.activation(rt[:, 0], rt[:, 0], ACT.Exp).then_inc(lg_exp, 1)
                        if c == 2:
                            act.wait_ge(two_ready, b + 1)
                            act.activation(rs[:, 3], rs[:, 2], ACT.Exp).then_inc(two_exp, 1)
                        for k in range(3):
                            n = b * NC_ * 3 + c * 3 + k
                            act.wait_ge(h1_done, n + 1)
                            if c:
                                act.wait_ge(h2_done, n - 2)
                            act.activation(h1[:, k, 0:w], pb[:, (c * 3 + k) % 2, 0:w], ACT.Relu).then_inc(h1_ready, 1)
                        for k in range(3):
                            n = b * NC_ * 3 + c * 3 + k
                            act.wait_ge(h2_done, n + 1)
                            if c >= 2:
                                act.wait_ge(ye_done, b * NT + (c - 1) * 3)
                            act.activation(h2[:, c % 2, k, 0:w], pb[:, 2 + (c * 3 + k) % 2, 0:w], ACT.Relu, bias=eb2[:, k:k + 1]).then_inc(h2_ready, 1)
                    ln_scalar(act, stat, S, b * 3 + 2)

            with nc.Block() as block:
                @block.tensor
                def _(pe):
                    turn_tensor(pe, xh, pb, ident, S, b * 3 + 2)

                @block.sync
                def _(sp):
                    sp.dma_start(h_tm[bass.ds(b * N, (NT - 1) * P), :].rearrange("(t p) c -> p t c", p=P), H[:, 0:NT - 1, :]).then_inc(stored, 16)
                    sp.dma_start(h_tm[bass.ds(b * N + (NT - 1) * P, LAST), :], H[0:LAST, NT - 1, :]).then_inc(stored, 16)
                    sp.wait_ge(S["xT"], (b * 3 + 3) * len(GROUPS))
                    sp.sem_inc(S["sp_passed"])
                    sp.dma_start(x_cm[:, bass.ds(b * N, N)], xT[0:C, 0:N]).then_inc(stored, 16)
                    sp.wait_ge(stored, (b + 1) * 48)
                    sp.sem_inc(S["sp_passed"])

                @block.scalar
                def _(act):
                    turn_scalar(act, xT, pb, S, b * 3 + 2)


H1 = 8
NI = N // 3
PI = NI // 8
UC = 2 * KC
UT = N // UC
UH = NT * UT
RC = 4


def phase_c(nc, io, x_cm, nmx_all, es_all, diag_all):
    with ExitStack() as ctx:
        sb = lambda n, s, d=F32: ctx.enter_context(nc.sbuf_tensor("c_" + n, s, d))
        sem = lambda n: ctx.enter_context(nc.semaphore("c_s_" + n))
        xqk = sb("xqk", [C + 1, 2, 2, NI])
        wh = sb("wh", [C + 1, 2, 3, C])
        scale = sb("scale", [P, 1])
        ones = sb("ones", [C, 1])
        y = sb("y", [P, N])
        kd = sb("kd", [C, N])
        prod = sb("prod", [C, N])
        stack = sb("stack", [P, 2, 3, N], F32R)
        nmx = sb("nmx", [P, 2, NT, UT])
        es = sb("es", [P, 2, NT, UT])
        diag = sb("diag", [P, 2, NT])
        pb = ctx.enter_context(nc.psum_tensor("c_ps", [P, 8, 512], F32))
        set_up = sem("set_up")
        x_in = sem("x_in")
        w_in = sem("w_in")
        pj_full = sem("pj_full")
        y_ready = sem("y_ready")
        part_ready = sem("part_ready")
        sub_done = sem("sub_done")
        kd_in = sem("kd_in")
        prod_ready = sem("prod_ready")
        k_stacked = sem("k_stacked")
        stacked = sem("stacked")
        dg_full = sem("dg_full")
        dg_read = sem("dg_read")
        s_full = sem("s_full")
        max_done = sem("max_done")
        exp_done = sem("exp_done")
        results = sem("results")
        passed = {e: sem("passed_" + e) for e in ("sp", "pe", "dve", "act", "pool")}
        HEADS = NB * H1
        DIAG = [(d * NT // 8, (d + 1) * NT // 8) for d in range(8)]
        T0 = 8
        ITEMS = []
        for t in range(NT):
            for u in range(UT):
                ITEMS.append(("unit", t * UT + u))
                if u == 1 and t < 8:
                    ITEMS.append(("diagonal", t))
                if u == 1 and T0 <= t < T0 + 8:
                    ITEMS.append(("chunk", t - T0))

        def bodies(eng, front, main):
            front(0, 0)
            main(0, 0, lambda part: front(1, 1, part))
            main(1, 1, lambda part: front(2, 0, part))
            with eng.Fori(2, HEADS - 2, 2) as G:
                main(G, 0, lambda part: front(G + 1, 1, part))
                main(G + 1, 1, lambda part: front(G + 2, 0, part))
            main(HEADS - 2, 0, lambda part: front(HEADS - 1, 1, part))
            main(HEADS - 1, 1, None)

        with nc.Block() as block:
            @block.sync
            def _(sp):
                sp.dma_start(scale[:], io["scale1"]).then_inc(set_up, 16)
                sp.wait_ge(set_up, 16)

            @block.vector
            def _(dve):
                dve.memset(xqk[C:C + 1, :, :, :], 1.0)
                dve.memset(ones[:], 1.0)
                dve.memset(nmx[:], 0.0)
                dve.memset(es[:], 1.0)
                dve.memset(diag[:], 0.0)

        with nc.Block() as block:
            @block.sync
            def _(sp):
                def front(G, buf, part=None):
                    if part in (None, 0):
                        if not (isinstance(G, int) and G < 2):
                            sp.wait_ge(y_ready, (G - 1) * 8)
                        for s in range(2):
                            sp.dma_start(xqk[0:C, buf, s, :], x_cm[:, bass.ds((G // H1) * NI + s * NB * NI, NI)]).then_inc(x_in, 16)
                        sp.dma_start(wh[:, buf, :, :], io["w_qk"][bass.ds(G % H1, 1)].rearrange("o c j d -> (o c) j d")).then_inc(w_in, 16)
                    if part in (None, 1):
                        sp.wait_ge(prod_ready, G)
                        sp.wait_ge(y_ready, (G + 1) * 8)
                        sp.dma_start(kd[:], y[C:P, :]).then_inc(kd_in, 16)
                        sp.wait_ge(sub_done, G + 1)
                        for p in range(2):
                            sp.dma_start(stack[p * C:(p + 1) * C, buf, 2, :].bitcast(F32), stack[C:P, buf, p, :].bitcast(F32)).then_inc(k_stacked, 16)
                        sp.wait_ge(k_stacked, (G + 1) * 32)
                        for p in range(2):
                            sp.dma_start(stack[C:P, buf, p, :].bitcast(F32), stack[0:C, buf, p, :].bitcast(F32)).then_inc(stacked, 16)

                def main(G, buf, nxt):
                    if nxt:
                        nxt(0)
                        nxt(1)
                    sp.wait_ge(exp_done, (G + 1) * UH)
                    sp.sem_inc(passed["sp"])
                    sp.wait_ge(dg_read, (G + 1) * 8)
                    for src, dst in ((nmx[:, buf].rearrange("p t u -> p (t u)"), nmx_all), (es[:, buf].rearrange("p t u -> p (t u)"), es_all),
                                     (diag[:, buf], diag_all)):
                        sp.dma_start(dst[:, bass.ds(G, 1), :].rearrange("p g n -> p (g n)"), src).then_inc(results, 16)

                bodies(sp, front, main)
                sp.wait_ge(results, HEADS * 48)

            @block.tensor
            def _(pe):
                pe.wait_ge(set_up, 16)

                def chunk(G, buf, c, bank):
                    if c == 0:
                        pe.wait_ge(x_in, (G + 1) * 32)
                        pe.wait_ge(w_in, (G + 1) * 16)
                    for s in range(2):
                        for j in range(3):
                            last = pe.matmul(pb[s * C:(s + 1) * C, bank, j * PI:(j + 1) * PI], wh[:, buf, j, :],
                                             xqk[:, buf, s, c * PI:(c + 1) * PI], start=True, stop=True)
                    last.then_inc(pj_full, 1)

                def front(G, buf, part=None):
                    if part is None:
                        for c in range(8):
                            if c >= 2:
                                pe.wait_ge(y_ready, c - 1)
                            chunk(G, buf, c, c % 2)
                    else:
                        chunk(G, buf, *part)

                def diagonal(G, d, bank):
                    if d == 0:
                        pe.wait_ge(prod_ready, G + 1)
                    for t in range(*DIAG[d]):
                        w = P if t < NT - 1 else LAST
                        last = pe.matmul(pb[0:w, bank, t - DIAG[d][0]:t - DIAG[d][0] + 1], prod[:, t * P:t * P + w], ones[:], start=True, stop=True)
                    last.then_inc(dg_full, 1)

                def unit(buf, j, r):
                    t, u = divmod(j, UT)
                    w = P if t < NT - 1 else LAST
                    for q in range(2):
                        for half in range(2):
                            c0 = u * UC + half * KC
                            last = pe.matmul(pb[0:w, r + half, 0:KC], stack[:, buf, 2, t * P:t * P + w],
                                             stack[:, buf, q, c0:c0 + KC], start=(q == 0), stop=(q == 1))
                    last.then_inc(s_full, 1)

                def await_read(G, item):
                    kind, n = item
                    if kind == "unit":
                        pe.wait_ge(exp_done, G * UH + n + 1)
                    elif kind == "diagonal":
                        pe.wait_ge(dg_read, G * 8 + n + 1)
                    else:
                        pe.wait_ge(y_ready, (G + 1) * 8 + n + 1)

                def main(G, buf, nxt):
                    pe.wait_ge(stacked, (G + 1) * 32)
                    present = lambda i: nxt or ITEMS[i][0] != "chunk"
                    for i, (kind, n) in enumerate(ITEMS):
                        if not present(i):
                            continue
                        before = [k for k in range(i % RC, i, RC) if present(k)]
                        if before:
                            await_read(G, ITEMS[before[-1]])
                        elif not (isinstance(G, int) and G == 0):
                            await_read(G - 1, ITEMS[max(k for k in range(i % RC, len(ITEMS), RC))])
                        r = i % RC * 2
                        if kind == "unit":
                            unit(buf, n, r)
                        elif kind == "diagonal":
                            diagonal(G, n, r)
                        else:
                            nxt((n, r))

                bodies(pe, front, main)

            @block.vector
            def _(dve):
                def main(G, buf, nxt):
                    if not (isinstance(G, int) and G < 2):
                        dve.wait_ge(results, (G - 1) * 48)
                    for i, (kind, n) in enumerate(ITEMS):
                        r = i % RC * 2
                        if kind == "unit":
                            t, u = divmod(n, UT)
                            w = P if t < NT - 1 else LAST
                            dve.wait_ge(s_full, G * UH + n + 1)
                            dve.tensor_reduce(nmx[0:w, buf, t, u:u + 1], pb[0:w, r:r + 2, 0:KC],
                                              AX.XY, ALU.max, negate=True).then_inc(max_done, 1)
                        elif kind == "diagonal":
                            t0, t1 = DIAG[n]
                            dve.wait_ge(dg_full, G * 8 + n + 1)
                            if t1 == NT:
                                dve.tensor_copy(diag[0:LAST, buf, NT - 1:NT], pb[0:LAST, r, t1 - 1 - t0:t1 - t0])
                                t1 -= 1
                            dve.tensor_copy(diag[:, buf, t0:t1], pb[:, r, 0:t1 - t0]).then_inc(dg_read, 1)

                bodies(dve, lambda G, buf, part=None: None, main)

            @block.gpsimd
            def _(pool):
                def front(G, buf, part=None):
                    pool.wait_ge(y_ready, (G + 1) * 8)
                    if not (isinstance(G, int) and G < 2):
                        pool.wait_ge(s_full, (G - 1) * UH)
                    pool.sem_inc(passed["pool"])
                    pool.tensor_copy(stack[:, buf, 0, :], y[:]).then_inc(part_ready, 1)
                    pool.wait_ge(part_ready, G + 1)
                    pool.tensor_tensor(stack[:, buf, 1, :], y[:], stack[:, buf, 0, :].bitcast(F32), ALU.subtract).then_inc(sub_done, 1)
                    pool.wait_ge(kd_in, (G + 1) * 16)
                    pool.wait_ge(dg_full, G * 8)
                    pool.tensor_tensor(prod[:], y[0:C, :], kd[:], ALU.mult).then_inc(prod_ready, 1)

                def main(G, buf, nxt):
                    if nxt:
                        nxt(0)

                bodies(pool, front, main)

            @block.scalar
            def _(act):
                def front(G, buf, part=None):
                    for c, bank in ([(c, c % 2) for c in range(8)] if part is None else (part,)):
                        if c == 0:
                            act.wait_ge(prod_ready, G)
                            act.wait_ge(kd_in, G * 16)
                        act.wait_ge(pj_full, G * 8 + c + 1)
                        act.activation(y[:].rearrange("p (j i) -> p j i", j=3)[:, :, c * PI:(c + 1) * PI],
                                       pb[:, bank, 0:KC].rearrange("p (j i) -> p j i", j=3), ACT.Copy,
                                       scale=scale[:, 0:1]).then_inc(y_ready, 1)

                def main(G, buf, nxt):
                    if not (isinstance(G, int) and G < 2):
                        act.wait_ge(results, (G - 1) * 48)
                    for i, (kind, n) in enumerate(ITEMS):
                        r = i % RC * 2
                        if kind == "unit":
                            t, u = divmod(n, UT)
                            w = P if t < NT - 1 else LAST
                            act.wait_ge(max_done, G * UH + n + 1)
                            block_of = pb[0:w, r:r + 2, 0:KC]
                            act.activation(block_of, block_of, ACT.Exp, bias=nmx[0:w, buf, t, u:u + 1],
                                           accum_out=es[0:w, buf, t, u:u + 1]).then_inc(exp_done, 1)
                        elif kind == "chunk" and nxt:
                            nxt((n, r))

                bodies(act, front, main)


E1 = 8


def segments():
    found = []
    for j in range(3):
        at, end = j * NI, (j + 1) * NI
        while at < end:
            t, p = divmod(at, P)
            if p == 0 and end - at >= P:
                n = (end - at) // P
                found.append((t, t + n, 0, P, j, at - j * NI))
                at += n * P
            else:
                n = min(end - at, P - p)
                if p and p + n > 64 > p:
                    n = 64 - p
                found.append((t, t + 1, p, p + n, j, at - j * NI))
                at += n
    return found


def phase_d(nc, io, x_cm, h_tm, nmx_all, es_all, diag_all, out):
    with ExitStack() as ctx:
        sb = lambda n, s, d=F32: ctx.enter_context(nc.sbuf_tensor("d_" + n, s, d))
        sem = lambda n: ctx.enter_context(nc.semaphore("d_s_" + n))
        HEADS = NB * H1
        SEG = segments()
        a_all = sb("a_all", [P, HEADS, NT])
        m_all = sb("m_all", [P, HEADS, NT])
        ab = sb("ab", [P, H1, NT])
        xv = sb("xv", [C + 1, NI])
        wvT = sb("wvT", [C, 3, H1, C + 1])
        w0 = sb("w0", [C, H1, C])
        wv = sb("wv", [C + 1, 3, H1, C])
        b0 = sb("b0", [P, C])
        ident = sb("ident", [P, P])
        parts = sb("parts", [1, 3, E1 * C], BF16)
        xT = sb("xT", [C + 1, NP])
        H = sb("H", [P, NT, C])
        xh = sb("xh", [P, NT, C])
        sq = sb("sq", [P, NT, C])
        stat = sb("stat", [P, 4, NT])
        w1 = sb("w1", [C + 1, 2, P])
        wg = sb("wg", [P, 2, E1])
        bg = sb("bg", [E1, 1])
        gT = sb("gT", [E1, NP])
        wd = sb("wd", [P, 2, E1 * C])
        bd = sb("bd", [1, E1 * C])
        bd3 = sb("bd3", [3, E1 * C], BF16)
        ones3 = sb("ones3", [3, P], BF16)
        iota = sb("iota", [P, NT, E1])
        hg = sb("hg", [P, 2, NP])
        rt = sb("rt", [P, 3, NT, E1])
        rs = sb("rs", [P, 2, NT])
        yw = sb("yw", [P, 3, E1, C])
        pb = ctx.enter_context(nc.psum_tensor("d_ps", [P, 8, 512], F32))
        loaded = sem("loaded")
        dve_own = [sem(f"dve_own{i}") for i in range(4)]
        s_low = sem("s_low")
        s_exp = sem("s_exp")
        d_low = sem("d_low")
        d_exp = sem("d_exp")
        h_in = sem("h_in")
        v_done = sem("v_done")
        av_ready = sem("av_ready")
        av_summed = sem("av_summed")
        w_full = sem("w_full")
        b_split = {n: sem("b_" + n) for n in ("own", "in")}
        S = {n: sem(n) for n in ("var", "std", "xh", "turned", "xT", "passed", "sp_passed")}
        hg_done = sem("hg_done")
        hg_ready = sem("hg_ready")
        gt_done = sem("gt_done")
        gt_ready = sem("gt_ready")
        lg_done = sem("lg_done")
        lg_ready = sem("lg_ready")
        lg_exp = sem("lg_exp")
        ye_done = sem("ye_done")
        ye_read = sem("ye_read")
        ye_summed = sem("ye_summed")
        stored = sem("stored")

        with nc.Block() as block:
            @block.sync
            def _(sp):
                loads = ((wvT, "wv1T"), (w0, "w0"), (b0, "b0"), (ident, "ident"), (w1, "w1"), (wg, "wg"), (bg, "bg"),
                         (wd, "wd"), (bd, "bd"), (iota, "iota8"))
                for t, k in loads:
                    sp.dma_start(t[:], io[k]).then_inc(loaded, 16)
                sp.wait_ge(loaded, 16 * len(loads))
                stack_parts(sp, b_split, parts, bd3)

            @block.tensor
            def _(pe):
                pe.wait_ge(loaded, 16 * 10)
                for j in range(3):
                    for h in range(H1):
                        last = pe.matmul(pb[0:C + 1, j, h * C:(h + 1) * C], wvT[:, j, h, :], w0[:, h, :], start=True, stop=True)
                last.then_inc(w_full, 1)

            @block.gpsimd
            def _(pool):
                pool.memset(xv[C:C + 1, :], 1.0)
                pool.memset(ones3[:], 1.0)
                pool.wait_ge(loaded, 16 * 10)
                split_row(pool, b_split, bd, parts)

            @block.vector
            def _(dve):
                dve.memset(xT[0:C, N:NP], 0.0)
                dve.memset(xT[C:C + 1, :], 1.0)
                dve.memset(H[:], 0.0)
                own = Chain(dve, dve_own[0], 0, 5)
                nmx = nmx_all[:].rearrange("p g (t u) -> p g t u", u=UT)
                es = es_all[:].rearrange("p g (t u) -> p g t u", u=UT)
                flat = lambda x: x[:].rearrange("p g n -> p (g n)")
                own.link(dve.tensor_reduce(m_all[:], nmx, AX.X, ALU.min))
                dve.tensor_tensor(nmx, m_all[:].unsqueeze(3).to_broadcast([P, HEADS, NT, UT]), nmx, ALU.subtract).then_inc(s_low, 1)
                own.link(dve.tensor_tensor(flat(diag_all), flat(diag_all), flat(m_all), ALU.add))
                dve.tensor_copy(flat(a_all), flat(diag_all)).then_inc(d_low, 1)
                dve.wait_ge(s_exp, 1)
                own.link(dve.tensor_tensor(flat(es_all), flat(es_all), flat(nmx_all), ALU.mult))
                own.link(dve.tensor_reduce(m_all[:], es, AX.X, ALU.add))
                own.link(dve.reciprocal(flat(m_all), flat(m_all)))
                dve.wait_ge(d_exp, 1)
                dve.tensor_tensor(flat(a_all), flat(a_all), flat(m_all), ALU.mult)
                own.end()

            @block.scalar
            def _(act):
                act.wait_ge(s_low, 1)
                act.activation(nmx_all[:], nmx_all[:], ACT.Exp).then_inc(s_exp, 1)
                act.wait_ge(d_low, 1)
                act.activation(a_all[:], a_all[:], ACT.Exp).then_inc(d_exp, 1)
                act.wait_ge(w_full, 1)
                act.activation(wv[:].rearrange("c j h o -> c j (h o)"), pb[0:C + 1, 0:3, :], ACT.Copy)

        with nc.Fori(0, NB) as b:
            RV = 4
            with nc.Block() as block:
                nload = 1 + len(SEG)

                @block.sync
                def _(sp):
                    sp.dma_start(xv[0:C, :], x_cm[:, bass.ds((b + 2 * NB) * NI, NI)]).then_inc(h_in, 16)
                    rows = h_tm.rearrange("(m q) c -> q m c", q=3)
                    for t0, t1, p0, p1, j, i0 in SEG:
                        n = (t1 - t0) * (p1 - p0)
                        sp.dma_start(H[p0:p1, t0:t1, :], rows[j, bass.ds(b * NI + i0, n), :].rearrange(
                            "(t p) c -> p t c", p=p1 - p0)).then_inc(h_in, 16)
                    sp.wait_ge(h_in, (b + 1) * 16 * nload)
                    sp.sem_inc(S["sp_passed"])


                @block.tensor
                def _(pe):
                    pe.wait_ge(h_in, (b + 1) * 16 * nload)

                    for t in range(NT):
                        if t >= RV:
                            pe.wait_ge(av_ready, b * NT + t - RV + 1)
                        for t0, t1, p0, p1, j, i0 in SEG:
                            if t0 <= t < t1:
                                i = i0 + (t - t0) * P
                                last = pe.matmul(pb[p0:p1, t % RV, :], xv[:, i:i + p1 - p0],
                                                 wv[:, j, :, :].rearrange("c h o -> c (h o)"), start=True, stop=True)
                        last.then_inc(v_done, 1)
                    turn_tensor(pe, xh, pb, ident, S, b)

                @block.vector
                def _(dve):
                    own = Chain(dve, dve_own[1], b, 9)
                    dve.wait_ge(h_in, (b + 1) * 16 * nload)
                    own.link(dve.tensor_copy(ab[:], a_all[:, bass.ds(b * H1, H1), :]))
                    own.link(dve.tensor_tensor(H[:], H[:], b0[:].unsqueeze(1).to_broadcast([P, NT, C]), ALU.add))
                    weigh(dve, b, lambda t: pb[:, t % RV, :].rearrange("p (h o) -> p h o", h=H1), lambda t: ab[:, :, t],
                          xh, yw, v_done, av_ready, av_summed, LAST)
                    dve.tensor_tensor(H[:, 0:NT - 1, :], H[:, 0:NT - 1, :], xh[:, 0:NT - 1, :], ALU.add)
                    own.link(dve.tensor_tensor(H[0:LAST, NT - 1, :], H[0:LAST, NT - 1, :], xh[0:LAST, NT - 1, :], ALU.add))
                    ln_vector(dve, own, H, xh, sq, stat, S, b)
                    own.end()

                @block.scalar
                def _(act):
                    ln_scalar(act, stat, S, b)
                    turn_scalar(act, xT, pb, S, b)

            CHUNKS = [(c * QC, QC) for c in range(NQ)] + [(NQ * QC, P)]
            ND = 2 * len(CHUNKS)
            GBANKS, YBANKS = (3, 5), (6, 7, 0, 1, 2, 3, 5)
            with nc.Block() as block:
                @block.tensor
                def _(pe):
                    def hidden(c):
                        c0, w = CHUNKS[c]
                        for k in range(2):
                            n = c * 2 + k
                            if n >= 3:
                                pe.wait_ge(hg_ready, b * ND + n - 2)
                            pe.matmul(pb[:, n % 3, 0:w], w1[:, k, :], xT[:, c0:c0 + w], start=True, stop=True).then_inc(hg_done, 1)

                    def gate(c):
                        c0, w = CHUNKS[c]
                        pe.wait_ge(hg_ready, b * ND + c * 2 + 2)
                        if c >= 2:
                            pe.wait_ge(gt_ready, b * len(CHUNKS) + c - 1)
                        for k in range(2):
                            last = pe.matmul(pb[0:E1, GBANKS[c % 2], 0:w], wg[:, k, :], hg[:, k, c0:c0 + w], start=(k == 0), stop=(k == 1))
                        last.then_inc(gt_done, 1)

                    hidden(0)
                    for c in range(1, len(CHUNKS)):
                        hidden(c)
                        gate(c - 1)
                    gate(len(CHUNKS) - 1)
                    pe.wait_ge(gt_ready, (b + 1) * len(CHUNKS))
                    pe.sem_inc(S["passed"])
                    for t in range(NT):
                        last = pe.transpose(pb[:, 4, t * E1:(t + 1) * E1], gT[:, t * P:(t + 1) * P], ident[0:E1, 0:E1])
                    last.then_inc(lg_done, 1)
                    for t in range(NT):
                        if t >= len(YBANKS):
                            pe.wait_ge(ye_read, b * NT + t - len(YBANKS) + 1)
                        dst = pb[:, YBANKS[t % len(YBANKS)], :]
                        pe.matmul(dst, ones3[:], bd3[:], start=True, stop=False)
                        for k in range(2):
                            last = pe.matmul(dst, hg[:, k, t * P:(t + 1) * P], wd[:, k, :], start=False, stop=(k == 1))
                        last.then_inc(ye_done, 1)

                @block.scalar
                def _(act):
                    def logits(c):
                        c0, w = CHUNKS[c]
                        act.wait_ge(gt_done, b * len(CHUNKS) + c + 1)
                        act.activation(gT[:, c0:c0 + w], pb[0:E1, GBANKS[c % 2], 0:w], ACT.Identity, bias=bg[:, 0:1]).then_inc(gt_ready, 1)

                    for c, (c0, w) in enumerate(CHUNKS):
                        for k in range(2):
                            n = c * 2 + k
                            act.wait_ge(hg_done, b * ND + n + 1)
                            act.activation(hg[:, k, c0:c0 + w], pb[:, n % 3, 0:w], ACT.Gelu).then_inc(hg_ready, 1)
                        if c:
                            logits(c - 1)
                    logits(len(CHUNKS) - 1)
                    act.wait_ge(lg_ready, b + 1)
                    act.activation(rt[:, 0], rt[:, 0], ACT.Exp).then_inc(lg_exp, 1)

                @block.vector
                def _(dve):
                    own = Chain(dve, dve_own[2], b, 10)
                    wide = lambda a: a.unsqueeze(2).to_broadcast([P, NT, E1])
                    tt = lambda o, a, c, op: own.link(dve.tensor_tensor(o, a, c, op))
                    dve.wait_ge(lg_done, b + 1)
                    lg = pb[:, 4, 0:NT * E1].rearrange("p (t e) -> p t e", e=E1)
                    own.link(dve.tensor_reduce(rs[:, 0], lg, AX.X, ALU.max))
                    dve.tensor_tensor(rt[:, 0], lg, wide(rs[:, 0]), ALU.subtract).then_inc(lg_ready, 1)
                    dve.wait_ge(lg_exp, b + 1)
                    own.link(dve.tensor_reduce(rs[:, 0], rt[:, 0], AX.X, ALU.add))
                    own.link(dve.reciprocal(rs[:, 1], rs[:, 0]))
                    tt(rt[:, 0], rt[:, 0], wide(rs[:, 1]), ALU.mult)
                    own.link(dve.tensor_reduce(rs[:, 0], rt[:, 0], AX.X, ALU.max))
                    tt(rt[:, 1], rt[:, 0], wide(rs[:, 0]), ALU.is_equal)
                    tt(rt[:, 2], rt[:, 1], iota[:], ALU.mult)
                    own.link(dve.tensor_reduce(rs[:, 1], rt[:, 2], AX.X, ALU.min))
                    tt(rt[:, 1], iota[:], wide(rs[:, 1]), ALU.is_equal)
                    tt(rt[:, 0], rt[:, 0], rt[:, 1], ALU.mult)
                    weigh(dve, b, lambda t: pb[:, YBANKS[t % len(YBANKS)], :].rearrange("p (e c) -> p e c", e=E1), lambda t: rt[:, 0, t, :],
                          xh, yw, ye_done, ye_read, ye_summed)
                    dve.tensor_tensor(H[:], H[:], xh[:], ALU.add)
                    own.end()

            with nc.Block() as block:
                @block.sync
                def _(sp):
                    rows = out.rearrange("b (i j) c -> (b i) j c", j=3)
                    for t0, t1, p0, p1, j, i0 in SEG:
                        n = (t1 - t0) * (p1 - p0)
                        sp.dma_start(rows[bass.ds(b * NI + i0, n), j, :].rearrange("(t p) c -> p t c", p=p1 - p0),
                                     H[p0:p1, t0:t1, :]).then_inc(stored, 16)
                    sp.wait_ge(stored, (b + 1) * 16 * len(SEG))
                    sp.sem_inc(S["sp_passed"])


def build(nc, out, **io):
    with ExitStack() as ctx:
        h_cm = nc.dram_tensor("h_cm", [C, NB * N], F32, kind="Internal").ap()
        x_cm = nc.dram_tensor("x_cm", [C, NB * N], F32, kind="Internal").ap()
        h_tm = nc.dram_tensor("h_tm", [NB * N, C], F32, kind="Internal").ap()
        phase_a(nc, io, h_cm)
        phase_b(nc, io, h_cm, x_cm, h_tm)
        nmx_all = ctx.enter_context(nc.sbuf_tensor("nmx_all", [P, NB * H1, UH], F32))
        es_all = ctx.enter_context(nc.sbuf_tensor("es_all", [P, NB * H1, UH], F32))
        diag_all = ctx.enter_context(nc.sbuf_tensor("diag_all", [P, NB * H1, NT], F32))
        phase_c(nc, io, x_cm, nmx_all, es_all, diag_all)
        phase_d(nc, io, x_cm, h_tm, nmx_all, es_all, diag_all, out)


def layout(a):
    import numpy as np

    d = {}
    half = lambda w: np.tile(w, (2, 1))
    with_bias = lambda w, b: np.concatenate([w, b[None]], 0)
    d["x"], d["txt"] = a["x"], a["txt"].transpose(2, 0, 1)
    d["tok_w1"] = np.tile(a["L0_tok_w1"].reshape(C, 3, C).transpose(2, 1, 0), (1, 1, 2))
    d["tok_b1"] = half(a["L0_tok_b1"].reshape(C, 3))
    d["tok_w2"] = half(a["L0_tok_w2"].T.reshape(NH, C // NH, C).transpose(1, 0, 2).reshape(C, C))
    d["tok_b2"] = half(a["L0_tok_b2"].reshape(C, 1))
    d["pos"] = a["L0_tok_pos_emb"].reshape(1, 2 * WS - 1, 2 * WS - 1)
    lane = np.arange(P)
    d["head_mask"] = (lane[:, None] % NH == np.arange(NH)).astype(np.float32)
    d["ident"] = np.eye(P, dtype=np.float32)
    token = np.arange(WT)
    row = (token[:, None] >= WT // 2) != (token[None] >= WT // 2)
    col = row.reshape(WS, WS, WS, WS).transpose(1, 0, 3, 2).reshape(WT, WT)
    unmet = np.zeros((4, 2, WT, WR, 2, WT), np.float32)
    unmet[:, :, :, WR - 1] += np.where(row, np.float32(MASKED), np.float32(0))[None, None, :, None]
    unmet[(HW - 1) % 4, 1, :, :, (HW - 1) // 4] += np.where(col, np.float32(MASKED), np.float32(0))[:, None]
    d["masks"] = unmet.reshape(P, WR, 2, WT)
    wq, bq = a["L0_attn_W_qkv"], a["L0_attn_b_qkv"]
    d["wqk"] = with_bias(wq[:2 * C].T, bq[:2 * C])
    d["wv"] = with_bias(wq[2 * C:].T, bq[2 * C:])
    d["scale"] = np.where(lane[:, None] < C, D0 ** -0.5, 1.0).astype(np.float32)
    d["scale1"] = np.where(lane[:, None] < C, C ** -0.5, 1.0).astype(np.float32)
    wp = np.zeros((G0, 32, G0 * C + G0), np.float32)
    for h in range(G0):
        wp[h, :D0, h * C:(h + 1) * C] = a["L0_attn_W_proj"].T.reshape(G0, D0, C)[h]
        wp[h, D0, G0 * C + h] = 1
    d["wp"], d["bp"] = wp.reshape(P, G0 * C + G0), np.broadcast_to(a["L0_attn_b_proj"], (P, C))
    d["rw1"] = with_bias(a["L0_ffn_router_w1"], a["L0_ffn_router_b1"])
    d["rw2"] = with_bias(a["L0_ffn_router_w2"], a["L0_ffn_router_b2"])
    w = a["L0_ffn_expert_w1"].reshape(3, 2, C, C).transpose(2, 0, 1, 3).reshape(C, 3, P)
    d["ew1"] = np.concatenate([w, a["L0_ffn_expert_b1"].reshape(1, 3, P)], 0)
    for k, n in (("ew2", "L0_ffn_expert_w2"), ("ew3", "L0_ffn_expert_w3")):
        z = np.zeros((2, C, 3, 2, C), np.float32)
        for e in range(2):
            z[e, :, :, e, :] = a[n].reshape(3, 2, C, C)[:, e].transpose(1, 0, 2)
        d[k] = z.reshape(P, 3, P)
    d["eb2"] = a["L0_ffn_expert_b2"].reshape(3, P).T
    d["eb3"] = a["L0_ffn_expert_b3"].reshape(1, 3 * P)
    d["iota"] = np.broadcast_to(np.arange(E0, dtype=np.float32), (P, NT, E0))
    d["iota8"] = np.broadcast_to(np.arange(E1, dtype=np.float32) - E1, (P, NT, E1))
    w = np.concatenate([a["L1_attn_Wqkv"], a["L1_attn_bqkv"][None]], 0)
    d["w_qk"] = w.reshape(C + 1, 3, C, H1).transpose(3, 0, 1, 2)
    d["wv1T"] = w.reshape(C + 1, 3, C, H1).transpose(2, 1, 3, 0)
    d["w0"] = a["L1_attn_W0"].reshape(C, H1, C)
    d["b0"] = np.broadcast_to(a["L1_attn_b0"], (P, C))
    d["w1"] = with_bias(a["L1_ffn_W1"], a["L1_ffn_b1"]).reshape(C + 1, 2, P)
    d["wg"] = a["L1_ffn_Wg"].reshape(2, P, E1).transpose(1, 0, 2)
    d["bg"] = a["L1_ffn_bg"][:, None]
    d["wd"] = a["L1_ffn_Wd"].transpose(1, 0, 2).reshape(2, P, E1 * C).transpose(1, 0, 2)
    d["bd"] = a["L1_ffn_bd"].reshape(1, E1 * C)
    return {k: np.ascontiguousarray(v) for k, v in d.items()}


def kernel(**inputs):
    import numpy as _np
    import concourse.bacc as _bacc
    from concourse.bass_utils import run_bass_kernel_spmd as _run

    nc = _bacc.Bacc("TRN2", target_bir_lowering=False, num_devices=1)
    arrays, io = {}, {}
    for name, a in layout({k: _np.asarray(v) for k, v in inputs.items()}).items():
        arrays["in_" + name] = a
        io[name] = nc.dram_tensor("in_" + name, a.shape, mybir.dt.from_np(a.dtype), kind="ExternalInput").ap()
    out = nc.dram_tensor("out_0", (NB, N, C), F32, kind="ExternalOutput").ap()
    build(nc, out, **io)
    r = _run(nc, [arrays], core_ids=[0])
    return r.results[0]["out_0"]
```
